# Optimizing a Trainium2 kernel written in Bass

```python
import numpy as np
import jax
import jax.numpy as jnp

def _softmax(x, axis=-1):
    return jax.nn.softmax(x, axis=axis)

def _gelu(x):
    return jax.nn.gelu(x, approximate=True)

def _silu(x):
    return jax.nn.silu(x)

def _sigmoid(x):
    return jax.nn.sigmoid(x)

def _layernorm(x, axis=-1, eps=1e-05):
    m = jnp.mean(x, axis=axis, keepdims=True)
    v = jnp.var(x, axis=axis, keepdims=True)
    return (x - m) / jnp.sqrt(v + eps)

def _scatter_add(tgt, idx, src, axis=0):
    return tgt.at[idx].add(src)

def _segment_sum(src, seg, n):
    return jax.ops.segment_sum(src, seg, n)
kernel_name = 'mk_gnn_resnorm_d4_gnn_r8_bacfab'

def setup_inputs(seed: int=0):
    np.random.seed(seed)
    _w = jnp.asarray

    def _rec_inputs():
        import jax
        import jax.numpy as jnp
        _gk = jax.random.key(seed)
        x = -0.000202 + 1 * jax.random.normal(jax.random.fold_in(_gk, 1), (6250, 128), jnp.float32)
        src = jax.random.randint(jax.random.fold_in(_gk, 2), (100000,), 0, 6250, jnp.int32)
        dst = jnp.minimum((6250 * jax.random.uniform(jax.random.fold_in(_gk, 3), (100000,)) ** 2.0).astype(jnp.int32), 49999)
        _o = jnp.argsort(dst, stable=True)
        src = src[_o]
        dst = dst[_o]
        edge_attr_64 = 0.000189758 + 1.00013 * jax.random.normal(jax.random.fold_in(_gk, 12), (100000, 64), jnp.float32)
        edge_type_64 = jax.random.randint(jax.random.fold_in(_gk, 14), (100000,), 0, 64, jnp.int32)
        edge_weight = jax.random.uniform(jax.random.fold_in(_gk, 15), (100000,), jnp.float32, 0.0, 0.999999)
        node_vec = jax.random.uniform(jax.random.fold_in(_gk, 16), (6250,), jnp.float32, 0.0, 0.999994)
        return (x, src, dst, edge_attr_64, edge_type_64, edge_weight, node_vec)
    x, src, dst, edge_attr_64, edge_type_64, edge_weight, node_vec = _rec_inputs()

    def _L0_gnn_setup():
        import jax, jax.numpy as jnp
        import numpy as np
        N = 6250
        E = 100000
        D_IN = 128
        D_NODE = 128
        D_EIN = 64
        D_EDGE = 128
        L = 2
        NEG_SLOPE = 0.2

        def _gat_conv(h, src, dst, W, a_src, a_dst, bias):
            g = h @ W
            s = (g * a_src).sum(-1)
            d = (g * a_dst).sum(-1)
            e = jax.nn.leaky_relu(s[src] + d[dst], NEG_SLOPE)
            m = jax.ops.segment_max(e, dst, num_segments=N)
            m = jnp.where(jnp.isfinite(m), m, 0.0)
            ex = jnp.exp(e - m[dst])
            z = jax.ops.segment_sum(ex, dst, num_segments=N)
            alpha = ex / z[dst]
            out = jax.ops.segment_sum(g[src] * alpha[:, None], dst, num_segments=N)
            return out + bias
        key = jax.random.key(seed)
        ks = jax.random.split(key, 12)
        s = 0.05
        return {'x': jax.random.normal(ks[0], (N, D_IN), jnp.float32), 'edge_index': jax.random.randint(ks[1], (2, E), 0, N), 'edge_attr': jax.random.normal(ks[2], (E, D_EIN), jnp.float32), 'W_node': jax.random.normal(ks[3], (D_IN, D_NODE), jnp.float32) * s, 'b_node': jnp.zeros((D_NODE,), jnp.float32), 'W_edge': jax.random.normal(ks[4], (D_EIN, D_EDGE), jnp.float32) * s, 'b_edge': jnp.zeros((D_EDGE,), jnp.float32), 'lyr_We': jax.random.normal(ks[5], (L, D_EDGE, D_NODE), jnp.float32) * s, 'lyr_be': jnp.zeros((L, D_NODE), jnp.float32), 'lyr_W': jax.random.normal(ks[6], (L, D_NODE, D_NODE), jnp.float32) * s, 'att_src': jax.random.normal(ks[7], (L, D_NODE), jnp.float32) * s, 'att_dst': jax.random.normal(ks[8], (L, D_NODE), jnp.float32) * s, 'lyr_bias': jnp.zeros((L, D_NODE), jnp.float32)}
    _L0_gnn_all = _L0_gnn_setup()
    _L0_gnn_in = {k: v for k, v in _L0_gnn_all.items() if k in ('W_node', 'b_node', 'W_edge', 'b_edge', 'lyr_We', 'lyr_be', 'lyr_W', 'att_src', 'att_dst', 'lyr_bias')}
    del _L0_gnn_all

    def _L1_gnn_setup():
        import jax, jax.numpy as jnp
        import numpy as np
        N = 12500
        E = 200000
        IN = 128
        OUT = 128
        key = jax.random.key(seed)
        k1, k2, k3, k4, k5 = jax.random.split(key, 5)
        x = jax.random.normal(k1, (N, IN), dtype=jnp.float32)
        edge_index = jax.random.randint(k2, (2, E), 0, N, dtype=jnp.int64)
        edge_attr = jax.random.uniform(k3, (E,), dtype=jnp.float32)
        W = jax.random.normal(k4, (IN, OUT), dtype=jnp.float32) * (1.0 / np.sqrt(IN))
        b = jnp.zeros((OUT,), dtype=jnp.float32)
        return {'x': x, 'edge_index': edge_index, 'edge_attr': edge_attr, 'W': W, 'b': b}
    _L1_gnn_all = _L1_gnn_setup()
    _L1_gnn_in = {k: v for k, v in _L1_gnn_all.items() if k in ('W', 'b')}
    del _L1_gnn_all

    def _L2_gnn_setup():
        import jax, jax.numpy as jnp
        import numpy as np
        N_NODES = 6250
        N_EDGES = 100000
        HIDDEN = 128
        N_REL = 64
        NUM_HEADS = 8
        HEAD_DIM = HIDDEN // NUM_HEADS
        key = jax.random.key(seed)
        ks = jax.random.split(key, 20)
        s = 0.05
        inp = {'x': jax.random.normal(ks[0], (N_NODES, HIDDEN), dtype=jnp.float32), 'timestamps': jax.random.uniform(ks[1], (N_NODES,), dtype=jnp.float32), 'src': jax.random.randint(ks[2], (N_EDGES,), 0, N_NODES), 'dst': jax.random.randint(ks[3], (N_EDGES,), 0, N_NODES), 'edge_type': jax.random.randint(ks[4], (N_EDGES,), 0, N_REL), 'edge_time': jax.random.uniform(ks[5], (N_EDGES,), dtype=jnp.float32), 'rel_table': jax.random.normal(ks[6], (N_REL, HIDDEN), dtype=jnp.float32) * s, 'Wq': jax.random.normal(ks[7], (HIDDEN, HIDDEN), dtype=jnp.float32) * s, 'bq': jnp.zeros((HIDDEN,), dtype=jnp.float32), 'Wk': jax.random.normal(ks[8], (HIDDEN, HIDDEN), dtype=jnp.float32) * s, 'bk': jnp.zeros((HIDDEN,), dtype=jnp.float32), 'Wv': jax.random.normal(ks[9], (HIDDEN, HIDDEN), dtype=jnp.float32) * s, 'bv': jnp.zeros((HIDDEN,), dtype=jnp.float32), 'W1': jax.random.normal(ks[10], (2 * HIDDEN + 1, HIDDEN), dtype=jnp.float32) * s, 'b1': jnp.zeros((HIDDEN,), dtype=jnp.float32), 'W2': jax.random.normal(ks[11], (HIDDEN, 1), dtype=jnp.float32) * s, 'b2': jnp.zeros((1,), dtype=jnp.float32), 'time_coeff': jnp.array(1.0, dtype=jnp.float32)}
        return inp
    _L2_gnn_all = _L2_gnn_setup()
    _L2_gnn_in = {k: v for k, v in _L2_gnn_all.items() if k in ('rel_table', 'Wq', 'bq', 'Wk', 'bk', 'Wv', 'bv', 'W1', 'b1', 'W2', 'b2', 'time_coeff')}
    del _L2_gnn_all

    def _L3_gnn_setup():
        import jax, jax.numpy as jnp
        import numpy as np
        N, E, D = (12500, 200000, 128)
        key = jax.random.key(seed)
        ks = jax.random.split(key, 10)
        s = 1.0 / np.sqrt(D)
        return {'x': jax.random.normal(ks[0], (N, D), dtype=jnp.float32), 'edge_index': jax.random.randint(ks[1], (2, E), 0, N, dtype=jnp.int64), 'W_in': jax.random.uniform(ks[2], (D, D), jnp.float32, -s, s), 'b_in': jnp.zeros((D,), jnp.float32), 'W_msg': jax.random.uniform(ks[3], (D, D), jnp.float32, -s, s), 'W_ih': jax.random.uniform(ks[4], (3 * D, D), jnp.float32, -s, s), 'b_ih': jax.random.uniform(ks[5], (3 * D,), jnp.float32, -s, s), 'W_hh': jax.random.uniform(ks[6], (3 * D, D), jnp.float32, -s, s), 'b_hh': jax.random.uniform(ks[7], (3 * D,), jnp.float32, -s, s), 'W_out': jax.random.uniform(ks[8], (D, D), jnp.float32, -s, s), 'b_out': jnp.zeros((D,), jnp.float32)}
    _L3_gnn_all = _L3_gnn_setup()
    _L3_gnn_in = {k: v for k, v in _L3_gnn_all.items() if k in ('W_in', 'b_in', 'W_msg', 'W_ih', 'b_ih', 'W_hh', 'b_hh', 'W_out', 'b_out')}
    del _L3_gnn_all
    return {'x': x, 'src': src, 'dst': dst, 'edge_attr_64': edge_attr_64, 'edge_type_64': edge_type_64, 'edge_weight': edge_weight, 'node_vec': node_vec, 'L0_gnn_W_node': _L0_gnn_in['W_node'], 'L0_gnn_b_node': _L0_gnn_in['b_node'], 'L0_gnn_W_edge': _L0_gnn_in['W_edge'], 'L0_gnn_b_edge': _L0_gnn_in['b_edge'], 'L0_gnn_lyr_We': _L0_gnn_in['lyr_We'], 'L0_gnn_lyr_be': _L0_gnn_in['lyr_be'], 'L0_gnn_lyr_W': _L0_gnn_in['lyr_W'], 'L0_gnn_att_src': _L0_gnn_in['att_src'], 'L0_gnn_att_dst': _L0_gnn_in['att_dst'], 'L0_gnn_lyr_bias': _L0_gnn_in['lyr_bias'], 'L1_gnn_W': _L1_gnn_in['W'], 'L1_gnn_b': _L1_gnn_in['b'], 'L2_gnn_rel_table': _L2_gnn_in['rel_table'], 'L2_gnn_Wq': _L2_gnn_in['Wq'], 'L2_gnn_bq': _L2_gnn_in['bq'], 'L2_gnn_Wk': _L2_gnn_in['Wk'], 'L2_gnn_bk': _L2_gnn_in['bk'], 'L2_gnn_Wv': _L2_gnn_in['Wv'], 'L2_gnn_bv': _L2_gnn_in['bv'], 'L2_gnn_W1': _L2_gnn_in['W1'], 'L2_gnn_b1': _L2_gnn_in['b1'], 'L2_gnn_W2': _L2_gnn_in['W2'], 'L2_gnn_b2': _L2_gnn_in['b2'], 'L2_gnn_time_coeff': _L2_gnn_in['time_coeff'], 'L3_gnn_W_in': _L3_gnn_in['W_in'], 'L3_gnn_b_in': _L3_gnn_in['b_in'], 'L3_gnn_W_msg': _L3_gnn_in['W_msg'], 'L3_gnn_W_ih': _L3_gnn_in['W_ih'], 'L3_gnn_b_ih': _L3_gnn_in['b_ih'], 'L3_gnn_W_hh': _L3_gnn_in['W_hh'], 'L3_gnn_b_hh': _L3_gnn_in['b_hh'], 'L3_gnn_W_out': _L3_gnn_in['W_out'], 'L3_gnn_b_out': _L3_gnn_in['b_out']}

def reference(x, src, dst, edge_attr_64, edge_type_64, edge_weight, node_vec, L0_gnn_W_node, L0_gnn_b_node, L0_gnn_W_edge, L0_gnn_b_edge, L0_gnn_lyr_We, L0_gnn_lyr_be, L0_gnn_lyr_W, L0_gnn_att_src, L0_gnn_att_dst, L0_gnn_lyr_bias, L1_gnn_W, L1_gnn_b, L2_gnn_rel_table, L2_gnn_Wq, L2_gnn_bq, L2_gnn_Wk, L2_gnn_bk, L2_gnn_Wv, L2_gnn_bv, L2_gnn_W1, L2_gnn_b1, L2_gnn_W2, L2_gnn_b2, L2_gnn_time_coeff, L3_gnn_W_in, L3_gnn_b_in, L3_gnn_W_msg, L3_gnn_W_ih, L3_gnn_b_ih, L3_gnn_W_hh, L3_gnn_b_hh, L3_gnn_W_out, L3_gnn_b_out):
    import jax
    import jax.numpy as jnp

    def _L0_gnn_ref(x, edge_index, edge_attr, W_node, b_node, W_edge, b_edge, lyr_We, lyr_be, lyr_W, att_src, att_dst, lyr_bias):
        import jax, jax.numpy as jnp
        import numpy as np
        N = 6250
        E = 100000
        D_IN = 128
        D_NODE = 128
        D_EIN = 64
        D_EDGE = 128
        L = 2
        NEG_SLOPE = 0.2

        def _gat_conv(h, src, dst, W, a_src, a_dst, bias):
            g = h @ W
            s = (g * a_src).sum(-1)
            d = (g * a_dst).sum(-1)
            e = jax.nn.leaky_relu(s[src] + d[dst], NEG_SLOPE)
            m = jax.ops.segment_max(e, dst, num_segments=N)
            m = jnp.where(jnp.isfinite(m), m, 0.0)
            ex = jnp.exp(e - m[dst])
            z = jax.ops.segment_sum(ex, dst, num_segments=N)
            alpha = ex / z[dst]
            out = jax.ops.segment_sum(g[src] * alpha[:, None], dst, num_segments=N)
            return out + bias
        h = x @ W_node + b_node
        ea = edge_attr @ W_edge + b_edge
        src, dst = (edge_index[0], edge_index[1])
        loop = jnp.arange(N)
        src_sl = jnp.concatenate([src, loop])
        dst_sl = jnp.concatenate([dst, loop])
        for l in range(L):
            _ = ea @ lyr_We[l] + lyr_be[l]
            h = _gat_conv(h, src_sl, dst_sl, lyr_W[l], att_src[l], att_dst[l], lyr_bias[l])
        return h

    def _L1_gnn_ref(x, edge_index, edge_attr, W, b):
        import jax, jax.numpy as jnp
        import numpy as np
        N = 12500
        E = 200000
        IN = 128
        OUT = 128
        n = x.shape[0]
        loop = jnp.arange(n, dtype=edge_index.dtype)
        row = jnp.concatenate([edge_index[0], loop])
        col = jnp.concatenate([edge_index[1], loop])
        w = jnp.concatenate([edge_attr, jnp.ones((n,), dtype=x.dtype)])
        deg = jax.ops.segment_sum(w, col, num_segments=n)
        dis = jnp.where(deg > 0, jax.lax.rsqrt(deg), 0.0)
        norm = dis[row] * w * dis[col]
        xw = x @ W
        msgs = xw[row] * norm[:, None]
        out = jax.ops.segment_sum(msgs, col, num_segments=n)
        return out + b

    def _L2_gnn_ref(x, timestamps, src, dst, edge_type, edge_time, rel_table, Wq, bq, Wk, bk, Wv, bv, W1, b1, W2, b2, time_coeff):
        import jax, jax.numpy as jnp
        import numpy as np
        N_NODES = 6250
        N_EDGES = 100000
        HIDDEN = 128
        N_REL = 64
        NUM_HEADS = 8
        HEAD_DIM = HIDDEN // NUM_HEADS
        N = x.shape[0]
        delta_t = (timestamps[dst] - edge_time) / (jnp.abs(time_coeff) + 1e-09)
        time_mask = jax.nn.sigmoid(delta_t)[:, None]
        rel_emb = rel_table[edge_type] * time_mask
        src_emb = x[src]
        weight_input = jnp.concatenate([src_emb, rel_emb, time_mask], axis=-1)
        h = jax.nn.relu(weight_input @ W1 + b1)
        dynamic_weights = jax.nn.sigmoid(h @ W2 + b2)
        message = src_emb * rel_emb * dynamic_weights
        q = (x[dst] @ Wq + bq).reshape(-1, NUM_HEADS, HEAD_DIM)
        k = (message @ Wk + bk).reshape(-1, NUM_HEADS, HEAD_DIM)
        v = (message @ Wv + bv).reshape(-1, NUM_HEADS, HEAD_DIM)
        scores = (q * k).sum(-1) / HEAD_DIM ** 0.5
        seg_max = jax.ops.segment_max(scores, dst, num_segments=N)
        e = jnp.exp(scores - seg_max[dst])
        denom = jax.ops.segment_sum(e, dst, num_segments=N)
        attn = e / denom[dst]
        out = jax.ops.segment_sum(v * attn[..., None], dst, num_segments=N)
        return out.reshape(N, NUM_HEADS * HEAD_DIM)

    def _L3_gnn_ref(x, edge_index, W_in, b_in, W_msg, W_ih, b_ih, W_hh, b_hh, W_out, b_out):
        import jax, jax.numpy as jnp
        import numpy as np
        N, E, D = (12500, 200000, 128)
        n_nodes = x.shape[0]
        src, dst = (edge_index[0], edge_index[1])
        h = x @ W_in.T + b_in
        m = h @ W_msg
        agg = jax.ops.segment_sum(m[src], dst, num_segments=n_nodes)
        gi = agg @ W_ih.T + b_ih
        gh = h @ W_hh.T + b_hh
        i_r, i_z, i_n = jnp.split(gi, 3, axis=-1)
        h_r, h_z, h_n = jnp.split(gh, 3, axis=-1)
        r = jax.nn.sigmoid(i_r + h_r)
        z = jax.nn.sigmoid(i_z + h_z)
        n = jnp.tanh(i_n + r * h_n)
        h_new = (1.0 - z) * n + z * h
        return h_new @ W_out.T + b_out
    edge_index = jnp.stack([src, dst])
    x = _layernorm(x + _L0_gnn_ref(x, edge_index, edge_attr_64, L0_gnn_W_node, L0_gnn_b_node, L0_gnn_W_edge, L0_gnn_b_edge, L0_gnn_lyr_We, L0_gnn_lyr_be, L0_gnn_lyr_W, L0_gnn_att_src, L0_gnn_att_dst, L0_gnn_lyr_bias), axis=-1)
    x = _layernorm(x + _L1_gnn_ref(x, edge_index, edge_weight, L1_gnn_W, L1_gnn_b), axis=-1)
    x = _layernorm(x + _L2_gnn_ref(x, node_vec, src, dst, edge_type_64, edge_weight, L2_gnn_rel_table, L2_gnn_Wq, L2_gnn_bq, L2_gnn_Wk, L2_gnn_bk, L2_gnn_Wv, L2_gnn_bv, L2_gnn_W1, L2_gnn_b1, L2_gnn_W2, L2_gnn_b2, L2_gnn_time_coeff), axis=-1)
    x = _layernorm(x + _L3_gnn_ref(x, edge_index, L3_gnn_W_in, L3_gnn_b_in, L3_gnn_W_msg, L3_gnn_W_ih, L3_gnn_b_ih, L3_gnn_W_hh, L3_gnn_b_hh, L3_gnn_W_out, L3_gnn_b_out), axis=-1)
    return x

_drawn_inputs = setup_inputs


def setup_inputs(seed=0):
    import zlib

    import numpy as np

    out = dict(_drawn_inputs(seed))
    spreads = {'L0_gnn_b_node': (0.0, 0.1),
     'L0_gnn_b_edge': (0.0, 0.1),
     'L0_gnn_lyr_be': (0.0, 0.1),
     'L0_gnn_lyr_bias': (0.0, 0.1),
     'L1_gnn_b': (0.0, 0.1),
     'L2_gnn_bq': (0.0, 0.8),
     'L2_gnn_bk': (0.0, 0.8),
     'L2_gnn_bv': (0.0, 0.1),
     'L2_gnn_b1': (0.0, 0.8),
     'L3_gnn_b_in': (0.0, 0.1),
     'L3_gnn_b_out': (0.0, 0.1)}
    factors = {'node_vec': 8.0,
     'L0_gnn_W_node': 3.204,
     'L0_gnn_att_src': 8.0,
     'L0_gnn_att_dst': 8.0,
     'L2_gnn_rel_table': 8.0,
     'L2_gnn_Wq': 8.0,
     'L2_gnn_Wk': 8.0,
     'L2_gnn_Wv': 8.0,
     'L2_gnn_W1': 8.0,
     'L2_gnn_W2': 8.0,
     'L3_gnn_b_ih': 4.131,
     'L3_gnn_b_hh': 7.545}
    for name, (base, spread) in spreads.items():
        noise = np.random.default_rng([zlib.crc32(name.encode()), seed]).standard_normal(out[name].shape)
        drawn = base * np.exp(spread * noise) if base else spread * noise
        out[name] = jnp.asarray(drawn.astype(out[name].dtype))
    for name, factor in factors.items():
        out[name] = (out[name] * factor).astype(out[name].dtype)
    return out
```

```python
from contextlib import ExitStack, contextmanager

import numpy as np

import concourse.bass as bass
from concourse import mybir

F32 = mybir.dt.float32
I32 = mybir.dt.int32
ALU = mybir.AluOpType
ACT = mybir.ActivationFunctionType
AX = mybir.AxisListType.X

P = 128
N = 6250
E = 100000
D = 128
BLOCKS = -(-N // P)
QUADS = -(-BLOCKS // 4)
NBP = QUADS * 4
NPAD = NBP * P
GT = 4
GE = GT * P
GROUPS = -(-E // GE)
HALF_G = GROUPS // 2
V = GROUPS + BLOCKS - 1
VC = -(-V // P)
VP = VC * P
FULL = E // GE
REST = E - FULL * GE
PAD = GE - REST
NO_NODE = 8191
BIG = float(2.0 ** 100)
RING = 4
SLOPE = 0.2
EPS = 1e-5
HEADS = 8
HD = D // HEADS
TYPES = 64


class Count:

    def __init__(self, sem):
        self.sem, self.n = sem, 0

    def inc(self, ins, by=1):
        ins.then_inc(self.sem, by)
        self.n += by
        return self.n


def build(nc, A, out):
    top = ExitStack()
    with top:
        def sb(stack, name, shape, dt=F32):
            return stack.enter_context(nc.sbuf_tensor(name, shape, dt))

        def ps(stack, name, shape, dt=F32):
            return stack.enter_context(nc.psum_tensor(name, shape, dt))

        used = []

        def sem(stack, name):
            s = stack.enter_context(nc.semaphore(name))
            used.append(s)
            return s

        @contextmanager
        def phase():
            with ExitStack() as st:
                used.clear()
                yield st
                with nc.Block() as block:
                    @block.gpsimd
                    def _(pool):
                        for s in used:
                            pool.sem_clear(s)

        ident = sb(top, "ident", [P, P])
        iota = sb(top, "iota", [P, P])
        x_n = sb(top, "x_n", [P, NBP * D])
        acc = sb(top, "acc", [P, NBP * D])
        tmp = sb(top, "tmp", [P, NBP * D])
        src_tab = sb(top, "src_tab", [P, VP * GT], I32)
        dst_tab = sb(top, "dst_tab", [P, VP * GT])
        w_tab = sb(top, "w_tab", [P, VP * GT])
        typ_tab = sb(top, "typ_tab", [P, VP * GT])
        reset_tab = sb(top, "reset_tab", [P, VP * GT])
        glast_tab = sb(top, "glast_tab", [P, VP * GT])
        blk_row = sb(top, "blk_row", [1, VP], I32)
        rows = sb(top, "rows", [P, RING, GT, 256])
        src_slot = sb(top, "src_slot", [P, RING, GT], I32)
        deg = sb(top, "deg", [P, NBP])

        edge_rows = nc.dram_tensor("edge_rows", (GROUPS, 5 * GE), I32).ap()
        gat_tab = [nc.dram_tensor(f"gat_tab{l}", (NPAD, 132), F32).ap() for l in range(2)]
        gcn_tab = nc.dram_tensor("gcn_tab", (NPAD, D), F32).ap()
        rel_tab = nc.dram_tensor("rel_tab", (NPAD, 2 * D), F32).ap()
        ggn_tab = nc.dram_tensor("ggn_tab", (NPAD, D), F32).ap()

        def row(ap):
            return ap.rearrange("(o f) -> o f", o=1)

        with phase() as st:
            padv = sb(st, "padv", [1, 2, PAD + 8], I32)
            drow = sb(st, "drow", [HALF_G, 2, GE], I32)
            gmax = sb(st, "gmax", [HALF_G, 2], I32)
            gsh = sb(st, "gsh", [HALF_G, 2], I32)
            last = sb(st, "last", [HALF_G, 2])
            giota = sb(st, "giota", [HALF_G, 2], I32)
            giotaf = sb(st, "giotaf", [HALF_G, 2])
            viota = sb(st, "viota", [P, VC], I32)
            viotaf = sb(st, "viotaf", [P, VC])
            iota_i = sb(st, "iota_i", [P, P], I32)
            cmp = sb(st, "cmp", [P, VC, GROUPS])
            gv = sb(st, "gv", [P, VC])
            gvi = sb(st, "gvi", [P, VC], I32)
            bv = sb(st, "bv", [P, VC])
            bv128 = sb(st, "bv128", [P, VC])
            er = sb(st, "er", [P, VC, 5, GE], I32)
            ef = sb(st, "ef", [P, VC, 6, GE])
            prevf = sb(st, "prevf", [P, VC, GE])
            ps_last = ps(st, "ps_last", [P, GROUPS])
            ps_blk = ps(st, "ps_blk", [1, VP])
            ps_tr = ps(st, "ps_tr", [P, 2, GE])
            s_c = sem(st, "p_c")
            s_cp = sem(st, "p_cp")
            s_pad = sem(st, "p_pad")
            s_dr = sem(st, "p_dr")
            s_dl = sem(st, "p_dl")
            s_last = sem(st, "p_last")
            s_pl = sem(st, "p_pl")
            s_gv = sem(st, "p_gv")
            s_er = sem(st, "p_er")
            s_ef = sem(st, "p_ef")
            s_tr = sem(st, "p_tr")
            s_trc = sem(st, "p_trc")
            s_x = sem(st, "p_x")
            s_bv = sem(st, "p_bv")
            s_z = sem(st, "p_z")
            with nc.Block() as block:
                @block.sync
                def _(sp):
                    n = 0
                    sp.wait_ge(s_pad, 2)
                    for a, name in enumerate(("dst", "src", "edge_type_64", "edge_weight")):
                        arr = A[name] if a < 3 else A[name].bitcast(I32)
                        sp.dma_start(edge_rows[0:FULL, a * GE:(a + 1) * GE],
                                     arr[0:FULL * GE].rearrange("(g e) -> g e", e=GE)).then_inc(s_dr, 16)
                        sp.dma_start(edge_rows[FULL:GROUPS, a * GE:a * GE + REST],
                                     row(arr[FULL * GE:E])).then_inc(s_dr, 16)
                        sp.dma_start(edge_rows[FULL:GROUPS, a * GE + REST:(a + 1) * GE],
                                     padv[0:1, 0 if a == 0 else 1, 0:PAD]).then_inc(s_dr, 16)
                    dst, o = A["dst"], 4 * GE
                    sp.dma_start(edge_rows[0:1, o + 1:o + GE], row(dst[0:GE - 1])).then_inc(s_dr, 16)
                    sp.dma_start(edge_rows[0:1, o:o + 1], padv[0:1, 0, 0:1]).then_inc(s_dr, 16)
                    sp.dma_start(edge_rows[1:FULL, o:o + GE],
                                 dst[GE - 1:FULL * GE - 1].rearrange("(g e) -> g e", e=GE)).then_inc(s_dr, 16)
                    sp.dma_start(edge_rows[FULL:GROUPS, o:o + REST + 1],
                                 row(dst[FULL * GE - 1:E])).then_inc(s_dr, 16)
                    sp.dma_start(edge_rows[FULL:GROUPS, o + REST + 1:o + GE],
                                 padv[0:1, 0, 0:PAD - 1]).then_inc(s_dr, 16)
                    n = 17 * 16
                    sp.wait_ge(s_dr, n)
                    sp.dma_start(drow[:, :, :], edge_rows[:, 0:GE].rearrange("(c p) e -> p c e", c=2)).then_inc(s_dl, 16)
                    sp.wait_ge(s_z, 1)
                    sp.dma_start(x_n[:, 0:(BLOCKS - 1) * D].rearrange("p (b d) -> p b d", d=D),
                                 A["x"][0:(BLOCKS - 1) * P, :].rearrange("(b p) d -> p b d", p=P)).then_inc(s_x, 16)
                    sp.dma_start(x_n[0:N - (BLOCKS - 1) * P, (BLOCKS - 1) * D:BLOCKS * D],
                                 A["x"][(BLOCKS - 1) * P:N, :]).then_inc(s_x, 16)
                    sp.wait_ge(s_x, 32)

                @block.gpsimd
                def _(pool):
                    g = nc.gpsimd
                    g.iota(giota[:, :], pattern=[[HALF_G, 2]], base=0, channel_multiplier=1).then_inc(s_cp, 1)
                    g.iota(viota[:, :], pattern=[[P, VC]], base=0, channel_multiplier=1).then_inc(s_cp, 1)
                    g.iota(iota_i[:, :], pattern=[[1, P]], base=0, channel_multiplier=0).then_inc(s_cp, 1)
                    g.memset(ident[:, :], 0.0).then_inc(s_cp, 1)
                    pool.wait_ge(s_cp, 4)
                    g.affine_select(out=ident[:, :], in_=ident[:, :], compare_op=ALU.not_equal, fill=1.0,
                                    base=0, pattern=[[-1, P]], channel_multiplier=1).then_inc(s_cp, 1)
                    pool.wait_ge(s_gv, 1)
                    for c in range(VC):
                        pool.indirect_dma_start(er[:, c, :, :].rearrange("p a e -> p (a e)"), None, edge_rows[:, :],
                                                bass.IndirectOffsetOnAxis(ap=gvi[:, c:c + 1], axis=0)).then_inc(s_er, 16)

                @block.vector
                def _(dve):
                    v = nc.vector
                    c = Count(s_c)

                    def link(ins):
                        dve.wait_ge(s_c, c.inc(ins))

                    v.memset(padv[0:1, 0, :], NO_NODE).then_inc(s_pad, 1)
                    v.memset(padv[0:1, 1, :], 0).then_inc(s_pad, 1)
                    v.memset(x_n[:, :], 0.0).then_inc(s_z, 1)
                    dve.wait_ge(s_cp, 5)
                    v.tensor_copy(giotaf[:, :], giota[:, :])
                    v.tensor_copy(viotaf[:, :], viota[:, :])
                    link(v.tensor_copy(iota[:, :], iota_i[:, :]))
                    dve.wait_ge(s_dl, 16)
                    link(v.tensor_reduce(gmax[:, :], drow[:, :, :], AX, ALU.max))
                    link(v.tensor_scalar(gsh[:, :], gmax[:, :], 7, None, ALU.arith_shift_right))
                    link(v.tensor_scalar(last[:, :], gsh[:, :], float(BLOCKS - 1), None, ALU.min))
                    v.tensor_tensor(last[:, :], last[:, :], giotaf[:, :], ALU.add).then_inc(s_last, 1)
                    dve.wait_ge(s_pl, 1)
                    for k in range(VC):
                        link(v.tensor_scalar(cmp[:, k, :], ps_last[:, :], viotaf[:, k:k + 1], None, ALU.is_lt))
                    link(v.tensor_reduce(gv[:, :], cmp[:, :, :], AX, ALU.add))
                    link(v.tensor_scalar(gv[:, :], gv[:, :], float(GROUPS - 1), None, ALU.min))
                    v.tensor_copy(gvi[:, :], gv[:, :]).then_inc(s_gv, 1)
                    link(v.tensor_tensor(bv[:, :], viotaf[:, :], gv[:, :], ALU.subtract))
                    link(v.tensor_scalar(bv[:, :], bv[:, :], float(BLOCKS - 1), None, ALU.min))
                    v.tensor_scalar(bv128[:, :], bv[:, :], float(P), None, ALU.mult).then_inc(s_bv, 1)
                    dve.wait_ge(s_bv, 1)
                    dve.wait_ge(s_er, 16 * VC)
                    for k in range(VC):
                        link(v.tensor_copy(ef[:, k, 0:3, :], er[:, k, 0:3, :]))
                        link(v.tensor_copy(ef[:, k, 3, :], er[:, k, 3, :].bitcast(F32)))
                        link(v.tensor_copy(prevf[:, k, :], er[:, k, 4, :]))
                        link(v.memset(ef[:, k, 5, :], 1.0))
                        link(v.tensor_tensor(ef[:, k, 4, :], ef[:, k, 0, :], prevf[:, k, :], ALU.not_equal))
                        link(v.tensor_copy(ef[:, k, 5, 0:GE - 1], ef[:, k, 4, 1:GE]))
                        link(v.tensor_scalar(ef[:, k, 4, :], ef[:, k, 4, :], -BIG, None, ALU.mult))
                        v.tensor_scalar(ef[:, k, 0, :], ef[:, k, 0, :], bv128[:, k:k + 1], None, ALU.subtract).then_inc(s_ef, 1)
                    n = 0
                    for k in range(VC):
                        for a, tab in enumerate((dst_tab, src_tab, typ_tab, w_tab, reset_tab, glast_tab)):
                            dve.wait_ge(s_tr, n + 1)
                            v.tensor_copy(tab[:, k * P * GT:(k + 1) * P * GT].rearrange("p (v t) -> p t v", t=GT),
                                          ps_tr[:, n % 2, :].rearrange("p (t v) -> p t v", t=GT)).then_inc(s_trc, 1)
                            n += 1
                    dve.wait_ge(s_tr, n + 1)
                    v.tensor_copy(blk_row[:, :], ps_blk[:, :]).then_inc(s_trc, 1)
                    dve.wait_ge(s_trc, n + 1)

                @block.tensor
                def _(pe):
                    pe.wait_ge(s_cp, 5)
                    pe.wait_ge(s_last, 1)
                    for c in range(2):
                        i = nc.tensor.matmul(ps_last[:, c * HALF_G:(c + 1) * HALF_G],
                                             last[:, c:c + 1].to_broadcast([HALF_G, P]), ident[0:HALF_G, 0:HALF_G],
                                             start=True, stop=True)
                    i.then_inc(s_pl, 1)
                    n = 0
                    pe.wait_ge(s_ef, VC)
                    for k in range(VC):
                        for a in range(6):
                            if n >= 2:
                                pe.wait_ge(s_trc, n - 1)
                            for t in range(GT):
                                i = nc.tensor.transpose(ps_tr[:, n % 2, t * P:(t + 1) * P],
                                                        ef[:, k, a, t * P:(t + 1) * P], ident[:, :])
                            i.then_inc(s_tr, 1)
                            n += 1
                    pe.wait_ge(s_bv, 1)
                    for k in range(VC):
                        i = nc.tensor.matmul(ps_blk[:, k * P:(k + 1) * P], bv[:, k:k + 1], ident[:, :], start=True, stop=True)
                    i.then_inc(s_tr, 1)

        def load(n, shape, src_ap):
            t = sb(top, "w_" + n, shape)
            loads.append((t, src_ap))
            return t

        def col(ap):
            return ap.rearrange("(p o) -> p o", o=1)

        def rep(ap):
            return ap.partition_broadcast(P)

        loads = []
        w_node = load("node", [P, D], A["L0_gnn_W_node"])
        b_node = load("b_node", [P, 1], col(A["L0_gnn_b_node"]))
        w_lyr = load("lyr", [P, 2, D], A["L0_gnn_lyr_W"].rearrange("l k f -> k l f"))
        att = load("att", [P, 2, 2], None)
        b_lyr = [load(f"b_lyr{l}", [P, D], rep(A["L0_gnn_lyr_bias"][l, :])) for l in range(2)]
        w_gcn = load("gcn", [P, D], A["L1_gnn_W"])
        b_gcn = load("b_gcn", [P, D], rep(A["L1_gnn_b"]))
        rel_t = load("rel", [TYPES, D], A["L2_gnn_rel_table"])
        w_xq = load("xq", [P, 2, D], None)
        w_1b = load("w1b", [P, D], A["L2_gnn_W1"][D:2 * D, :])
        w_1c = load("w1c", [TYPES, D], A["L2_gnn_W1"][2 * D, :].partition_broadcast(TYPES))
        b_1 = load("b1", [P, D], rep(A["L2_gnn_b1"]))
        w_2 = load("w2", [P, D], rep(A["L2_gnn_W2"].rearrange("k o -> (k o)")))
        b_2 = load("b2", [P, 1], rep(A["L2_gnn_b2"]))
        b_q = load("bq", [P, D], rep(A["L2_gnn_bq"]))
        b_k = load("bk", [P, D], rep(A["L2_gnn_bk"]))
        b_v = load("bv", [P, D], rep(A["L2_gnn_bv"]))
        w_kv = load("kv", [P, 2, D], None)
        tc = load("tc", [P, 1], rep(A["L2_gnn_time_coeff"]))
        w_in = load("in", [P, D], A["L3_gnn_W_in"])
        b_in = load("b_in", [P, 1], col(A["L3_gnn_b_in"]))
        w_msg = load("msg", [P, D], A["L3_gnn_W_msg"])
        w_ih = load("ih", [P, 3, D], A["L3_gnn_W_ih"].rearrange("(g p) k -> p g k", p=P))
        w_hh = load("hh", [P, 3, D], A["L3_gnn_W_hh"].rearrange("(g p) k -> p g k", p=P))
        b_ih = load("b_ih", [P, 3], None)
        b_hh = load("b_hh", [P, 3], None)
        w_out = load("out", [P, D], A["L3_gnn_W_out"])
        b_out = load("b_out", [P, D], rep(A["L3_gnn_b_out"]))
        loads = [x for x in loads if x[1] is not None]
        for l in range(2):
            loads.append((att[:, l, 0:1], col(A["L0_gnn_att_src"][l, :])))
            loads.append((att[:, l, 1:2], col(A["L0_gnn_att_dst"][l, :])))
        loads.append((w_xq[:, 0, :], A["L2_gnn_W1"][0:D, :]))
        loads.append((w_xq[:, 1, :], A["L2_gnn_Wq"]))
        loads.append((w_kv[:, 0, :], A["L2_gnn_Wk"]))
        loads.append((w_kv[:, 1, :], A["L2_gnn_Wv"]))
        for g in range(3):
            loads.append((b_ih[:, g:g + 1], col(A["L3_gnn_b_ih"][g * D:(g + 1) * D])))
            loads.append((b_hh[:, g:g + 1], col(A["L3_gnn_b_hh"][g * D:(g + 1) * D])))
        nv = sb(top, "nv", [P, NBP])

        w_gat = sb(top, "w_gat", [P, 2, D + 2])
        relR = sb(top, "relR", [TYPES, 2 * D])
        w_inT = sb(top, "w_inT", [P, D])
        w_ihT = sb(top, "w_ihT", [P, 3, D])
        w_hhT = sb(top, "w_hhT", [P, 3, D])
        w_outT = sb(top, "w_outT", [P, D])
        half_rz = sb(top, "half_rz", [P, 2])
        rtc = sb(top, "rtc", [P, 1])
        neg_b2 = sb(top, "neg_b2", [P, 1])
        low_t = sb(top, "low_t", [P, 1])
        low_d = sb(top, "low_d", [P, 1])
        dis = sb(top, "dis", [P, NBP])
        ones = sb(top, "ones", [P, 1])
        eps_c = sb(top, "eps_c", [P, 1])
        with phase() as st:
            wT = sb(st, "wT", [P, 2, D])
            relT = sb(st, "relT", [P, TYPES])
            ps_t = [ps(st, f"ps_wt{i}", [P, D]) for i in range(2)]
            s_ld = sem(st, "w_ld")
            s_wt = sem(st, "w_t")
            s_wc = sem(st, "w_c")
            s_wd = sem(st, "w_d")
            s_nv = sem(st, "w_nv")
            NL = 16 * len(loads)
            trans = [(w_lyr[:, 0, :], wT[:, 0, :]), (w_lyr[:, 1, :], wT[:, 1, :]), (w_in[:, :], w_inT[:, :]),
                     (w_out[:, :], w_outT[:, :]), (rel_t[:, :], relT[:, :])]
            trans += [(w_ih[:, g, :], w_ihT[:, g, :]) for g in range(3)]
            trans += [(w_hh[:, g, :], w_hhT[:, g, :]) for g in range(3)]
            with nc.Block() as block:
                @block.sync
                def _(sp):
                    with nc.allow_non_contiguous_dma(reason="small bias columns"):
                        for dst, s in loads:
                            sp.dma_start(dst[tuple(slice(None) for _ in dst.shape)], s).then_inc(s_ld, 16)
                        sp.wait_ge(s_nv, 1)
                        sp.dma_start(nv[:, 0:BLOCKS - 1], A["node_vec"][0:(BLOCKS - 1) * P].rearrange("(b p) -> p b", p=P)).then_inc(s_ld, 16)
                        sp.dma_start(nv[0:N - (BLOCKS - 1) * P, BLOCKS - 1:BLOCKS],
                                     col(A["node_vec"][(BLOCKS - 1) * P:N])).then_inc(s_ld, 16)
                    sp.wait_ge(s_ld, NL + 32)

                @block.tensor
                def _(pe):
                    pe.wait_ge(s_ld, NL + 32)
                    n = 0
                    for n, (s, _) in enumerate(trans):
                        if n >= 2:
                            pe.wait_ge(s_wc, n - 1)
                        k, m = s.shape
                        nc.tensor.transpose(ps_t[n % 2][0:m, 0:k], s, ident[0:k, 0:k]).then_inc(s_wt, 1)
                    n = len(trans)
                    for l in range(2):
                        pe.wait_ge(s_wc, n - 1)
                        nc.tensor.matmul(ps_t[n % 2][:, 0:2], wT[:, l, :], att[:, l, :], start=True, stop=True).then_inc(s_wt, 1)
                        n += 1
                    pe.wait_ge(s_wc, n - 1)
                    nc.tensor.matmul(ps_t[n % 2][0:TYPES, :], relT[:, :], w_1b[:, :], start=True, stop=True).then_inc(s_wt, 1)

                @block.vector
                def _(dve):
                    v = nc.vector
                    c = Count(s_wd)

                    def link(ins):
                        dve.wait_ge(s_wd, c.inc(ins))

                    v.memset(nv[:, :], 0.0).then_inc(s_nv, 1)
                    v.memset(ones[:, :], 1.0)
                    v.memset(eps_c[:, :], EPS)
                    dve.wait_ge(s_ld, NL + 32)
                    for n, (s, d) in enumerate(trans):
                        k, m = s.shape
                        dve.wait_ge(s_wt, n + 1)
                        v.tensor_copy(d, ps_t[n % 2][0:m, 0:k]).then_inc(s_wc, 1)
                    n = len(trans)
                    for l in range(2):
                        dve.wait_ge(s_wt, n + 1)
                        v.tensor_copy(w_gat[:, l, 0:D], w_lyr[:, l, :])
                        v.tensor_copy(w_gat[:, l, D:D + 2], ps_t[n % 2][:, 0:2]).then_inc(s_wc, 1)
                        n += 1
                    dve.wait_ge(s_wt, n + 1)
                    v.tensor_copy(relR[:, 0:D], rel_t[:, :])
                    v.tensor_tensor(relR[:, D:2 * D], ps_t[n % 2][0:TYPES, :], w_1c[:, :], ALU.add).then_inc(s_wc, 1)
                    link(v.tensor_tensor(half_rz[:, :], b_ih[:, 0:2], b_hh[:, 0:2], ALU.add))
                    link(v.tensor_scalar(half_rz[:, :], half_rz[:, :], 0.5, None, ALU.mult))
                    link(v.tensor_scalar(rtc[:, :], tc[:, :], -1.0, None, ALU.mult))
                    link(v.tensor_tensor(rtc[:, :], rtc[:, :], tc[:, :], ALU.max))
                    link(v.tensor_scalar(rtc[:, :], rtc[:, :], 1e-9, None, ALU.add))
                    link(v.tensor_scalar(low_t[:, :], rtc[:, :], -80.0, None, ALU.mult))
                    link(v.reciprocal(rtc[:, :], rtc[:, :]))
                    link(v.tensor_scalar(rtc[:, :], rtc[:, :], -1.0, None, ALU.mult))
                    link(v.tensor_scalar(neg_b2[:, :], b_2[:, :], -1.0, None, ALU.mult))
                    link(v.tensor_scalar(low_d[:, :], neg_b2[:, :], 80.0, None, ALU.subtract))
                    dve.wait_ge(s_wc, n + 1)

        def quad(t, q, width=D):
            return t[:, bass.ds(q * (4 * width), 4 * width)]

        def table_rows(tab, q):
            return tab[bass.ds(q * (4 * P), 4 * P), :].rearrange("(j p) c -> p j c", p=P)

        def wide(ap, n):
            return ap.unsqueeze(2).to_broadcast([P, ap.shape[1], n])

        gat = ExitStack()
        mcur = sb(gat, "mcur", [P, NBP])
        zsum = sb(gat, "zsum", [P, NBP])
        dcol = sb(gat, "dcol", [P, NBP])

        def gat_nodes(l):
            with phase() as st:
                xs = sb(st, f"n{l}_xs", [P, 4 * D])
                xT = sb(st, f"n{l}_xT", [P, 4 * P])
                hT = sb(st, f"n{l}_hT", [P, 4 * P])
                gsb = sb(st, f"n{l}_gsb", [P, 4, 132])
                u = sb(st, f"n{l}_u", [P, NBP])
                sall = sb(st, f"n{l}_s", [P, NBP])
                rz = sb(st, f"n{l}_rz", [P, NBP])
                ps_a = ps(st, f"n{l}_psa", [P, 4 * P])
                ps_b = ps(st, f"n{l}_psb", [P, 4 * P])
                ps_c = ps(st, f"n{l}_psc", [P, 4, 256])
                s_xs = sem(st, f"n{l}_xs_ready")
                s_tr = sem(st, f"n{l}_transposed")
                s_xT = sem(st, f"n{l}_xT_ready")
                s_h = sem(st, f"n{l}_h_done")
                s_hT = sem(st, f"n{l}_hT_ready")
                s_g = sem(st, f"n{l}_g_done")
                s_gsb = sem(st, f"n{l}_gsb_ready")
                s_out = sem(st, f"n{l}_stored")
                s_free = sem(st, f"n{l}_store_buffer_free")
                s_ch = sem(st, f"n{l}_chain")
                with nc.Block() as block:
                    @block.vector
                    def _(dve):
                        v = nc.vector
                        if l == 0:
                            v.memset(gsb[:, :, :], 0.0)
                        else:
                            v.reciprocal(rz[:, :], zsum[:, :]).then_inc(s_ch, 1)
                            dve.wait_ge(s_ch, 1)
                            v.memset(gsb[:, :, :], 0.0)
                        with dve.Fori(0, QUADS) as q:
                            if l == 0:
                                v.tensor_copy(xs[:, :], quad(x_n, q)).then_inc(s_xs, 1)
                            else:
                                a3 = quad(acc, q).rearrange("p (j d) -> p j d", d=D)
                                x3 = xs[:, :].rearrange("p (j d) -> p j d", d=D)
                                v.tensor_tensor(x3, a3, wide(rz[:, bass.ds(q * 4, 4)], D), ALU.mult).then_inc(s_ch, 1)
                                dve.wait_ge(s_ch, q + 2)
                                v.tensor_tensor(x3, x3, b_lyr[0][:, :].unsqueeze(1).to_broadcast([P, 4, D]), ALU.add).then_inc(s_xs, 1)
                            dve.wait_ge(s_tr, q + 1)
                            v.tensor_copy(xT[:, :], ps_a[:, :]).then_inc(s_xT, 1)
                            dve.wait_ge(s_g, q + 1)
                            dve.wait_ge(s_free, q + 1)
                            v.tensor_copy(gsb[:, :, 0:D + 1], ps_c[:, :, 0:D + 1])
                            v.tensor_copy(quad(acc, q).rearrange("p (j d) -> p j d", d=D), ps_c[:, :, 0:D])
                            v.tensor_copy(sall[:, bass.ds(q * 4, 4)].unsqueeze(2), ps_c[:, :, D:D + 1])
                            v.tensor_copy(dcol[:, bass.ds(q * 4, 4)].unsqueeze(2), ps_c[:, :, D + 1:D + 2]).then_inc(s_gsb, 1)
                        dve.wait_ge(s_gsb, QUADS)
                        v.memset(zsum[:, :], 1.0)
                        n = (QUADS + 1) * l
                        v.tensor_tensor(u[:, :], sall[:, :], dcol[:, :], ALU.add).then_inc(s_ch, 1)
                        dve.wait_ge(s_ch, n + 1)
                        v.scalar_tensor_tensor(mcur[:, :], u[:, :], SLOPE, u[:, :], ALU.mult, ALU.max)
                        if l == 0:
                            v.memset(deg[:, :], 1.0)

                    @block.tensor
                    def _(pe):
                        with pe.Fori(0, QUADS) as q:
                            pe.wait_ge(s_xs, q + 1)
                            for j in range(4):
                                i = nc.tensor.transpose(ps_a[:, j * P:(j + 1) * P], xs[:, j * D:(j + 1) * D], ident[:, :])
                            i.then_inc(s_tr, 1)
                            pe.wait_ge(s_xT, q + 1)
                            if l == 0:
                                nc.tensor.matmul(ps_b[:, :], w_node[:, :], xT[:, :], start=True, stop=True).then_inc(s_h, 1)
                                pe.wait_ge(s_hT, q + 1)
                            lhs = hT if l == 0 else xT
                            for j in range(4):
                                i = nc.tensor.matmul(ps_c[:, j, 0:D + 2], lhs[:, j * P:(j + 1) * P], w_gat[:, l, :],
                                                     start=True, stop=True)
                            i.then_inc(s_g, 1)

                    @block.scalar
                    def _(act):
                        if l == 0:
                            with act.Fori(0, QUADS) as q:
                                act.wait_ge(s_h, q + 1)
                                nc.scalar.activation(hT[:, :], ps_b[:, :], ACT.Identity, bias=b_node[:, :]).then_inc(s_hT, 1)

                    @block.sync
                    def _(sp):
                        sp.sem_inc(s_free, 1)
                        with sp.Fori(0, QUADS) as q:
                            sp.wait_ge(s_gsb, q + 1)
                            sp.dma_start(table_rows(gat_tab[l], q), gsb[:, :, :]).then_inc(s_out, 16)
                            sp.wait_ge(s_out, q * 16 + 16)
                            sp.sem_inc(s_free, 1)

        def gather_rows(pool, tab, width, s_idx, s_row, s_used):
            with pool.Fori(0, V // RING) as i:
                for k in range(RING):
                    pool.wait_ge(s_used, i * RING + k + 1)
                    nc.gpsimd.tensor_copy(src_slot[:, k, :], src_tab[:, bass.ds((i * RING + k) * GT, GT)]).then_inc(s_idx, 1)
                    pool.wait_ge(s_idx, i * RING + k + 1)
                    pool.sem_inc(s_turn, 1)
                    for t in range(GT):
                        pool.indirect_dma_start(rows[:, k, t, 0:width], None, tab[:, :],
                                                bass.IndirectOffsetOnAxis(ap=src_slot[:, k, t:t + 1], axis=0)).then_inc(s_row[k], 16)

        s_turn = sem(top, "gather_turn")

        def steps(first, body):
            whole = (V - 1) // RING
            with first.Fori(0, whole) as i:
                for k in range(RING):
                    body(i * RING + k, k)
            for v in range(whole * RING, V - 1):
                body(v, v % RING)

        def gat_edges(l):
            with phase() as st:
                mask = sb(st, f"e{l}_mask", [P, 2, GT, P])
                ow = sb(st, f"e{l}_ow", [P, 2, GT, P])
                un = sb(st, f"e{l}_un", [P, 2, GE])
                lr = sb(st, f"e{l}_lr", [P, 2, GE])
                pr = sb(st, f"e{l}_pr", [P, 2, GE])
                prT = sb(st, f"e{l}_prT", [P, 2, GE])
                dsl = sb(st, f"e{l}_dsl", [P, 2])
                sm = sb(st, f"e{l}_sm", [P, 2, 6])
                al = sb(st, f"e{l}_al", [P, 2])
                zp = sb(st, f"e{l}_zp", [P, 2])
                ps_s = [ps(st, f"e{l}_pss{i}", [P, GE]) for i in range(2)]
                ps_t = [ps(st, f"e{l}_pst{i}", [P, GE]) for i in range(2)]
                ps_o = [ps(st, f"e{l}_pso{i}", [P, 512]) for i in range(2)]
                s_idx = sem(st, f"e{l}_idx")
                s_row = [sem(st, f"e{l}_row{k}") for k in range(RING)]
                s_mask = sem(st, f"e{l}_mask_ready")
                s_s = sem(st, f"e{l}_scores_done")
                s_m = sem(st, f"e{l}_max_ready")
                s_u = sem(st, f"e{l}_logits_in")
                s_lr = sem(st, f"e{l}_logits_ready")
                s_p = sem(st, f"e{l}_probs_ready")
                s_t = sem(st, f"e{l}_probs_transposed")
                s_pT = sem(st, f"e{l}_probsT_ready")
                s_o = sem(st, f"e{l}_sums_done")
                s_acc = sem(st, f"e{l}_sums_added")
                s_ch = sem(st, f"e{l}_chain")
                NCH = 6
                with nc.Block() as block:
                    @block.gpsimd
                    def _(pool):
                        pool.sem_inc(s_o, RING)
                        gather_rows(pool, gat_tab[l], 132, s_idx, s_row, s_o)

                    @block.vector
                    def _(dve):
                        v_ = nc.vector

                        def front(v, k, first=False):
                            h = k % 2
                            for t in range(GT):
                                i = v_.tensor_scalar(mask[:, h, t, :], iota[:, :], dst_tab[:, bass.ds(v * GT + t, 1)], -BIG,
                                                     ALU.not_equal, ALU.mult)
                            if l == 0:
                                for t in range(GT):
                                    i = v_.tensor_scalar(ow[:, h, t, :], iota[:, :], dst_tab[:, bass.ds(v * GT + t, 1)],
                                                         w_tab[:, bass.ds(v * GT + t, 1)], ALU.is_equal, ALU.mult)
                            i.then_inc(s_mask, 1)
                            b = dve.value_load(blk_row[0:1, bass.ds(v, 1)], min_val=0, max_val=BLOCKS - 1)
                            v_.tensor_copy(dsl[:, h:h + 1], dcol[:, bass.ds(b, 1)]).then_inc(s_ch, 1)
                            dve.wait_ge(s_s, v + 1)
                            v_.tensor_reduce(sm[:, h, 0:1], ps_s[h][:, :], AX, ALU.max).then_inc(s_ch, 1)
                            dve.wait_ge(s_ch, v * NCH + 2)
                            v_.tensor_tensor(sm[:, h, 1:2], sm[:, h, 0:1], dsl[:, h:h + 1], ALU.add).then_inc(s_ch, 1)
                            dve.wait_ge(s_ch, v * NCH + 3)
                            v_.scalar_tensor_tensor(sm[:, h, 2:3], sm[:, h, 1:2], SLOPE, sm[:, h, 1:2], ALU.mult, ALU.max).then_inc(s_ch, 1)
                            dve.wait_ge(s_ch, v * NCH + 4)
                            if not first:
                                dve.wait_ge(s_m, v)
                            v_.tensor_tensor(sm[:, h, 3:4], sm[:, h, 2:3], mcur[:, bass.ds(b, 1)], ALU.max).then_inc(s_ch, 1)
                            dve.wait_ge(s_ch, v * NCH + 5)
                            v_.tensor_scalar(sm[:, h, 4:5], sm[:, h, 3:4], -1.0, None, ALU.mult)
                            v_.tensor_tensor(sm[:, h, 5:6], mcur[:, bass.ds(b, 1)], sm[:, h, 3:4], ALU.subtract).then_inc(s_ch, 1)
                            dve.wait_ge(s_ch, v * NCH + 6)
                            v_.tensor_tensor(mcur[:, bass.ds(b, 1)], mcur[:, bass.ds(b, 1)], sm[:, h, 2:3], ALU.max).then_inc(s_m, 1)
                            dve.wait_ge(s_u, v + 1)
                            v_.scalar_tensor_tensor(lr[:, h, :], un[:, h, :], SLOPE, un[:, h, :], ALU.mult, ALU.max).then_inc(s_lr, 1)

                        def back(v, k):
                            h = k % 2
                            b = dve.value_load(blk_row[0:1, bass.ds(v, 1)], min_val=0, max_val=BLOCKS - 1)
                            dve.wait_ge(s_p, v + 1)
                            dve.wait_ge(s_acc, v + 2)
                            zb = zsum[:, bass.ds(b, 1)]
                            v_.scalar_tensor_tensor(zb, zb, al[:, h:h + 1], zp[:, h:h + 1], ALU.mult, ALU.add)
                            dve.wait_ge(s_o, v + 1 + RING)
                            ab = acc[:, bass.ds(b * D, D)]
                            i = v_.scalar_tensor_tensor(ab, ab, al[:, h:h + 1], ps_o[h][:, 0:D], ALU.mult, ALU.add)
                            if l == 0:
                                gb = deg[:, bass.ds(b, 1)]
                                i = v_.tensor_tensor(gb, gb, ps_o[h][:, D:D + 1], ALU.add)
                            i.then_inc(s_acc, 1)

                        front(0, 0, first=True)

                        def body(v, k):
                            front(v + 1, k + 1)
                            back(v, k)

                        steps(dve, body)
                        back(V - 1, (V - 1) % RING)
                        dve.wait_ge(s_acc, V + 2)

                    @block.tensor
                    def _(pe):
                        def scores(v, k, fill):
                            h = k % 2
                            pe.wait_ge(s_mask, v + 1)
                            pe.wait_ge(s_row[k % RING], fill)
                            for t in range(GT):
                                o = ps_s[h][:, t * P:(t + 1) * P]
                                nc.tensor.matmul(o, mask[:, h, t, :], ident[:, :], start=True, stop=False)
                                i = nc.tensor.matmul(o, rows[:, k % RING, t, D:D + 1].to_broadcast([P, P]), ident[:, :],
                                                     start=False, stop=True)
                            i.then_inc(s_s, 1)

                        def spread(v, k):
                            h = k % 2
                            pe.wait_ge(s_p, v + 1)
                            for t in range(GT):
                                i = nc.tensor.transpose(ps_t[h][:, t * P:(t + 1) * P], pr[:, h, t * P:(t + 1) * P], ident[:, :])
                            i.then_inc(s_t, 1)
                            pe.wait_ge(s_pT, v + 1)
                            pe.wait_ge(s_acc, v + 1)
                            for t in range(GT):
                                i = nc.tensor.matmul(ps_o[h][:, 0:D], prT[:, h, t * P:(t + 1) * P], rows[:, k, t, 0:D],
                                                     start=(t == 0), stop=(t == GT - 1))
                            if l == 0:
                                for t in range(GT):
                                    i = nc.tensor.matmul(ps_o[h][:, D:D + 1], ow[:, h, t, :], ones[:, :],
                                                         start=(t == 0), stop=(t == GT - 1))
                            i.then_inc(s_o, 1)

                        pe.sem_inc(s_acc, 2)
                        scores(0, 0, 16 * GT)
                        whole = (V - 1) // RING
                        with pe.Fori(0, whole) as i:
                            for k in range(RING):
                                v = i * RING + k
                                scores(v + 1, k + 1, (i + (2 if k == RING - 1 else 1)) * (16 * GT))
                                spread(v, k)
                        for v in range(whole * RING, V - 1):
                            scores(v + 1, v % RING + 1, ((v + 1) // RING + 1) * 16 * GT)
                            spread(v, v % RING)
                        spread(V - 1, (V - 1) % RING)

                    @block.scalar
                    def _(act):
                        def probs(v, k):
                            h = k % 2
                            act.wait_ge(s_ch, v * NCH + 2)
                            nc.scalar.activation(un[:, h, :], ps_s[h][:, :], ACT.Identity, bias=dsl[:, h:h + 1]).then_inc(s_u, 1)
                            act.wait_ge(s_m, v + 1)
                            nc.scalar.activation(al[:, h:h + 1], sm[:, h, 5:6], ACT.Exp)
                            act.wait_ge(s_lr, v + 1)
                            nc.scalar.activation(pr[:, h, :], lr[:, h, :], ACT.Exp, bias=sm[:, h, 4:5],
                                                 accum_out=zp[:, h:h + 1]).then_inc(s_p, 1)

                        def copyT(v, k):
                            h = k % 2
                            act.wait_ge(s_t, v + 1)
                            nc.scalar.activation(prT[:, h, :], ps_t[h][:, :], ACT.Copy).then_inc(s_pT, 1)

                        probs(0, 0)

                        def body(v, k):
                            copyT(v, k)
                            probs(v + 1, k + 1)

                        steps(act, body)
                        copyT(V - 1, (V - 1) % RING)

        def residual_norm(name, prep):
            with phase() as st:
                mean = sb(st, f"{name}_mean", [P, NBP])
                var = sb(st, f"{name}_var", [P, NBP])
                sd = sb(st, f"{name}_sd", [P, NBP])
                s_ch = sem(st, f"{name}_chain")
                s_var = sem(st, f"{name}_var_ready")
                s_sd = sem(st, f"{name}_sd_ready")
                t3 = tmp[:, :].rearrange("p (b d) -> p b d", d=D)
                x3 = x_n[:, :].rearrange("p (b d) -> p b d", d=D)
                with nc.Block() as block:
                    @block.vector
                    def _(dve):
                        v = nc.vector
                        c = Count(s_ch)

                        def link(ins):
                            dve.wait_ge(s_ch, c.inc(ins))

                        prep(link, st, t3, x3)
                        link(v.tensor_reduce(mean[:, :], t3, AX, ALU.add))
                        link(v.tensor_scalar(mean[:, :], mean[:, :], 1.0 / D, None, ALU.mult))
                        link(v.tensor_tensor(t3, t3, wide(mean[:, :], D), ALU.subtract))
                        link(v.tensor_tensor(x3, t3, t3, ALU.mult))
                        v.tensor_reduce(var[:, :], x3, AX, ALU.add).then_inc(s_var, 1)
                        dve.wait_ge(s_sd, 1)
                        link(v.reciprocal(sd[:, :], sd[:, :]))
                        link(v.tensor_tensor(x3, t3, wide(sd[:, :], D), ALU.mult))

                    @block.scalar
                    def _(act):
                        act.wait_ge(s_var, 1)
                        nc.scalar.activation(sd[:, :], var[:, :], ACT.Sqrt, bias=eps_c[:, :], scale=1.0 / D).then_inc(s_sd, 1)

        def every(b):
            return b[:, :].unsqueeze(1).to_broadcast([P, NBP, D])

        def gat_out(link, st, t3, x3):
            v = nc.vector
            rz = sb(st, "go_rz", [P, NBP])
            link(v.reciprocal(rz[:, :], zsum[:, :]))
            link(v.tensor_tensor(t3, acc[:, :].rearrange("p (b d) -> p b d", d=D), wide(rz[:, :], D), ALU.mult))
            link(v.tensor_tensor(t3, t3, every(b_lyr[1]), ALU.add))
            link(v.tensor_tensor(t3, t3, x3, ALU.add))

        def table_nodes(name, take, w_first, b_first, keep, w_second, width, tab, tab_width, give, start=None):
            with phase() as st:
                xs = sb(st, f"{name}_xs", [P, 4 * D])
                xT = sb(st, f"{name}_xT", [P, 4 * P])
                hT = sb(st, f"{name}_hT", [P, 4 * P])
                gsb = sb(st, f"{name}_gsb", [P, 4, tab_width])
                scr = sb(st, f"{name}_scr", [P, 4, D])
                ps_a = ps(st, f"{name}_psa", [P, 4 * P])
                ps_b = ps(st, f"{name}_psb", [P, 4 * P])
                ps_c = ps(st, f"{name}_psc", [P, 4, 256])
                s_xs = sem(st, f"{name}_xs_ready")
                s_tr = sem(st, f"{name}_transposed")
                s_xT = sem(st, f"{name}_xT_ready")
                s_h = sem(st, f"{name}_h_done")
                s_hT = sem(st, f"{name}_hT_ready")
                s_g = sem(st, f"{name}_products_done")
                s_gsb = sem(st, f"{name}_rows_ready")
                s_out = sem(st, f"{name}_stored")
                s_free = sem(st, f"{name}_store_buffer_free")
                s_ch = sem(st, f"{name}_chain")
                s_pre = sem(st, f"{name}_start")
                s_act = sem(st, f"{name}_act")
                with nc.Block() as block:
                    @block.vector
                    def _(dve):
                        v = nc.vector
                        if start is not None:
                            start(dve, v, s_pre, s_act)
                        with dve.Fori(0, QUADS) as q:
                            take(dve, v, q, xs).then_inc(s_xs, 1)
                            dve.wait_ge(s_tr, q + 1)
                            v.tensor_copy(xT[:, :], ps_a[:, :]).then_inc(s_xT, 1)
                            dve.wait_ge(s_g, q + 1)
                            dve.wait_ge(s_free, q + 1)
                            give(dve, v, q, ps_c, xs, gsb, scr, s_ch).then_inc(s_gsb, 1)
                        dve.wait_ge(s_gsb, QUADS)

                    @block.tensor
                    def _(pe):
                        with pe.Fori(0, QUADS) as q:
                            pe.wait_ge(s_xs, q + 1)
                            for j in range(4):
                                i = nc.tensor.transpose(ps_a[:, j * P:(j + 1) * P], xs[:, j * D:(j + 1) * D], ident[:, :])
                            i.then_inc(s_tr, 1)
                            pe.wait_ge(s_xT, q + 1)
                            if w_first is not None:
                                nc.tensor.matmul(ps_b[:, :], w_first[:, :], xT[:, :], start=True, stop=True).then_inc(s_h, 1)
                                pe.wait_ge(s_hT, q + 1)
                            lhs = hT if w_first is not None else xT
                            for j in range(4):
                                i = nc.tensor.matmul(ps_c[:, j, 0:width], lhs[:, j * P:(j + 1) * P], w_second,
                                                     start=True, stop=True)
                            i.then_inc(s_g, 1)

                    @block.scalar
                    def _(act):
                        if start is not None:
                            start(act, None, s_pre, s_act)
                        if w_first is not None:
                            with act.Fori(0, QUADS) as q:
                                act.wait_ge(s_h, q + 1)
                                nc.scalar.activation(quad(keep, q), ps_b[:, :], ACT.Identity, bias=b_first[:, :])
                                nc.scalar.activation(hT[:, :], ps_b[:, :], ACT.Identity, bias=b_first[:, :]).then_inc(s_hT, 1)

                    @block.sync
                    def _(sp):
                        sp.sem_inc(s_free, 1)
                        with sp.Fori(0, QUADS) as q:
                            sp.wait_ge(s_gsb, q + 1)
                            sp.dma_start(table_rows(tab, q), gsb[:, :, :]).then_inc(s_out, 16)
                            sp.wait_ge(s_out, q * 16 + 16)
                            sp.sem_inc(s_free, 1)

        def take_x(dve, v, q, xs):
            return v.tensor_copy(xs[:, :], quad(x_n, q))

        def sum_edges(name, tab, weighted):
            with phase() as st:
                oh = sb(st, f"{name}_oh", [P, 2, GT, P])
                ps_o = [ps(st, f"{name}_pso{i}", [P, 512]) for i in range(2)]
                s_idx = sem(st, f"{name}_idx")
                s_row = [sem(st, f"{name}_row{k}") for k in range(RING)]
                s_oh = sem(st, f"{name}_onehot_ready")
                s_o = sem(st, f"{name}_sums_done")
                s_acc = sem(st, f"{name}_sums_added")
                with nc.Block() as block:
                    @block.gpsimd
                    def _(pool):
                        pool.sem_inc(s_o, RING)
                        gather_rows(pool, tab, D, s_idx, s_row, s_o)

                    @block.vector
                    def _(dve):
                        v_ = nc.vector

                        def front(v, k):
                            for t in range(GT):
                                col_ = bass.ds(v * GT + t, 1)
                                if weighted:
                                    i = v_.tensor_scalar(oh[:, k % 2, t, :], iota[:, :], dst_tab[:, col_], w_tab[:, col_],
                                                         ALU.is_equal, ALU.mult)
                                else:
                                    i = v_.tensor_scalar(oh[:, k % 2, t, :], iota[:, :], dst_tab[:, col_], None, ALU.is_equal)
                            i.then_inc(s_oh, 1)

                        def back(v, k):
                            b = dve.value_load(blk_row[0:1, bass.ds(v, 1)], min_val=0, max_val=BLOCKS - 1)
                            dve.wait_ge(s_acc, v + 2)
                            dve.wait_ge(s_o, v + 1 + RING)
                            ab = acc[:, bass.ds(b * D, D)]
                            v_.tensor_tensor(ab, ab, ps_o[k % 2][:, 0:D], ALU.add).then_inc(s_acc, 1)

                        front(0, 0)

                        def body(v, k):
                            front(v + 1, k + 1)
                            back(v, k)

                        steps(dve, body)
                        back(V - 1, (V - 1) % RING)
                        dve.wait_ge(s_acc, V + 2)

                    @block.tensor
                    def _(pe):
                        pe.sem_inc(s_acc, 2)
                        with pe.Fori(0, V // RING) as i:
                            for k in range(RING):
                                v = i * RING + k
                                pe.wait_ge(s_oh, v + 1)
                                pe.wait_ge(s_row[k], i * (16 * GT) + 16 * GT)
                                pe.wait_ge(s_acc, v + 1)
                                for t in range(GT):
                                    m = nc.tensor.matmul(ps_o[k % 2][:, 0:D], oh[:, k % 2, t, :], rows[:, k, t, 0:D],
                                                         start=(t == 0), stop=(t == GT - 1))
                                m.then_inc(s_o, 1)


        def gcn_start(eng, v, s_pre, s_act):
            if v is None:
                eng.wait_ge(s_pre, 1)
                nc.scalar.activation(dis[:, :], dis[:, :], ACT.Sqrt).then_inc(s_act, 1)
                return
            v.tensor_scalar(dis[:, :], deg[:, :], 1e-30, None, ALU.max).then_inc(s_pre, 1)
            v.tensor_scalar(deg[:, :], deg[:, :], 0.0, None, ALU.is_gt).then_inc(s_pre, 1)
            eng.wait_ge(s_pre, 2)
            eng.wait_ge(s_act, 1)
            v.reciprocal(dis[:, :], dis[:, :]).then_inc(s_pre, 1)
            eng.wait_ge(s_pre, 3)
            v.tensor_tensor(dis[:, :], dis[:, :], deg[:, :], ALU.mult).then_inc(s_pre, 1)
            eng.wait_ge(s_pre, 4)

        def gcn_give(dve, v, q, ps_c, xs, gsb, scr, s_ch):
            dq = wide(dis[:, bass.ds(q * 4, 4)], D)
            v.tensor_tensor(quad(acc, q).rearrange("p (j d) -> p j d", d=D), ps_c[:, :, 0:D], dq, ALU.mult)
            return v.tensor_tensor(gsb[:, :, :], ps_c[:, :, 0:D], dq, ALU.mult)

        def gcn_out(link, st, t3, x3):
            v = nc.vector
            link(v.tensor_tensor(t3, acc[:, :].rearrange("p (b d) -> p b d", d=D), wide(dis[:, :], D), ALU.mult))
            link(v.tensor_tensor(t3, t3, every(b_gcn), ALU.add))
            link(v.tensor_tensor(t3, t3, x3, ALU.add))

        def ggn_start(eng, v, s_pre, s_act):
            if v is not None:
                v.memset(acc[:, :], 0.0)

        def ggn_give(dve, v, q, ps_c, xs, gsb, scr, s_ch):
            return v.tensor_copy(gsb[:, :, :], ps_c[:, :, 0:D])

        def ggn_gates():
            with phase() as st:
                xs = sb(st, "gru_xs", [P, 4 * D])
                aT = sb(st, "gru_aT", [P, 4 * P])
                er = sb(st, "gru_r", [P, 4 * P])
                ez = sb(st, "gru_z", [P, 4 * P])
                nn = sb(st, "gru_n", [P, 4 * P])
                hn = sb(st, "gru_h", [P, 4 * P])
                ps_a = ps(st, "gru_psa", [P, 4 * P])
                ps_g = [ps(st, f"gru_psg{i}", [P, 4 * P]) for i in range(4)]
                ps_c = ps(st, "gru_psc", [P, 4, D])
                s_xs = sem(st, "gru_xs_ready")
                s_tr = sem(st, "gru_transposed")
                s_aT = sem(st, "gru_aT_ready")
                s_g = sem(st, "gru_gates_done")
                s_e = sem(st, "gru_exp_ready")
                s_n = sem(st, "gru_n_in")
                s_t = sem(st, "gru_tanh_ready")
                s_hn = sem(st, "gru_h_ready")
                s_c = sem(st, "gru_out_done")
                s_ac = sem(st, "gru_out_taken")
                s_ch = sem(st, "gru_chain")
                NCH = 5
                with nc.Block() as block:
                    @block.vector
                    def _(dve):
                        v = nc.vector
                        with dve.Fori(0, QUADS) as q:
                            v.tensor_copy(xs[:, :], quad(acc, q)).then_inc(s_xs, 1)
                            dve.wait_ge(s_tr, q + 1)
                            v.tensor_copy(aT[:, :], ps_a[:, :]).then_inc(s_aT, 1)
                            dve.wait_ge(s_e, q + 1)
                            for g in (er, ez):
                                v.tensor_scalar(g[:, :], g[:, :], 0.5, 0.5, ALU.mult, ALU.add).then_inc(s_ch, 1)
                            dve.wait_ge(s_ch, q * NCH + 2)
                            v.scalar_tensor_tensor(nn[:, :], ps_g[3][:, :], b_hh[:, 2:3], er[:, :], ALU.add, ALU.mult).then_inc(s_ch, 1)
                            dve.wait_ge(s_ch, q * NCH + 3)
                            v.tensor_tensor(nn[:, :], nn[:, :], ps_g[2][:, :], ALU.add).then_inc(s_n, 1)
                            dve.wait_ge(s_t, q + 1)
                            v.tensor_tensor(hn[:, :], quad(tmp, q), nn[:, :], ALU.subtract).then_inc(s_ch, 1)
                            dve.wait_ge(s_ch, q * NCH + 4)
                            v.tensor_tensor(hn[:, :], hn[:, :], ez[:, :], ALU.mult).then_inc(s_ch, 1)
                            dve.wait_ge(s_ch, q * NCH + 5)
                            v.tensor_tensor(hn[:, :], hn[:, :], nn[:, :], ALU.add).then_inc(s_hn, 1)
                            dve.wait_ge(s_c, q + 1)
                            v.tensor_tensor(quad(acc, q).rearrange("p (j d) -> p j d", d=D), ps_c[:, :, :],
                                            b_out[:, :].unsqueeze(1).to_broadcast([P, 4, D]), ALU.add).then_inc(s_ac, 1)
                        dve.wait_ge(s_ac, QUADS)

                    @block.tensor
                    def _(pe):
                        with pe.Fori(0, QUADS) as q:
                            pe.wait_ge(s_xs, q + 1)
                            for j in range(4):
                                i = nc.tensor.transpose(ps_a[:, j * P:(j + 1) * P], xs[:, j * D:(j + 1) * D], ident[:, :])
                            i.then_inc(s_tr, 1)
                            pe.wait_ge(s_aT, q + 1)
                            for g in range(2):
                                nc.tensor.matmul(ps_g[g][:, :], w_ihT[:, g, :], aT[:, :], start=True, stop=False)
                                nc.tensor.matmul(ps_g[g][:, :], w_hhT[:, g, :], quad(tmp, q), start=False, stop=True)
                            nc.tensor.matmul(ps_g[2][:, :], w_ihT[:, 2, :], aT[:, :], start=True, stop=True)
                            nc.tensor.matmul(ps_g[3][:, :], w_hhT[:, 2, :], quad(tmp, q), start=True, stop=True).then_inc(s_g, 1)
                            pe.wait_ge(s_hn, q + 1)
                            for j in range(4):
                                i = nc.tensor.matmul(ps_c[:, j, :], hn[:, j * P:(j + 1) * P], w_outT[:, :], start=True, stop=True)
                            i.then_inc(s_c, 1)

                    @block.scalar
                    def _(act):
                        with act.Fori(0, QUADS) as q:
                            act.wait_ge(s_g, q + 1)
                            nc.scalar.activation(er[:, :], ps_g[0][:, :], ACT.Tanh, bias=half_rz[:, 0:1], scale=0.5)
                            nc.scalar.activation(ez[:, :], ps_g[1][:, :], ACT.Tanh, bias=half_rz[:, 1:2], scale=0.5).then_inc(s_e, 1)
                            act.wait_ge(s_n, q + 1)
                            nc.scalar.activation(nn[:, :], nn[:, :], ACT.Tanh, bias=b_ih[:, 2:3]).then_inc(s_t, 1)

        def ggn_out(link, st, t3, x3):
            link(nc.vector.tensor_tensor(t3, acc[:, :].rearrange("p (b d) -> p b d", d=D), x3, ALU.add))

        QW = D + HEADS + 1
        rel = ExitStack()
        qx = sb(rel, "qx", [P, NBP * QW])
        mrun = sb(rel, "mrun", [P, NBP * HEADS])
        zrel = sb(rel, "zrel", [P, NBP * HEADS])

        def rel_start(eng, v, s_pre, s_act):
            if v is not None:
                v.memset(acc[:, :], 0.0)
                v.memset(zrel[:, :], 0.0)
                v.memset(mrun[:, :], -BIG)

        def rel_give(dve, v, q, ps_c, xs, gsb, scr, s_ch):
            def bias(b):
                return b[:, :].unsqueeze(1).to_broadcast([P, 4, D])
            q3 = quad(qx, q, QW).rearrange("p (j c) -> p j c", c=QW)
            v.tensor_copy(gsb[:, :, 0:D], xs[:, :].rearrange("p (j d) -> p j d", d=D))
            v.tensor_tensor(gsb[:, :, D:2 * D], ps_c[:, :, 0:D], bias(b_1), ALU.add)
            v.tensor_tensor(scr[:, :, :], ps_c[:, :, D:2 * D], bias(b_q), ALU.add).then_inc(s_ch, 1)
            dve.wait_ge(s_ch, q * 3 + 1)
            v.tensor_scalar(scr[:, :, :], scr[:, :, :], float(HD) ** -0.5, None, ALU.mult).then_inc(s_ch, 1)
            dve.wait_ge(s_ch, q * 3 + 2)
            v.tensor_scalar(q3[:, :, 0:D], scr[:, :, :], 1.0, None, ALU.mult)
            v.tensor_tensor(xs[:, :].rearrange("p (j d) -> p j d", d=D), scr[:, :, :], bias(b_k), ALU.mult).then_inc(s_ch, 1)
            dve.wait_ge(s_ch, q * 3 + 3)
            v.tensor_reduce(scr[:, :, 0:HEADS], xs[:, :].rearrange("p (j h d) -> p j h d", h=HEADS, d=HD), AX, ALU.add).then_inc(s_ch2, 1)
            dve.wait_ge(s_ch2, q + 1)
            v.tensor_scalar(q3[:, :, D:D + HEADS], scr[:, :, 0:HEADS], 1.0, None, ALU.mult)
            return v.tensor_copy(q3[:, :, D + HEADS:QW], nv[:, bass.ds(q * 4, 4)].unsqueeze(2))

        s_ch2 = sem(top, "rel_chain2")

        def rel_edges():
            with phase() as st:
                oh = sb(st, "r_oh", [P, 2, GT, P])
                ot = sb(st, "r_ot", [P, 2, GE])
                to = sb(st, "r_to", [P, GT, TYPES])
                tt = sb(st, "r_tt", [TYPES, GE])
                rsx = sb(st, "r_rsx", [P, 2, GT, HEADS])
                rsT = sb(st, "r_rsT", [HEADS, GE])
                qs = sb(st, "r_qs", [P, GT, D + HEADS])
                sm = sb(st, "r_sm", [P, 6, GT])
                hm = tmp[:, 0 * GT * D:1 * GT * D].rearrange("p (t d) -> p t d", d=D)
                junk = tmp[:, 1 * GT * D:2 * GT * D].rearrange("p (t d) -> p t d", d=D)
                msg = tmp[:, 2 * GT * D:3 * GT * D].rearrange("p (t d) -> p t d", d=D)
                msgT = sb(st, "r_msgT", [P, GE])
                pq = tmp[:, 3 * GT * D:4 * GT * D].rearrange("p (t d) -> p t d", d=D)
                sc = sb(st, "r_sc", [P, 2, GT, HEADS])
                vs = sb(st, "r_vs", [P, 2, GT, D])
                F = sb(st, "r_F", [HEADS, 2, GE])
                fg = sb(st, "r_fg", [P, GT, HEADS + 1])
                mn = sb(st, "r_mn", [P, HEADS])
                df = sb(st, "r_df", [P, HEADS])
                nh = sb(st, "r_nh", [P, 1])
                al = sb(st, "r_al", [P, HEADS])
                sd = sb(st, "r_sd", [P, GT, HEADS])
                wv = sb(st, "r_wv", [P, GT, D + HEADS])
                at = sb(st, "r_at", [P, D])
                zt = sb(st, "r_zt", [P, HEADS])
                ps_ot = ps(st, "r_psot", [P, GE])
                ps_tt = ps(st, "r_pstt", [TYPES, GE])
                ps_q = ps(st, "r_psq", [P, GT, 256])
                ps_r = ps(st, "r_psr", [P, GT, 256])
                ps_b0 = ps(st, "r_psb0", [P, 512])
                ps_b1 = ps(st, "r_psb1", [P, 512])
                names = ("sr idx oh oht ot qr dt ez qs hc dz dw mt mT kv sc sT rs FT fg M al me sd we wv o ca cb").split()
                S = {n: sem(st, "r_" + n) for n in names}
                s_row = [sem(st, f"r_row{k}") for k in range(RING)]
                s_msg = sem(st, "r_msg_ready")
                s_acc = sem(st, "r_sums_added")
                s_mn = sem(st, "r_new_max")
                s_v = sem(st, "r_values_ready")
                s_F = sem(st, "r_scan_done")
                NCA, NCB = 8, 5
                T = [slice(t * P, (t + 1) * P) for t in range(GT)]

                def blk(eng, v):
                    return eng.value_load(blk_row[0:1, bass.ds(v, 1)], min_val=0, max_val=BLOCKS - 1)

                with nc.Block() as block:
                    @block.gpsimd
                    def _(pool):
                        pool.sem_inc(s_msg, RING)
                        gather_rows(pool, rel_tab, 2 * D, S["idx"], s_row, s_msg)

                    @block.vector
                    def _(dve):
                        v_ = nc.vector

                        def a1(v, k):
                            for t in range(GT):
                                v_.tensor_scalar(oh[:, k % 2, t, :], iota[:, :], dst_tab[:, bass.ds(v * GT + t, 1)], None, ALU.is_equal)
                                v_.tensor_scalar(to[:, t, :], iota[:, 0:TYPES], typ_tab[:, bass.ds(v * GT + t, 1)], None, ALU.is_equal)
                            v_.tensor_copy(rsx[:, k % 2, :, :], wide(reset_tab[:, bass.ds(v * GT, GT)], HEADS)).then_inc(S["oh"], 1)

                        def a2(v, k):
                            dve.wait_ge(S["qr"], v + 1)
                            v_.tensor_tensor(sm[:, 0, :], ps_q[:, :, D + HEADS:QW].rearrange("p t o -> p (t o)"),
                                             w_tab[:, bass.ds(v * GT, GT)], ALU.subtract).then_inc(S["ca"], 1)
                            dve.wait_ge(S["ca"], v * NCA + 1)
                            v_.tensor_scalar(sm[:, 0, :], sm[:, 0, :], low_t[:, :], None, ALU.max).then_inc(S["dt"], 1)

                        def a3(v, k, fill):
                            dve.wait_ge(S["ez"], v + 1)
                            v_.tensor_scalar(sm[:, 2, :], sm[:, 1, :], 1.0, None, ALU.add).then_inc(S["ca"], 1)
                            dve.wait_ge(S["ca"], v * NCA + 2)
                            v_.reciprocal(sm[:, 2, :], sm[:, 2, :]).then_inc(S["ca"], 1)
                            dve.wait_ge(S["ca"], v * NCA + 3)
                            dve.wait_ge(s_row[k % RING], fill)
                            for t in range(GT):
                                i = v_.scalar_tensor_tensor(hm[:, t, :], ps_r[:, t, D:2 * D], sm[:, 2, t:t + 1], rows[:, k % RING, t, D:2 * D],
                                                            ALU.mult, ALU.add)
                            i.then_inc(S["ca"], 1)
                            dve.wait_ge(S["ca"], v * NCA + 4)
                            for t in range(GT):
                                i = v_.scalar_tensor_tensor(junk[:, t, :], hm[:, t, :], 0.0, w_2[:, :], ALU.max, ALU.mult,
                                                            accum_out=sm[:, 3, t:t + 1])
                            i.then_inc(S["hc"], 1)
                            dve.wait_ge(S["hc"], v + 1)
                            v_.tensor_scalar(sm[:, 3, :], sm[:, 3, :], low_d[:, :], None, ALU.max).then_inc(S["dz"], 1)

                        def a4(v, k):
                            dve.wait_ge(S["dw"], v + 1)
                            v_.tensor_scalar(sm[:, 5, :], sm[:, 4, :], 1.0, None, ALU.add).then_inc(S["ca"], 1)
                            dve.wait_ge(S["ca"], v * NCA + 5)
                            v_.reciprocal(sm[:, 5, :], sm[:, 5, :]).then_inc(S["ca"], 1)
                            dve.wait_ge(S["ca"], v * NCA + 6)
                            v_.tensor_tensor(sm[:, 5, :], sm[:, 5, :], sm[:, 2, :], ALU.mult).then_inc(S["ca"], 1)
                            dve.wait_ge(S["ca"], v * NCA + 7)
                            for t in range(GT):
                                i = v_.scalar_tensor_tensor(msg[:, t, :], ps_r[:, t, 0:D], sm[:, 5, t:t + 1], rows[:, k % RING, t, 0:D],
                                                            ALU.mult, ALU.mult)
                            i.then_inc(s_msg, 1)

                        def a5(v, k):
                            dve.wait_ge(S["kv"], v + 1)
                            dve.wait_ge(S["qs"], v + 1)
                            v_.tensor_tensor(pq[:, :, :], ps_r[:, :, 0:D], qs[:, :, 0:D], ALU.mult).then_inc(S["ca"], 1)
                            dve.wait_ge(S["ca"], v * NCA + 8)
                            v_.tensor_reduce(sc[:, k % 2, :, :].rearrange("p t h -> p (t h)"),
                                             pq[:, :, :].rearrange("p t (h d) -> p (t h) d", d=HD), AX, ALU.add).then_inc(S["sr"], 1)
                            dve.wait_ge(S["sr"], v + 1)
                            v_.tensor_tensor(sc[:, k % 2, :, :], sc[:, k % 2, :, :], qs[:, :, D:D + HEADS], ALU.add).then_inc(S["sc"], 1)

                        def b1(v, k):
                            dve.wait_ge(S["rs"], v + 1)
                            dve.wait_ge(s_F, v + 1)
                            v_.tensor_tensor_scan(F[:, k % 2, :], rsT[:, :], ps_b0[0:HEADS, :], F[:, (k + 1) % 2, GE - 1:GE],
                                                  ALU.add, ALU.max).then_inc(s_F, 1)

                        def b2(v, k):
                            gl = glast_tab[:, bass.ds(v * GT, GT)]
                            dve.wait_ge(S["FT"], v + 1)
                            v_.tensor_tensor(fg[:, :, 0:HEADS], ps_b1[:, 0:GT * HEADS].rearrange("p (t h) -> p t h", h=HEADS),
                                             wide(gl, HEADS), ALU.mult)
                            v_.tensor_copy(fg[:, :, HEADS:HEADS + 1], gl.unsqueeze(2)).then_inc(S["fg"], 1)

                        def b3(v, k):
                            b = blk(dve, v)
                            mo = mrun[:, bass.ds(b * HEADS, HEADS)]
                            dve.wait_ge(S["M"], v + 1)
                            v_.tensor_scalar(nh[:, :], ps_b0[:, HEADS:HEADS + 1], -1.0, 1.0, ALU.mult, ALU.add).then_inc(S["cb"], 1)
                            dve.wait_ge(s_mn, v + 1)
                            dve.wait_ge(S["cb"], v * NCB + 1)
                            v_.scalar_tensor_tensor(mn[:, :], mo, nh[:, :], ps_b0[:, 0:HEADS], ALU.mult, ALU.add).then_inc(S["cb"], 1)
                            dve.wait_ge(S["cb"], v * NCB + 2)
                            v_.tensor_tensor(df[:, :], mo, mn[:, :], ALU.subtract).then_inc(S["cb"], 1)
                            dve.wait_ge(S["cb"], v * NCB + 3)
                            v_.tensor_scalar(mo, mn[:, :], 1.0, None, ALU.mult).then_inc(s_mn, 1)

                        def b4(v, k):
                            dve.wait_ge(S["me"], v + 1)
                            v_.tensor_tensor(sd[:, :, :], sc[:, k % 2, :, :], ps_b1[:, 64:64 + GT * HEADS].rearrange("p (t h) -> p t h", h=HEADS),
                                             ALU.subtract).then_inc(S["sd"], 1)

                        def b5(v, k):
                            dve.wait_ge(S["we"], v + 1)
                            dve.wait_ge(s_v, v + 2)
                            v_.tensor_tensor(wv[:, :, 0:D].rearrange("p t (h d) -> p t h d", d=HD),
                                             vs[:, k % 2, :, :].rearrange("p t (h d) -> p t h d", d=HD),
                                             wv[:, :, D:D + HEADS].unsqueeze(3).to_broadcast([P, GT, HEADS, HD]), ALU.mult).then_inc(S["wv"], 1)

                        def b6(v, k):
                            b = blk(dve, v)
                            ab = acc[:, bass.ds(b * D, D)]
                            zb = zrel[:, bass.ds(b * HEADS, HEADS)]
                            dve.wait_ge(S["al"], v + 1)
                            dve.wait_ge(s_acc, v + 1)
                            v_.tensor_tensor(at[:, :].rearrange("p (h d) -> p h d", d=HD), ab.rearrange("p (h d) -> p h d", d=HD),
                                             wide(al[:, :], HD), ALU.mult).then_inc(S["cb"], 1)
                            v_.tensor_tensor(zt[:, :], zb, al[:, :], ALU.mult).then_inc(S["cb"], 1)
                            dve.wait_ge(S["o"], v + 1)
                            dve.wait_ge(S["cb"], v * NCB + 5)
                            v_.tensor_tensor(ab, at[:, :], ps_b0[:, P:P + D], ALU.add)
                            v_.tensor_tensor(zb, zt[:, :], ps_b0[:, P + D:P + D + HEADS], ALU.add).then_inc(s_acc, 1)

                        v_.memset(F[:, 1, :], -BIG).then_inc(s_F, 1)
                        dve.sem_inc(s_acc, 1)
                        dve.sem_inc(s_mn, 1)
                        dve.sem_inc(s_v, 1)
                        a1(0, 0)
                        a2(0, 0)
                        a3(0, 0, 16 * GT)
                        a4(0, 0)
                        a5(0, 0)

                        def both(v, k, fill):
                            a1(v + 1, k + 1)
                            b1(v, k)
                            a2(v + 1, k + 1)
                            b2(v, k)
                            a3(v + 1, k + 1, fill)
                            b3(v, k)
                            a4(v + 1, k + 1)
                            b4(v, k)
                            b5(v, k)
                            a5(v + 1, k + 1)
                            b6(v, k)

                        whole = (V - 1) // RING
                        with dve.Fori(0, whole) as i:
                            for k in range(RING):
                                both(i * RING + k, k, (i + (2 if k == RING - 1 else 1)) * (16 * GT))
                        for v in range(whole * RING, V - 1):
                            both(v, v % RING, ((v + 1) // RING + 1) * 16 * GT)
                        v, k = V - 1, (V - 1) % RING
                        b1(v, k)
                        b2(v, k)
                        b3(v, k)
                        b4(v, k)
                        b5(v, k)
                        b6(v, k)
                        dve.wait_ge(s_acc, V + 1)

                    @block.tensor
                    def _(pe):
                        mm, tr = nc.tensor.matmul, nc.tensor.transpose

                        def a1(v, k):
                            pe.wait_ge(S["oh"], v + 1)
                            for t in range(GT):
                                tr(ps_ot[:, T[t]], oh[:, k % 2, t, :], ident[:, :])
                                i = tr(ps_tt[:, T[t]], to[:, t, :], ident[:, :])
                            i.then_inc(S["oht"], 1)

                        def a2(v, k):
                            b = blk(pe, v)
                            pe.wait_ge(s_v, v + 1)
                            pe.wait_ge(S["ot"], v + 1)
                            for t in range(GT):
                                mm(ps_q[:, t, 0:QW], ot[:, k % 2, T[t]], qx[:, bass.ds(b * QW, QW)], start=True, stop=True)
                                i = mm(ps_r[:, t, :], tt[:, T[t]], relR[:, :], start=True, stop=True)
                            i.then_inc(S["qr"], 1)

                        def a3(v, k):
                            pe.wait_ge(s_msg, v + 1 + RING)
                            for t in range(GT):
                                i = tr(ps_ot[:, T[t]], msg[:, t, :], ident[:, :])
                            i.then_inc(S["mt"], 1)

                        def a4(v, k):
                            pe.wait_ge(S["mT"], v + 1)
                            for t in range(GT):
                                i = mm(ps_r[:, t, :], msgT[:, T[t]], w_kv[:, :, :].rearrange("p a d -> p (a d)"), start=True, stop=True)
                            i.then_inc(S["kv"], 1)

                        def b1(v, k):
                            pe.wait_ge(s_acc, v + 1)
                            pe.wait_ge(S["sc"], v + 1)
                            for t in range(GT):
                                tr(ps_b0[0:HEADS, T[t]], sc[:, k % 2, t, :], ident[:, :])
                                i = tr(ps_b1[0:HEADS, T[t]], rsx[:, k % 2, t, :], ident[:, :])
                            i.then_inc(S["sT"], 1)

                        def b2(v, k):
                            pe.wait_ge(s_F, v + 2)
                            for t in range(GT):
                                i = mm(ps_b1[:, t * HEADS:(t + 1) * HEADS], F[:, k % 2, T[t]], ident[0:HEADS, 0:HEADS], start=True, stop=True)
                            i.then_inc(S["FT"], 1)

                        def b3(v, k):
                            pe.wait_ge(S["fg"], v + 1)
                            for t in range(GT):
                                i = mm(ps_b0[:, 0:HEADS + 1], oh[:, k % 2, t, :], fg[:, t, :], start=(t == 0), stop=(t == GT - 1))
                            i.then_inc(S["M"], 1)

                        def b4(v, k):
                            pe.wait_ge(s_mn, v + 2)
                            for t in range(GT):
                                i = mm(ps_b1[:, 64 + t * HEADS:64 + (t + 1) * HEADS], ot[:, k % 2, T[t]], mn[:, :], start=True, stop=True)
                            i.then_inc(S["me"], 1)

                        def b5(v, k):
                            pe.wait_ge(S["wv"], v + 1)
                            for t in range(GT):
                                i = mm(ps_b0[:, P:P + D + HEADS], oh[:, k % 2, t, :], wv[:, t, :], start=(t == 0), stop=(t == GT - 1))
                            i.then_inc(S["o"], 1)

                        a1(0, 0)
                        a2(0, 0)
                        a3(0, 0)
                        a4(0, 0)

                        def both(v, k):
                            b1(v, k)
                            a1(v + 1, k + 1)
                            a2(v + 1, k + 1)
                            b2(v, k)
                            b3(v, k)
                            b4(v, k)
                            a3(v + 1, k + 1)
                            a4(v + 1, k + 1)
                            b5(v, k)

                        steps(pe, both)
                        v, k = V - 1, (V - 1) % RING
                        b1(v, k)
                        b2(v, k)
                        b3(v, k)
                        b4(v, k)
                        b5(v, k)

                    @block.scalar
                    def _(act):
                        f = nc.scalar.activation

                        def a1(v, k):
                            act.wait_ge(S["oht"], v + 1)
                            f(ot[:, k % 2, :], ps_ot[:, :], ACT.Copy)
                            f(tt[:, :], ps_tt[:, :], ACT.Copy).then_inc(S["ot"], 1)

                        def a2(v, k):
                            act.wait_ge(S["dt"], v + 1)
                            f(sm[:, 1, :], sm[:, 0, :], ACT.Exp, scale=rtc[:, :]).then_inc(S["ez"], 1)
                            f(qs[:, :, :], ps_q[:, :, 0:D + HEADS], ACT.Copy).then_inc(S["qs"], 1)

                        def a3(v, k):
                            act.wait_ge(S["dz"], v + 1)
                            f(sm[:, 4, :], sm[:, 3, :], ACT.Exp, scale=-1.0, bias=neg_b2[:, :]).then_inc(S["dw"], 1)

                        def a4(v, k):
                            act.wait_ge(S["mt"], v + 1)
                            f(msgT[:, :], ps_ot[:, :], ACT.Copy).then_inc(S["mT"], 1)

                        def a5(v, k):
                            act.wait_ge(S["sc"], v + 1)
                            f(vs[:, k % 2, :, :], ps_r[:, :, D:2 * D], ACT.Copy).then_inc(s_v, 1)

                        def b1(v, k):
                            act.wait_ge(S["sT"], v + 1)
                            f(rsT[:, :], ps_b1[0:HEADS, :], ACT.Copy).then_inc(S["rs"], 1)

                        def b2(v, k):
                            act.wait_ge(s_mn, v + 2)
                            f(al[:, :], df[:, :], ACT.Exp).then_inc(S["al"], 1)

                        def b3(v, k):
                            act.wait_ge(S["sd"], v + 1)
                            f(wv[:, :, D:D + HEADS], sd[:, :, :], ACT.Exp).then_inc(S["we"], 1)

                        a1(0, 0)
                        a2(0, 0)
                        a3(0, 0)
                        a4(0, 0)
                        a5(0, 0)

                        def both(v, k):
                            b1(v, k)
                            a1(v + 1, k + 1)
                            a2(v + 1, k + 1)
                            a3(v + 1, k + 1)
                            b2(v, k)
                            b3(v, k)
                            a4(v + 1, k + 1)
                            a5(v + 1, k + 1)

                        steps(act, both)
                        v, k = V - 1, (V - 1) % RING
                        b1(v, k)
                        b2(v, k)
                        b3(v, k)

        def rel_out(link, st, t3, x3):
            v = nc.vector
            rz = sb(st, "ro_rz", [P, NBP * HEADS])
            has = sb(st, "ro_has", [P, NBP * HEADS])

            def heads(t):
                return t[:, :].rearrange("p (b d) -> p b d", d=HD)

            link(v.tensor_scalar(rz[:, :], zrel[:, :], 1e-30, None, ALU.max))
            link(v.reciprocal(rz[:, :], rz[:, :]))
            link(v.tensor_scalar(has[:, :], zrel[:, :], 0.0, None, ALU.is_gt))
            link(v.tensor_tensor(heads(tmp), heads(acc), wide(rz[:, :], HD), ALU.mult))
            link(v.tensor_tensor(acc[:, :].rearrange("p (b d) -> p b d", d=D), every(b_v),
                                 has[:, :].rearrange("p (b h) -> p b h", h=HEADS)[:, :, 0:1].to_broadcast([P, NBP, D]), ALU.mult))
            link(v.tensor_tensor(t3, t3, acc[:, :].rearrange("p (b d) -> p b d", d=D), ALU.add))
            link(v.tensor_tensor(t3, t3, x3, ALU.add))

        gat_nodes(0)
        gat_edges(0)
        gat_nodes(1)
        gat_edges(1)
        residual_norm("ln0", gat_out)
        table_nodes("gcn", take_x, None, None, None, w_gcn[:, :], D, gcn_tab, D, gcn_give, gcn_start)
        sum_edges("gcn_e", gcn_tab, True)
        residual_norm("ln1", gcn_out)
        table_nodes("reln", take_x, None, None, None, w_xq[:, :, :].rearrange("p a d -> p (a d)"), 2 * D, rel_tab, 2 * D,
                    rel_give, rel_start)
        rel_edges()
        residual_norm("ln2", rel_out)
        table_nodes("ggn", take_x, w_inT, b_in, tmp, w_msg[:, :], D, ggn_tab, D, ggn_give, ggn_start)
        sum_edges("ggn_e", ggn_tab, False)
        ggn_gates()
        residual_norm("ln3", ggn_out)
        rel.close()
        gat.close()
        s = sem(top, 'out_stored')
        with nc.Block() as block:
            @block.sync
            def _(sp):
                sp.dma_start(out[0:(BLOCKS - 1) * P, :].rearrange("(b p) d -> p b d", p=P), x_n[:, 0:(BLOCKS - 1) * D].rearrange("p (b d) -> p b d", d=D)).then_inc(s, 16)
                sp.dma_start(out[(BLOCKS - 1) * P:N, :], x_n[0:N - (BLOCKS - 1) * P, (BLOCKS - 1) * D:BLOCKS * D]).then_inc(s, 16)
                sp.wait_ge(s, 32)


_INS = ['x', 'src', 'dst', 'edge_type_64', 'edge_weight', 'node_vec', 'L0_gnn_W_node', 'L0_gnn_b_node', 'L0_gnn_lyr_W',
        'L0_gnn_att_src', 'L0_gnn_att_dst', 'L0_gnn_lyr_bias', 'L1_gnn_W', 'L1_gnn_b', 'L2_gnn_rel_table', 'L2_gnn_Wq',
        'L2_gnn_bq', 'L2_gnn_Wk', 'L2_gnn_bk', 'L2_gnn_Wv', 'L2_gnn_bv', 'L2_gnn_W1', 'L2_gnn_b1', 'L2_gnn_W2', 'L2_gnn_b2',
        'L2_gnn_time_coeff', 'L3_gnn_W_in', 'L3_gnn_b_in', 'L3_gnn_W_msg', 'L3_gnn_W_ih', 'L3_gnn_b_ih', 'L3_gnn_W_hh',
        'L3_gnn_b_hh', 'L3_gnn_W_out', 'L3_gnn_b_out']


def kernel(**inputs):
    import concourse.bacc as _bacc
    from concourse.bass_utils import run_bass_kernel_spmd as _run

    nc = _bacc.Bacc("TRN2", target_bir_lowering=False, num_devices=1)
    arrays, args = {}, {}
    for name in _INS:
        a = np.ascontiguousarray(inputs[name])
        if a.ndim == 0:
            a = a.reshape(1)
        arrays[f"in_{name}"] = a
        args[name] = nc.dram_tensor(f"in_{name}", a.shape, mybir.dt.from_np(a.dtype), kind="ExternalInput").ap()
    out = nc.dram_tensor("out_0", (N, D), F32, kind="ExternalOutput").ap()
    build(nc, args, out)
    r = _run(nc, [arrays], core_ids=[0])
    return r.results[0]["out_0"]
```

```python
from contextlib import ExitStack, contextmanager

import numpy as np

import concourse.bass as bass
from concourse import mybir

F32 = mybir.dt.float32
I32 = mybir.dt.int32
BF16 = mybir.dt.bfloat16
ALU = mybir.AluOpType
ACT = mybir.ActivationFunctionType
AX = mybir.AxisListType.X

P = 128
N = 6250
E = 100000
D = 128
BLOCKS = -(-N // P)
QUADS = -(-BLOCKS // 4)
NBP = QUADS * 4
NPAD = NBP * P
GT = 4
GE = GT * P
GROUPS = -(-E // GE)
HALF_G = GROUPS // 2
TILES = GROUPS * GT
V = GROUPS + BLOCKS - 1
VC = -(-V // P)
VP = VC * P
FULL = E // GE
REST = E - FULL * GE
PAD = GE - REST
NO_NODE = 8191
BIG = float(2.0 ** 100)
RING = 4
SLOTS = 7
SLOPE = 0.2
EPS = 1e-5
HEADS = 8
HD = D // HEADS
TYPES = 64


class Count:

    def __init__(self, sem):
        self.sem, self.n = sem, 0

    def inc(self, ins, by=1):
        ins.then_inc(self.sem, by)
        self.n += by
        return self.n


def build(nc, A, out):
    top = ExitStack()
    with top:
        def sb(stack, name, shape, dt=F32):
            return stack.enter_context(nc.sbuf_tensor(name, shape, dt))

        def ps(stack, name, shape, dt=F32):
            return stack.enter_context(nc.psum_tensor(name, shape, dt))

        used = []

        def sem(stack, name):
            s = stack.enter_context(nc.semaphore(name))
            used.append(s)
            return s

        @contextmanager
        def phase():
            with ExitStack() as st:
                used.clear()
                yield st
                with nc.Block() as block:
                    @block.gpsimd
                    def _(pool):
                        for s in used:
                            pool.sem_clear(s)

        ident = sb(top, "ident", [P, P])
        iota = sb(top, "iota", [P, P])
        x_n = sb(top, "x_n", [P, NBP * D])
        acc = sb(top, "acc", [P, NBP * D])
        tmp = sb(top, "tmp", [P, NBP * D])
        dst_tab = sb(top, "dst_tab", [P, VP * GT])
        w_tab = sb(top, "w_tab", [P, VP * GT])
        blk_row = sb(top, "blk_row", [1, VP], I32)
        grp_row = sb(top, "grp_row", [1, VP], I32)
        src_g = sb(top, "src_g", [P, TILES], I32)
        dst_g = sb(top, "dst_g", [P, TILES], I32)
        w_g = sb(top, "w_g", [P, TILES])
        src_hi = sb(top, "src_hi", [P, TILES])
        dst_hi = sb(top, "dst_hi", [P, TILES])
        slot_row = sb(top, "slot_row", [1, VP], I32)
        done_row = sb(top, "done_row", [1, GROUPS], I32)
        src_slot = sb(top, "src_slot", [P, SLOTS, GT], I32)
        deg = sb(top, "deg", [P, NBP])

        edge_rows = nc.dram_tensor("edge_rows", (GROUPS, 4 * GE), I32).ap()
        dst_flat = nc.dram_tensor("dst_flat", (GROUPS * GE + 2,), I32).ap()
        type_rows = nc.dram_tensor("type_rows", (GROUPS, GE), BF16).ap()
        lo_rows = nc.dram_tensor("lo_rows", (GROUPS, 2 * GE), BF16).ap()
        edge_v = nc.dram_tensor("edge_v", (GROUPS * P, GE), F32).ap()
        gat_tab = [nc.dram_tensor(f"gat_tab{l}", (NPAD, D), F32).ap() for l in range(2)]
        gcn_tab = nc.dram_tensor("gcn_tab", (NPAD, D), F32).ap()
        q_tab = nc.dram_tensor("q_tab", (NPAD, D + HEADS + 1), F32).ap()
        rel_tab = nc.dram_tensor("rel_tab", (NPAD, 2 * D), F32).ap()
        ggn_tab = nc.dram_tensor("ggn_tab", (NPAD, D), F32).ap()

        def row(ap):
            return ap.rearrange("(o f) -> o f", o=1)

        with phase() as st:
            padv = sb(st, "padv", [1, 2, PAD + 8], I32)
            grow = sb(st, "grow", [HALF_G, 2, 4 * GE], I32)
            gf = sb(st, "gf", [HALF_G, 2, 3, GE])
            tb = sb(st, "tb", [HALF_G, 2, GE], BF16)
            lo_i = sb(st, "lo_i", [HALF_G, 2, 2 * GE], I32)
            lo = sb(st, "lo", [HALF_G, 2, 2 * GE], BF16)
            hi_i = sb(st, "hi_i", [P, 2, TILES], I32)
            gmax = sb(st, "gmax", [HALF_G, 2], I32)
            gsh = sb(st, "gsh", [HALF_G, 2], I32)
            last = sb(st, "last", [HALF_G, 2])
            giota = sb(st, "giota", [HALF_G, 2], I32)
            giotaf = sb(st, "giotaf", [HALF_G, 2])
            viota = sb(st, "viota", [P, VC], I32)
            viotaf = sb(st, "viotaf", [P, VC])
            iota_i = sb(st, "iota_i", [P, P], I32)
            cmp = sb(st, "cmp", [P, VC, GROUPS])
            gv = sb(st, "gv", [P, VC])
            gvi = sb(st, "gvi", [P, VC], I32)
            bv = sb(st, "bv", [P, VC])
            bv128 = sb(st, "bv128", [P, VC])
            er = sb(st, "er", [P, VC, 4, GE], I32)
            ef = sb(st, "ef", [P, VC, 2, GE])
            ps_last = ps(st, "ps_last", [P, GROUPS])
            ps_blk = ps(st, "ps_blk", [1, VP])
            ps_grp = ps(st, "ps_grp", [1, VP])
            ps_slot = ps(st, "ps_slot", [1, VP])
            slotv = sb(st, "slotv", [P, VC])
            mult = sb(st, "mult", [P, GROUPS // SLOTS])
            ps_tr = ps(st, "ps_tr", [P, 2, GE])
            s_c = sem(st, "p_c")
            s_cp = sem(st, "p_cp")
            s_pad = sem(st, "p_pad")
            s_dr = sem(st, "p_dr")
            s_dl = sem(st, "p_dl")
            s_last = sem(st, "p_last")
            s_pl = sem(st, "p_pl")
            s_gv = sem(st, "p_gv")
            s_er = top.enter_context(nc.semaphore("p_edge_rows"))
            s_ef = sem(st, "p_ef")
            s_tr = sem(st, "p_tr")
            s_trc = sem(st, "p_trc")
            s_x = sem(st, "p_x")
            s_bv = sem(st, "p_bv")
            s_tb = sem(st, "p_types")
            s_gf = sem(st, "p_group_arrays")
            s_z = sem(st, "p_z")
            with nc.Block() as block:
                @block.sync
                def _(sp):
                    n = 0
                    sp.wait_ge(s_pad, 2)
                    for a, name in enumerate(("dst", "src", "edge_type_64", "edge_weight")):
                        arr = A[name] if a < 3 else A[name].bitcast(I32)
                        sp.dma_start(edge_rows[0:FULL, a * GE:(a + 1) * GE],
                                     arr[0:FULL * GE].rearrange("(g e) -> g e", e=GE)).then_inc(s_dr, 16)
                        sp.dma_start(edge_rows[FULL:GROUPS, a * GE:a * GE + REST],
                                     row(arr[FULL * GE:E])).then_inc(s_dr, 16)
                        sp.dma_start(edge_rows[FULL:GROUPS, a * GE + REST:(a + 1) * GE],
                                     padv[0:1, 0 if a == 0 else 1, 0:PAD]).then_inc(s_dr, 16)
                    dst = A["dst"]
                    sp.dma_start(row(dst_flat[0:1]), padv[0:1, 0, 0:1]).then_inc(s_dr, 16)
                    sp.dma_start(row(dst_flat[1:1 + E]), row(dst)).then_inc(s_dr, 16)
                    sp.dma_start(row(dst_flat[1 + E:GROUPS * GE + 2]), padv[0:1, 0, 0:PAD + 1]).then_inc(s_dr, 16)
                    n = 15 * 16
                    sp.wait_ge(s_dr, n)
                    sp.dma_start(grow[:, :, :], edge_rows[:, :].rearrange("(c p) e -> p c e", c=2)).then_inc(s_dl, 16)
                    sp.wait_ge(s_z, 1)
                    sp.dma_start(x_n[:, 0:(BLOCKS - 1) * D].rearrange("p (b d) -> p b d", d=D),
                                 A["x"][0:(BLOCKS - 1) * P, :].rearrange("(b p) d -> p b d", p=P)).then_inc(s_x, 16)
                    sp.dma_start(x_n[0:N - (BLOCKS - 1) * P, (BLOCKS - 1) * D:BLOCKS * D],
                                 A["x"][(BLOCKS - 1) * P:N, :]).then_inc(s_x, 16)
                    sp.wait_ge(s_tb, 1)
                    sp.dma_start(type_rows[:, :].rearrange("(c p) e -> p c e", c=2), tb[:, :, :]).then_inc(s_x, 16)
                    sp.wait_ge(s_tb, 2)
                    sp.dma_start(lo_rows[:, :].rearrange("(c p) e -> p c e", c=2), lo[:, :, :]).then_inc(s_x, 16)
                    sp.wait_ge(s_x, 64)

                @block.gpsimd
                def _(pool):
                    g = nc.gpsimd
                    g.iota(giota[:, :], pattern=[[HALF_G, 2]], base=0, channel_multiplier=1).then_inc(s_cp, 1)
                    g.iota(viota[:, :], pattern=[[P, VC]], base=0, channel_multiplier=1).then_inc(s_cp, 1)
                    g.iota(iota_i[:, :], pattern=[[1, P]], base=0, channel_multiplier=0).then_inc(s_cp, 1)
                    g.memset(ident[:, :], 0.0).then_inc(s_cp, 1)
                    pool.wait_ge(s_cp, 4)
                    g.affine_select(out=ident[:, :], in_=ident[:, :], compare_op=ALU.not_equal, fill=1.0,
                                    base=0, pattern=[[-1, P]], channel_multiplier=1).then_inc(s_cp, 1)
                    pool.wait_ge(s_gv, 1)
                    for c in range(VC):
                        pool.indirect_dma_start(er[:, c, :, :].rearrange("p a e -> p (a e)"), None, edge_rows[:, :],
                                                bass.IndirectOffsetOnAxis(ap=gvi[:, c:c + 1], axis=0)).then_inc(s_er, 16)

                @block.vector
                def _(dve):
                    v = nc.vector
                    c = Count(s_c)

                    def link(ins):
                        dve.wait_ge(s_c, c.inc(ins))

                    v.memset(padv[0:1, 0, :], NO_NODE).then_inc(s_pad, 1)
                    v.memset(padv[0:1, 1, :], 0).then_inc(s_pad, 1)
                    v.memset(x_n[:, :], 0.0).then_inc(s_z, 1)
                    dve.wait_ge(s_cp, 5)
                    v.tensor_copy(giotaf[:, :], giota[:, :])
                    v.tensor_copy(viotaf[:, :], viota[:, :])
                    link(v.tensor_copy(iota[:, :], iota_i[:, :]))
                    dve.wait_ge(s_dl, 16)
                    link(v.tensor_reduce(gmax[:, :], grow[:, :, 0:GE], AX, ALU.max))
                    link(v.tensor_scalar(gsh[:, :], gmax[:, :], 7, None, ALU.arith_shift_right))
                    link(v.tensor_scalar(last[:, :], gsh[:, :], float(BLOCKS - 1), None, ALU.min))
                    v.tensor_tensor(last[:, :], last[:, :], giotaf[:, :], ALU.add).then_inc(s_last, 1)
                    dve.wait_ge(s_pl, 1)
                    for k in range(VC):
                        link(v.tensor_scalar(cmp[:, k, :], ps_last[:, :], viotaf[:, k:k + 1], None, ALU.is_lt))
                    link(v.tensor_reduce(gv[:, :], cmp[:, :, :], AX, ALU.add))
                    link(v.tensor_scalar(gv[:, :], gv[:, :], float(GROUPS - 1), None, ALU.min))
                    v.tensor_copy(gvi[:, :], gv[:, :]).then_inc(s_gv, 1)
                    M = GROUPS // SLOTS
                    link(v.tensor_scalar(mult[:, :], iota[:, 0:M], float(SLOTS), None, ALU.mult))
                    for k in range(VC):
                        link(v.tensor_scalar(cmp[:, k, 0:M], mult[:, :], gv[:, k:k + 1], None, ALU.is_le))
                    link(v.tensor_reduce(slotv[:, :], cmp[:, :, 0:M], AX, ALU.add))
                    link(v.tensor_scalar(slotv[:, :], slotv[:, :], -1.0, -float(SLOTS), ALU.add, ALU.mult))
                    link(v.tensor_tensor(slotv[:, :], gv[:, :], slotv[:, :], ALU.add))
                    v.tensor_scalar(done_row[:, :], ps_last[0:1, :], 1.0, None, ALU.add)
                    link(v.tensor_tensor(bv[:, :], viotaf[:, :], gv[:, :], ALU.subtract))
                    link(v.tensor_scalar(bv[:, :], bv[:, :], float(BLOCKS - 1), None, ALU.min))
                    v.tensor_scalar(bv128[:, :], bv[:, :], float(P), None, ALU.mult).then_inc(s_bv, 1)
                    dve.wait_ge(s_bv, 1)
                    v.tensor_copy(tb[:, :, :], grow[:, :, 2 * GE:3 * GE]).then_inc(s_tb, 1)
                    link(v.tensor_scalar(lo_i[:, :, :], grow[:, :, 0:2 * GE], P - 1, None, ALU.bitwise_and))
                    v.tensor_copy(lo[:, :, :], lo_i[:, :, :]).then_inc(s_tb, 1)
                    link(v.tensor_copy(gf[:, :, 0:2, :], grow[:, :, 0:2 * GE].rearrange("p c (a e) -> p c a e", a=2)))
                    link(v.tensor_scalar(gf[:, :, 0, :], gf[:, :, 0, :], float(NPAD - 1), None, ALU.min))
                    v.tensor_copy(gf[:, :, 2, :], grow[:, :, 3 * GE:4 * GE].bitcast(F32)).then_inc(s_gf, 1)
                    dve.wait_ge(s_er, 16 * VC)
                    for k in range(VC):
                        link(v.tensor_copy(ef[:, k, 0, :], er[:, k, 0, :]))
                        link(v.tensor_copy(ef[:, k, 1, :], er[:, k, 3, :].bitcast(F32)))
                        v.tensor_scalar(ef[:, k, 0, :], ef[:, k, 0, :], bv128[:, k:k + 1], None, ALU.subtract).then_inc(s_ef, 1)
                    n = 0
                    for k in range(VC):
                        for a, tab in enumerate((dst_tab, w_tab)):
                            dve.wait_ge(s_tr, n + 1)
                            v.tensor_copy(tab[:, k * P * GT:(k + 1) * P * GT].rearrange("p (v t) -> p t v", t=GT),
                                          ps_tr[:, n % 2, :].rearrange("p (t v) -> p t v", t=GT)).then_inc(s_trc, 1)
                            n += 1
                    HT = HALF_G * GT
                    for half in range(2):
                        for a, tab in enumerate((dst_g, src_g, w_g)):
                            dve.wait_ge(s_tr, n + 1)
                            v.tensor_copy(tab[:, half * HT:(half + 1) * HT].rearrange("p (g t) -> p t g", t=GT),
                                          ps_tr[:, n % 2, 0:HT].rearrange("p (t g) -> p t g", t=GT)).then_inc(s_trc, 1)
                            n += 1
                    dve.wait_ge(s_tr, n + 1)
                    v.tensor_copy(grp_row[:, :], ps_grp[:, :])
                    v.tensor_copy(slot_row[:, :], ps_slot[:, :])
                    v.tensor_copy(blk_row[:, :], ps_blk[:, :]).then_inc(s_trc, 1)
                    dve.wait_ge(s_trc, n)
                    link(v.tensor_scalar(hi_i[:, 0, :], dst_g[:, :], 7, None, ALU.arith_shift_right))
                    link(v.tensor_scalar(hi_i[:, 1, :], src_g[:, :], 7, None, ALU.arith_shift_right))
                    link(v.tensor_copy(dst_hi[:, :], hi_i[:, 0, :]))
                    link(v.tensor_copy(src_hi[:, :], hi_i[:, 1, :]))
                    dve.wait_ge(s_trc, n + 1)

                @block.tensor
                def _(pe):
                    pe.wait_ge(s_cp, 5)
                    pe.wait_ge(s_last, 1)
                    for c in range(2):
                        i = nc.tensor.matmul(ps_last[:, c * HALF_G:(c + 1) * HALF_G],
                                             last[:, c:c + 1].to_broadcast([HALF_G, P]), ident[0:HALF_G, 0:HALF_G],
                                             start=True, stop=True)
                    i.then_inc(s_pl, 1)
                    n = 0
                    pe.wait_ge(s_ef, VC)
                    for k in range(VC):
                        for a in range(2):
                            if n >= 2:
                                pe.wait_ge(s_trc, n - 1)
                            for t in range(GT):
                                i = nc.tensor.transpose(ps_tr[:, n % 2, t * P:(t + 1) * P],
                                                        ef[:, k, a, t * P:(t + 1) * P], ident[:, :])
                            i.then_inc(s_tr, 1)
                            n += 1
                    pe.wait_ge(s_gf, 1)
                    for c in range(2):
                        for a in range(3):
                            pe.wait_ge(s_trc, n - 1)
                            for t in range(GT):
                                i = nc.tensor.transpose(ps_tr[:, n % 2, t * HALF_G:(t + 1) * HALF_G],
                                                        gf[:, c, a, t * P:(t + 1) * P], ident[0:HALF_G, 0:HALF_G])
                            i.then_inc(s_tr, 1)
                            n += 1
                    pe.wait_ge(s_bv, 1)
                    for k in range(VC):
                        nc.tensor.matmul(ps_slot[:, k * P:(k + 1) * P], slotv[:, k:k + 1], ident[:, :], start=True, stop=True)
                        nc.tensor.matmul(ps_grp[:, k * P:(k + 1) * P], gv[:, k:k + 1], ident[:, :], start=True, stop=True)
                        i = nc.tensor.matmul(ps_blk[:, k * P:(k + 1) * P], bv[:, k:k + 1], ident[:, :], start=True, stop=True)
                    i.then_inc(s_tr, 1)

        def load(n, shape, src_ap):
            t = sb(top, "w_" + n, shape)
            loads.append((t, src_ap))
            return t

        def col(ap):
            return ap.rearrange("(p o) -> p o", o=1)

        def rep(ap):
            return ap.partition_broadcast(P)

        loads = []
        w_node = load("node", [P, D], A["L0_gnn_W_node"])
        b_node = load("b_node", [P, 1], col(A["L0_gnn_b_node"]))
        w_lyr = load("lyr", [P, 2, D], A["L0_gnn_lyr_W"].rearrange("l k f -> k l f"))
        att = load("att", [P, 2, 2], None)
        b_lyr = [load(f"b_lyr{l}", [P, D], rep(A["L0_gnn_lyr_bias"][l, :])) for l in range(2)]
        w_gcn = load("gcn", [P, D], A["L1_gnn_W"])
        b_gcn = load("b_gcn", [P, D], rep(A["L1_gnn_b"]))
        rel_t = load("rel", [2 * TYPES, D], None)
        w_xq = load("xq", [P, 2, D], None)
        w_1b = load("w1b", [P, D], A["L2_gnn_W1"][D:2 * D, :])
        w_1c = load("w1c", [P, D], rep(A["L2_gnn_W1"][2 * D, :]))
        b_1 = load("b1", [P, D], rep(A["L2_gnn_b1"]))
        w_2 = load("w2", [P, D], rep(A["L2_gnn_W2"].rearrange("k o -> (k o)")))
        b_2 = load("b2", [P, 1], rep(A["L2_gnn_b2"]))
        b_q = load("bq", [P, D], rep(A["L2_gnn_bq"]))
        b_k = load("bk", [P, D], rep(A["L2_gnn_bk"]))
        b_v = load("bv", [P, D], rep(A["L2_gnn_bv"]))
        w_kv = load("kv", [P, 2, D], None)
        tc = load("tc", [P, 1], rep(A["L2_gnn_time_coeff"]))
        w_in = load("in", [P, D], A["L3_gnn_W_in"])
        b_in = load("b_in", [P, 1], col(A["L3_gnn_b_in"]))
        w_msg = load("msg", [P, D], A["L3_gnn_W_msg"])
        w_ih = load("ih", [P, 3, D], A["L3_gnn_W_ih"].rearrange("(g p) k -> p g k", p=P))
        w_hh = load("hh", [P, 3, D], A["L3_gnn_W_hh"].rearrange("(g p) k -> p g k", p=P))
        b_ih = load("b_ih", [P, 3], None)
        b_hh = load("b_hh", [P, 3], None)
        w_out = load("out", [P, D], A["L3_gnn_W_out"])
        b_out = load("b_out", [P, D], rep(A["L3_gnn_b_out"]))
        loads = [x for x in loads if x[1] is not None]
        for l in range(2):
            loads.append((att[:, l, 0:1], col(A["L0_gnn_att_src"][l, :])))
            loads.append((att[:, l, 1:2], col(A["L0_gnn_att_dst"][l, :])))
        for i in range(2):
            loads.append((rel_t[i * TYPES:(i + 1) * TYPES, :], A["L2_gnn_rel_table"]))
        loads.append((w_xq[:, 0, :], A["L2_gnn_W1"][0:D, :]))
        loads.append((w_xq[:, 1, :], A["L2_gnn_Wq"]))
        loads.append((w_kv[:, 0, :], A["L2_gnn_Wk"]))
        loads.append((w_kv[:, 1, :], A["L2_gnn_Wv"]))
        for g in range(3):
            loads.append((b_ih[:, g:g + 1], col(A["L3_gnn_b_ih"][g * D:(g + 1) * D])))
            loads.append((b_hh[:, g:g + 1], col(A["L3_gnn_b_hh"][g * D:(g + 1) * D])))
        nv = sb(top, "nv", [P, NBP])

        w_gat = sb(top, "w_gat", [P, 2, D + 2])
        rel_hm = sb(top, "rel_hm", [P, 2 * D], BF16)
        rel_lo = sb(top, "rel_lo", [P, 2 * D], BF16)
        w_inT = sb(top, "w_inT", [P, D])
        w_ihT = sb(top, "w_ihT", [P, 3, D])
        w_hhT = sb(top, "w_hhT", [P, 3, D])
        w_outT = sb(top, "w_outT", [P, D])
        half_rz = sb(top, "half_rz", [P, 2])
        half_rtc = sb(top, "half_rtc", [P, 1])
        half_b2 = sb(top, "half_b2", [P, 1])
        dis = sb(top, "dis", [P, NBP])
        ones = sb(top, "ones", [P, 1])
        eps_c = sb(top, "eps_c", [P, 1])
        with phase() as st:
            wT = sb(st, "wT", [P, 2, D])
            relT = sb(st, "relT", [P, P])
            relR = sb(st, "relR", [P, 2 * D])
            rel_r1 = sb(st, "rel_r1", [P, 2 * D])
            rel_hi = sb(st, "rel_hi", [P, 2 * D], BF16)
            ps_t = [ps(st, f"ps_wt{i}", [P, D]) for i in range(2)]
            s_ld = sem(st, "w_ld")
            s_wt = sem(st, "w_t")
            s_wc = sem(st, "w_c")
            s_wd = sem(st, "w_d")
            s_nv = sem(st, "w_nv")
            NL = 16 * len(loads)
            trans = [(w_lyr[:, 0, :], wT[:, 0, :]), (w_lyr[:, 1, :], wT[:, 1, :]), (w_in[:, :], w_inT[:, :]),
                     (w_out[:, :], w_outT[:, :]), (rel_t[:, :], relT[:, :])]
            trans += [(w_ih[:, g, :], w_ihT[:, g, :]) for g in range(3)]
            trans += [(w_hh[:, g, :], w_hhT[:, g, :]) for g in range(3)]
            with nc.Block() as block:
                @block.sync
                def _(sp):
                    with nc.allow_non_contiguous_dma(reason="small bias columns"):
                        for dst, s in loads:
                            sp.dma_start(dst[tuple(slice(None) for _ in dst.shape)], s).then_inc(s_ld, 16)
                        sp.wait_ge(s_nv, 1)
                        sp.dma_start(nv[:, 0:BLOCKS - 1], A["node_vec"][0:(BLOCKS - 1) * P].rearrange("(b p) -> p b", p=P)).then_inc(s_ld, 16)
                        sp.dma_start(nv[0:N - (BLOCKS - 1) * P, BLOCKS - 1:BLOCKS],
                                     col(A["node_vec"][(BLOCKS - 1) * P:N])).then_inc(s_ld, 16)
                    sp.wait_ge(s_ld, NL + 32)

                @block.tensor
                def _(pe):
                    pe.wait_ge(s_ld, NL + 32)
                    n = 0
                    for n, (s, _) in enumerate(trans):
                        if n >= 2:
                            pe.wait_ge(s_wc, n - 1)
                        k, m = s.shape
                        nc.tensor.transpose(ps_t[n % 2][0:m, 0:k], s, ident[0:k, 0:k]).then_inc(s_wt, 1)
                    n = len(trans)
                    for l in range(2):
                        pe.wait_ge(s_wc, n - 1)
                        nc.tensor.matmul(ps_t[n % 2][:, 0:2], wT[:, l, :], att[:, l, :], start=True, stop=True).then_inc(s_wt, 1)
                        n += 1
                    pe.wait_ge(s_wc, n - 1)
                    nc.tensor.matmul(ps_t[n % 2][:, :], relT[:, :], w_1b[:, :], start=True, stop=True).then_inc(s_wt, 1)

                @block.vector
                def _(dve):
                    v = nc.vector
                    c = Count(s_wd)

                    def link(ins):
                        dve.wait_ge(s_wd, c.inc(ins))

                    v.memset(nv[:, :], 0.0).then_inc(s_nv, 1)
                    v.memset(ones[:, :], 1.0)
                    v.memset(eps_c[:, :], EPS)
                    dve.wait_ge(s_ld, NL + 32)
                    for n, (s, d) in enumerate(trans):
                        k, m = s.shape
                        dve.wait_ge(s_wt, n + 1)
                        v.tensor_copy(d, ps_t[n % 2][0:m, 0:k]).then_inc(s_wc, 1)
                    n = len(trans)
                    for l in range(2):
                        dve.wait_ge(s_wt, n + 1)
                        v.tensor_copy(w_gat[:, l, 0:D], w_lyr[:, l, :])
                        v.tensor_copy(w_gat[:, l, D:D + 2], ps_t[n % 2][:, 0:2]).then_inc(s_wc, 1)
                        n += 1
                    dve.wait_ge(s_wt, n + 1)
                    v.tensor_copy(relR[:, 0:D], rel_t[:, :])
                    v.tensor_tensor(relR[:, D:2 * D], ps_t[n % 2][:, :], w_1c[:, :], ALU.add).then_inc(s_wc, 1)
                    link(v.tensor_tensor(half_rz[:, :], b_ih[:, 0:2], b_hh[:, 0:2], ALU.add))
                    link(v.tensor_scalar(half_rz[:, :], half_rz[:, :], 0.5, None, ALU.mult))
                    link(v.tensor_scalar(half_rtc[:, :], tc[:, :], -1.0, None, ALU.mult))
                    link(v.tensor_tensor(half_rtc[:, :], half_rtc[:, :], tc[:, :], ALU.max))
                    link(v.tensor_scalar(half_rtc[:, :], half_rtc[:, :], 1e-9, None, ALU.add))
                    link(v.reciprocal(half_rtc[:, :], half_rtc[:, :]))
                    link(v.tensor_scalar(half_rtc[:, :], half_rtc[:, :], 0.5, None, ALU.mult))
                    link(v.tensor_scalar(half_b2[:, :], b_2[:, :], 0.5, None, ALU.mult))
                    dve.wait_ge(s_wc, n + 1)
                    link(v.tensor_copy(rel_hi[:, :], relR[:, :]))
                    link(v.tensor_tensor(rel_r1[:, :], relR[:, :], rel_hi[:, :], ALU.subtract))
                    link(v.tensor_copy(rel_hm[:, :], rel_r1[:, :]))
                    link(v.tensor_tensor(relR[:, :], rel_r1[:, :], rel_hm[:, :], ALU.subtract))
                    link(v.tensor_copy(rel_lo[:, :], relR[:, :]))
                    link(v.tensor_copy(rel_hm[0:TYPES, :], rel_hi[0:TYPES, :]))

        def quad(t, q, width=D):
            return t[:, bass.ds(q * (4 * width), 4 * width)]

        def table_rows(tab, q):
            return tab[bass.ds(q * (4 * P), 4 * P), :].rearrange("(j p) c -> p j c", p=P)

        def wide(ap, n):
            return ap.unsqueeze(2).to_broadcast([P, ap.shape[1], n])

        gat = ExitStack()
        COLS = 3
        gx = sb(gat, "gx", [P, COLS, TILES])
        zx = sb(gat, "zx", [P, NBP * COLS])
        scol = sb(gat, "scol", [P, NBP])
        dcol = sb(gat, "dcol", [P, NBP])
        of_sum = sb(gat, "of_sum", [P, NBP])
        of_self = sb(gat, "of_self", [P, NBP])

        def gat_nodes(l):
            with phase() as st:
                xs = sb(st, f"n{l}_xs", [P, 4 * D])
                xT = sb(st, f"n{l}_xT", [P, 4 * P])
                hT = sb(st, f"n{l}_hT", [P, 4 * P])
                gsb = sb(st, f"n{l}_gsb", [P, 4, D])
                gs = sb(st, f"n{l}_gs", [P, 4, D])
                ps_a = ps(st, f"n{l}_psa", [P, 4 * P])
                ps_b = ps(st, f"n{l}_psb", [P, 4 * P])
                ps_c = ps(st, f"n{l}_psc", [P, 4, 256])
                s_xs = sem(st, f"n{l}_xs_ready")
                s_tr = sem(st, f"n{l}_transposed")
                s_xT = sem(st, f"n{l}_xT_ready")
                s_h = sem(st, f"n{l}_h_done")
                s_hT = sem(st, f"n{l}_hT_ready")
                s_g = sem(st, f"n{l}_g_done")
                s_gsb = sem(st, f"n{l}_gsb_ready")
                s_out = sem(st, f"n{l}_stored")
                s_free = sem(st, f"n{l}_store_buffer_free")
                s_ch = sem(st, f"n{l}_chain")
                with nc.Block() as block:
                    @block.vector
                    def _(dve):
                        v = nc.vector
                        with dve.Fori(0, QUADS) as q:
                            if l == 0:
                                v.tensor_copy(xs[:, :], quad(x_n, q)).then_inc(s_xs, 1)
                            else:
                                g3 = quad(tmp, q).rearrange("p (j d) -> p j d", d=D)
                                a3 = quad(acc, q).rearrange("p (j d) -> p j d", d=D)
                                x3 = xs[:, :].rearrange("p (j d) -> p j d", d=D)
                                v.tensor_tensor(x3, a3, wide(of_sum[:, bass.ds(q * 4, 4)], D), ALU.mult)
                                v.tensor_tensor(gs[:, :, :], g3, wide(of_self[:, bass.ds(q * 4, 4)], D), ALU.mult).then_inc(s_ch, 1)
                                dve.wait_ge(s_ch, q * 2 + 1)
                                v.tensor_tensor(x3, x3, gs[:, :, :], ALU.add).then_inc(s_ch, 1)
                                dve.wait_ge(s_ch, q * 2 + 2)
                                v.tensor_tensor(x3, x3, b_lyr[0][:, :].unsqueeze(1).to_broadcast([P, 4, D]), ALU.add).then_inc(s_xs, 1)
                            dve.wait_ge(s_tr, q + 1)
                            v.tensor_copy(xT[:, :], ps_a[:, :]).then_inc(s_xT, 1)
                            dve.wait_ge(s_g, q + 1)
                            dve.wait_ge(s_free, q + 1)
                            v.tensor_copy(gsb[:, :, :], ps_c[:, :, 0:D])
                            v.tensor_copy(quad(tmp, q).rearrange("p (j d) -> p j d", d=D), ps_c[:, :, 0:D])
                            v.tensor_copy(scol[:, bass.ds(q * 4, 4)].unsqueeze(2), ps_c[:, :, D:D + 1])
                            v.tensor_copy(dcol[:, bass.ds(q * 4, 4)].unsqueeze(2), ps_c[:, :, D + 1:D + 2]).then_inc(s_gsb, 1)
                        dve.wait_ge(s_gsb, QUADS)

                    @block.tensor
                    def _(pe):
                        with pe.Fori(0, QUADS) as q:
                            pe.wait_ge(s_xs, q + 1)
                            for j in range(4):
                                i = nc.tensor.transpose(ps_a[:, j * P:(j + 1) * P], xs[:, j * D:(j + 1) * D], ident[:, :])
                            i.then_inc(s_tr, 1)
                            pe.wait_ge(s_xT, q + 1)
                            if l == 0:
                                nc.tensor.matmul(ps_b[:, :], w_node[:, :], xT[:, :], start=True, stop=True).then_inc(s_h, 1)
                                pe.wait_ge(s_hT, q + 1)
                            lhs = hT if l == 0 else xT
                            for j in range(4):
                                i = nc.tensor.matmul(ps_c[:, j, 0:D + 2], lhs[:, j * P:(j + 1) * P], w_gat[:, l, :],
                                                     start=True, stop=True)
                            i.then_inc(s_g, 1)

                    @block.scalar
                    def _(act):
                        if l == 0:
                            with act.Fori(0, QUADS) as q:
                                act.wait_ge(s_h, q + 1)
                                nc.scalar.activation(hT[:, :], ps_b[:, :], ACT.Identity, bias=b_node[:, :]).then_inc(s_hT, 1)

                    @block.sync
                    def _(sp):
                        sp.sem_inc(s_free, 1)
                        with sp.Fori(0, QUADS) as q:
                            sp.wait_ge(s_gsb, q + 1)
                            sp.dma_start(table_rows(gat_tab[l], q), gsb[:, :, :]).then_inc(s_out, 16)
                            sp.wait_ge(s_out, q * 16 + 16)
                            sp.sem_inc(s_free, 1)

        def gather_rows(pool, rows, tab, s_idx, s_row, s_used):
            def gather(r, k):
                pool.wait_ge(s_idx[k], r * 16 + 16)
                pool.sem_inc(s_turn, 1)
                for t in range(GT):
                    pool.indirect_dma_start(rows[:, k, t, :], None, tab[:, :],
                                            bass.IndirectOffsetOnAxis(ap=src_slot[:, k, t:t + 1], axis=0)).then_inc(s_row[k], 16)

            for k in range(SLOTS):
                gather(0, k)
            with pool.Fori(1, GROUPS // SLOTS) as i:
                for k in range(SLOTS):
                    n = pool.value_load(done_row[0:1, bass.ds(i * SLOTS + (k - SLOTS), 1)], min_val=1, max_val=V)
                    pool.wait_ge(s_used, n + RING)
                    gather(i, k)

        def announce(sp, s_idx, s_row, s_landed):
            def indices(g, k):
                sp.dma_start(src_slot[:, k, :], src_g[:, bass.ds(g * GT, GT)]).then_inc(s_idx[k], 16)

            def arrived(r, k):
                sp.wait_ge(s_row[k], r * (16 * GT) + 16 * GT)
                sp.sem_inc(s_landed, 1)

            rounds = GROUPS // SLOTS
            for k in range(SLOTS):
                indices(k, k)
            with sp.Fori(0, rounds - 1) as i:
                for k in range(SLOTS):
                    arrived(i, k)
                    indices(i * SLOTS + (k + SLOTS), k)
            for k in range(SLOTS):
                arrived(rounds - 1, k)

        def group_of(eng, v):
            return eng.value_load(grp_row[0:1, bass.ds(v, 1)], min_val=0, max_val=GROUPS - 1)

        def slot_of(eng, v):
            return eng.value_load(slot_row[0:1, bass.ds(v, 1)], min_val=0, max_val=SLOTS - 1)

        def landed(name):
            return [top.enter_context(nc.semaphore(f"{name}_landed{k}")) for k in range(SLOTS)]

        s_turn = sem(top, "gather_turn")

        def steps(first, body):
            whole = (V - 1) // RING
            with first.Fori(0, whole) as i:
                for k in range(RING):
                    body(i * RING + k, k)
            for v in range(whole * RING, V - 1):
                body(v, v % RING)

        def gat_logits(l):
            with phase() as st:
                part = sb(st, f"g{l}_parts", [P, 2, 3, NBP], BF16)
                rest = sb(st, f"g{l}_rest", [P, 2, NBP])
                trow = sb(st, f"g{l}_lo_rows", [P, RING, 2 * GE], BF16)
                oh = sb(st, f"g{l}_oh", [P, RING, 2 * GE], BF16)
                pid = sb(st, f"g{l}_pid", [P, 1])
                neg_pid = sb(st, f"g{l}_neg_pid", [P, 1])
                sq = sb(st, f"g{l}_sq", [P, 2, GE])
                pid_i = sb(st, f"g{l}_pid_i", [P, 1], I32)
                junk = sb(st, f"g{l}_junk", [P, 2, 2 * GT, NBP])
                pick = sb(st, f"g{l}_pick", [P, 2, 2, GT])
                u = sb(st, f"g{l}_u", [P, TILES])
                ps_c = [ps(st, f"g{l}_psc{i}", [P, 2 * GT, 64]) for i in range(2)]
                s_pid = sem(st, f"g{l}_pid_ready")
                s_part = sem(st, f"g{l}_parts_ready")
                s_lo = [sem(st, f"g{l}_lo{k}") for k in range(RING)]
                s_oh = sem(st, f"g{l}_onehot_ready")
                s_oh2 = sem(st, f"g{l}_onehot2_ready")
                s_sq = sem(st, f"g{l}_squares_ready")
                s_c = sem(st, f"g{l}_candidates")
                s_pick = sem(st, f"g{l}_picked")
                s_u = sem(st, f"g{l}_sum_ready")
                tabs = (dcol, scol)
                with nc.Block() as block:
                    @block.gpsimd
                    def _(pool):
                        nc.gpsimd.iota(pid_i[:, :], pattern=[[0, 1]], base=0, channel_multiplier=1).then_inc(s_pid, 1)
                        pool.wait_ge(s_pid, 1)
                        nc.gpsimd.tensor_copy(pid[:, :], pid_i[:, :]).then_inc(s_pid, 1)
                        pool.wait_ge(s_pid, 2)
                        pool.sem_inc(s_oh, RING)
                        with pool.Fori(0, GROUPS // RING) as i:
                            for k in range(RING):
                                g = i * RING + k
                                pool.wait_ge(s_c, g + 1)
                                pool.wait_ge(s_lo[k], i * 16 + 16)
                                pool.sem_inc(s_turn, 1)
                                nc.gpsimd.tensor_scalar(oh[:, k, 0:GE], trow[:, k, 0:GE], pid[:, :], None, ALU.is_equal).then_inc(s_oh, 1)

                    @block.scalar
                    def _(act):
                        act.wait_ge(s_pid, 2)
                        nc.scalar.activation(neg_pid[:, :], pid[:, :], ACT.Copy, scale=-1.0).then_inc(s_pid, 1)
                        act.wait_ge(s_pid, 3)
                        act.sem_inc(s_oh2, RING)
                        with act.Fori(0, GROUPS // RING) as i:
                            for k in range(RING):
                                g = i * RING + k
                                act.wait_ge(s_c, g + 1)
                                act.wait_ge(s_lo[k], i * 16 + 16)
                                nc.scalar.activation(sq[:, k % 2, :], trow[:, k, GE:2 * GE], ACT.Square, bias=neg_pid[:, :]).then_inc(s_sq, 1)
                                act.wait_ge(s_sq, g + 1)
                                nc.scalar.activation(oh[:, k, GE:2 * GE], sq[:, k % 2, :], ACT.Relu, scale=-1.0, bias=1.0).then_inc(s_oh2, 1)

                    @block.sync
                    def _(sp):
                        with sp.Fori(0, GROUPS // RING) as i:
                            for k in range(RING):
                                g = i * RING + k
                                sp.wait_ge(s_oh, g + 1)
                                sp.wait_ge(s_oh2, g + 1)
                                sp.dma_start(trow[:, k, :], lo_rows[bass.ds(g, 1), :].to_broadcast([P, 2 * GE])).then_inc(s_lo[k], 16)

                    @block.vector
                    def _(dve):
                        v = nc.vector

                        def choose(g, k):
                            dve.wait_ge(s_c, g + 1 + RING)
                            for a, hi in enumerate((dst_hi, src_hi)):
                                for t in range(GT):
                                    n = v.scalar_tensor_tensor(junk[:, k % 2, a * GT + t, :], iota[:, 0:NBP], hi[:, bass.ds(g * GT + t, 1)],
                                                               ps_c[k % 2][:, a * GT + t, 0:NBP], ALU.is_equal, ALU.mult,
                                                               accum_out=pick[:, k % 2, a, t:t + 1])
                            n.then_inc(s_pick, 1)

                        def add(g, k):
                            dve.wait_ge(s_pick, g + 3)
                            v.tensor_tensor(u[:, bass.ds(g * GT, GT)], pick[:, k % 2, 0, :], pick[:, k % 2, 1, :], ALU.add).then_inc(s_u, 1)
                            dve.wait_ge(s_u, g + 1)

                        dve.sem_inc(s_pick, 2)
                        n = 0
                        for a, tab in enumerate(tabs):
                            left = tab[:, :]
                            for i in range(3):
                                v.tensor_copy(part[:, a, i, :], left).then_inc(s_part, 1)
                                n += 1
                                dve.wait_ge(s_part, n)
                                if i < 2:
                                    v.tensor_tensor(rest[:, a, :], left, part[:, a, i, :], ALU.subtract).then_inc(s_part, 1)
                                    n += 1
                                    dve.wait_ge(s_part, n)
                                    left = rest[:, a, :]
                        choose(0, 0)
                        whole = (GROUPS - 1) // RING
                        with dve.Fori(0, whole) as i:
                            for k in range(RING):
                                choose(i * RING + (k + 1), k + 1)
                                add(i * RING + k, k)
                        for g in range(whole * RING, GROUPS):
                            if g + 1 < GROUPS:
                                choose(g + 1, g + 1)
                            add(g, g)
                        v.tensor_copy(gx[:, 2, :], w_g[:, :]).then_inc(s_u, 1)
                        v.scalar_tensor_tensor(gx[:, 0, :], u[:, :], SLOPE, u[:, :], ALU.mult, ALU.max).then_inc(s_u, 1)
                        dve.wait_ge(s_u, GROUPS + 2)

                    @block.tensor
                    def _(pe):
                        pe.sem_inc(s_c, RING)
                        pe.wait_ge(s_part, 10)
                        with pe.Fori(0, GROUPS // RING) as i:
                            for k in range(RING):
                                g = i * RING + k
                                pe.wait_ge(s_oh, g + 1 + RING)
                                pe.wait_ge(s_oh2, g + 1 + RING)
                                pe.wait_ge(s_pick, g + 1)
                                for a in range(2):
                                    for t in range(GT):
                                        for n in range(3):
                                            m = nc.tensor.matmul(ps_c[k % 2][:, a * GT + t, 0:NBP], oh[:, k, a * GE + t * P:a * GE + (t + 1) * P],
                                                                 part[:, a, n, :], start=(n == 0), stop=(n == 2))
                                m.then_inc(s_c, 1)

        def segment_softmax(name, x, heads, last_max=None):
            CH = {1: 112, HEADS: 16}[heads]
            J = TILES // CH
            R = heads * CH
            W = J * P
            with phase() as st:
                if heads == 1:
                    xs = sb(st, name + "_x", [R, W])[:, :]
                    new = sb(st, name + "_new", [R, W])[:, :]
                else:
                    xs = tmp[0:R, 0:W]
                    new = acc[0:R, 0:W]
                da = sb(st, name + "_dst", [R, W], I32)
                db = sb(st, name + "_dst_next", [R, W], I32)
                fw = db[:, :].bitcast(F32)
                bw = da[:, :].bitcast(F32)
                tail = sb(st, name + "_tail", [R, 4])
                edge = sb(st, name + "_edge", [1, 2, R])
                first = sb(st, name + "_first", [1, 2, R])
                run = sb(st, name + "_run", [1, R])
                has = edge[:, 1, :]
                give = edge[:, 0, :]
                start = sb(st, name + "_start", [R, 1])
                ps_x = [ps(st, f"{name}_psx{i}", [P, 512]) for i in range(2)]
                ps_e = ps(st, name + "_pse", [1, 2, P])
                ps_s = ps(st, name + "_pss", [P, 1])
                s_d = sem(st, name + "_dst_in")
                s_db = sem(st, name + "_next_free")
                s_x = sem(st, name + "_chunks")
                s_xc = sem(st, name + "_chunks_copied")
                s_t = sem(st, name + "_tails")
                s_e = sem(st, name + "_edges")
                s_g = sem(st, name + "_given")
                s_s = sem(st, name + "_starts")
                s_m = sem(st, name + "_max_ready")
                s_o = sem(st, name + "_max_back")
                s_oc = sem(st, name + "_max_taken")
                s_c = sem(st, name + "_chain")
                xj = x[:, :, :].rearrange("p h (c j) -> p (h c) j", j=J)
                parts = [(j, min(4, J - j)) for j in range(0, J, 4)]
                with nc.Block() as block:
                    @block.sync
                    def _(sp):
                        def load(t, o):
                            for h in range(heads):
                                sp.dma_start(t[h * CH:(h + 1) * CH, :],
                                             dst_flat[o:o + TILES * P].rearrange("(c i) -> c i", c=CH)).then_inc(s_d, 16)
                        load(da, 1)
                        load(db, 0)
                        sp.wait_ge(s_db, 1)
                        load(new.bitcast(I32), 2)
                        sp.wait_ge(s_d, 3 * 16 * heads)

                    @block.tensor
                    def _(pe):
                        for n, (j, m) in enumerate(parts):
                            if n >= 2:
                                pe.wait_ge(s_xc, n - 1)
                            for i in range(m):
                                t = nc.tensor.transpose(ps_x[n % 2][0:R, i * P:(i + 1) * P], xj[:, :, j + i], ident[:, :])
                            t.then_inc(s_x, 1)
                        for way in range(2):
                            pe.wait_ge(s_t, way + 1)
                            for i in range(2):
                                t = nc.tensor.matmul(ps_e[:, i, 0:R], tail[:, 2 * way + i:2 * way + i + 1], ident[0:R, 0:R], start=True, stop=True)
                            t.then_inc(s_e, 1)
                            pe.wait_ge(s_g, way + 1)
                            nc.tensor.matmul(ps_s[0:R, :], give, ones[0:1, :], start=True, stop=True).then_inc(s_s, 1)
                        pe.wait_ge(s_m, 1)
                        for n, (j, m) in enumerate(parts if last_max is None else parts + parts):
                            if n >= 2:
                                pe.wait_ge(s_oc, n - 1)
                            if n == len(parts):
                                pe.wait_ge(s_m, 2)
                            for i in range(m):
                                t = nc.tensor.transpose(ps_x[n % 2][:, i * R:(i + 1) * R], (fw if n < len(parts) else bw)[:, (j + i) * P:(j + i + 1) * P], ident[0:R, 0:R])
                            t.then_inc(s_o, 1)

                    @block.scalar
                    def _(act):
                        for n, (j, m) in enumerate(parts):
                            act.wait_ge(s_x, n + 1)
                            nc.scalar.activation(xs[:, j * P:(j + m) * P], ps_x[n % 2][0:R, 0:m * P], ACT.Copy).then_inc(s_xc, 1)
                        act.wait_ge(s_oc, len(parts))
                        nc.scalar.activation(x[:, :, :], x[:, :, :], ACT.Exp).then_inc(s_xc, 1)
                        act.wait_ge(s_xc, len(parts) + 1)

                    @block.vector
                    def _(dve):
                        v = nc.vector
                        c = Count(s_c)

                        def link(ins):
                            dve.wait_ge(s_c, c.inc(ins))

                        f3 = first[:, :, :].rearrange("o w (h c) -> o w h c", c=CH)
                        link(v.memset(first[:, :, :], 0.0))
                        v.memset(f3[:, 0, :, 0:1], -BIG)
                        link(v.memset(f3[:, 1, :, CH - 1:CH], -BIG))

                        def scan(out, way, init):
                            def rev(ap):
                                return ap[:, ::-1] if way else ap
                            return v.tensor_tensor_scan(rev(out), rev(new), rev(xs), init, ALU.add, ALU.max)

                        def row_(t):
                            return t[:, ::-1] if t is not None else t

                        for way in range(2):
                            dve.wait_ge(s_d, (2 + way) * 16 * heads)
                            if way == 0:
                                link(v.tensor_tensor(new, da[:, :], db[:, :], ALU.not_equal))
                            else:
                                link(v.tensor_tensor(new, da[:, :], new.bitcast(I32), ALU.not_equal))
                            link(v.tensor_scalar(new, new, -BIG, None, ALU.mult))
                            out = bw if way else fw
                            dve.wait_ge(s_xc, len(parts))
                            link(scan(out, way, -BIG))
                            end = 0 if way else W - 1
                            v.tensor_copy(tail[:, 2 * way:2 * way + 1], out[:, end:end + 1])
                            link(v.tensor_reduce(tail[:, 2 * way + 1:2 * way + 2], new, AX, ALU.min))
                            v.tensor_copy(run[0:1, 0:1], first[0:1, 0, 0:1]).then_inc(s_t, 1)
                            dve.wait_ge(s_e, way + 1)
                            link(v.tensor_copy(edge[:, :, :], ps_e[:, :, 0:R]))
                            link(v.tensor_tensor(has, has, first[:, way, :], ALU.add))
                            h_, e_, r_ = has, edge[:, 0, :], run[:, :]
                            if way:
                                h_, e_, r_ = h_[:, ::-1], e_[:, ::-1], r_[:, ::-1]
                            link(v.tensor_tensor_scan(r_, h_, e_, -BIG, ALU.add, ALU.max))
                            g3 = give.rearrange("o (h c) -> o h c", c=CH)
                            r3 = run[:, :].rearrange("o (h c) -> o h c", c=CH)
                            link(v.memset(give, -BIG))
                            if way:
                                v.tensor_copy(g3[:, :, 0:CH - 1], r3[:, :, 1:CH]).then_inc(s_g, 1)
                            else:
                                v.tensor_copy(g3[:, :, 1:CH], r3[:, :, 0:CH - 1]).then_inc(s_g, 1)
                            dve.wait_ge(s_s, way + 1)
                            link(v.tensor_copy(start[:, :], ps_s[0:R, :]))
                            i = scan(out, way, start[:, :])
                            if way == 0:
                                i.then_inc(s_db, 1)
                        link(v.tensor_copy(run[0:1, 0:1], first[0:1, 0, 0:1]))
                        v.tensor_tensor(fw, fw, bw, ALU.max).then_inc(s_m, 1)
                        if last_max is not None:
                            dve.wait_ge(s_m, 1)
                            v.scalar_tensor_tensor(bw, new, 0.0, fw, ALU.is_lt, ALU.mult).then_inc(s_m, 1)
                        for n, (j, m) in enumerate(parts):
                            dve.wait_ge(s_o, n + 1)
                            v.tensor_tensor(xj[:, :, j:j + m], xj[:, :, j:j + m],
                                            ps_x[n % 2][:, 0:m * R].rearrange("p (j r) -> p r j", r=R), ALU.subtract).then_inc(s_oc, 1)
                        if last_max is not None:
                            lj = last_max.rearrange("p (c j) -> p c j", j=J)
                            for n, (j, m) in enumerate(parts):
                                dve.wait_ge(s_o, len(parts) + n + 1)
                                v.tensor_copy(lj[:, :, j:j + m], ps_x[(len(parts) + n) % 2][:, 0:m * R].rearrange("p (j r) -> p r j", r=R)).then_inc(s_oc, 1)
                        dve.wait_ge(s_oc, len(parts) * (1 if last_max is None else 2))

        def edge_sums(name, x, heads, cols, zacc, tab, finish=None):
            with phase() as st:
                vr = sb(st, name + "_values", [P, RING if tab is None else SLOTS, GT, D])
                oh = sb(st, name + "_oh", [P, RING, GT, P])
                wv = sb(st, name + "_wv", [P, RING, GT, D + cols])
                ps_o = [ps(st, name + f"_pso{i}", [P, 512]) for i in range(RING)]
                s_val = [sem(st, name + f"_val{k}") for k in range(RING)] if tab is None else landed(name)
                s_idx = [sem(st, name + f"_idx{k}") for k in range(SLOTS)] if tab is not None else None
                s_landed = sem(st, name + "_groups_landed")
                s_fin = sem(st, name + "_finish")
                s_e = sem(st, name + "_finish_exp")
                s_wv = sem(st, name + "_weighted_ready")
                s_we = sem(st, name + "_weights_ready")
                s_o = sem(st, name + "_sums_done")
                s_acc = sem(st, name + "_sums_added")
                s_z = sem(st, name + "_cleared")
                s_take = sem(st, name + "_sums_copied")
                if tab is None:
                    so = sb(st, name + "_sums", [P, RING, D + cols])

                AHEAD = 2

                def back(eng, v_, v, k):
                    h = k % RING
                    b = eng.value_load(blk_row[0:1, bass.ds(v, 1)], min_val=0, max_val=BLOCKS - 1)
                    ab = acc[:, bass.ds(b * D, D)]
                    zb = zacc[:, bass.ds(b * cols, cols)]
                    eng.wait_ge(s_acc, v + RING)
                    sums = ps_o[h] if tab is not None else so[:, h, :]
                    eng.wait_ge(s_o if tab is not None else s_take, v + 1 + RING)
                    if tab is None:
                        eng.sem_inc(s_turn, 1)
                    v_.tensor_tensor(ab, ab, sums[:, 0:D], ALU.add)
                    v_.tensor_tensor(zb, zb, sums[:, D:D + cols], ALU.add).then_inc(s_acc, 1)

                with nc.Block() as block:
                    @block.gpsimd
                    def _(pool):
                        if tab is not None:
                            gather_rows(pool, vr, tab, s_idx, s_val, s_wv)
                        else:
                            pool.wait_ge(s_z, 1)
                            with pool.Fori(0, V // RING) as i:
                                for k in range(RING):
                                    back(pool, nc.gpsimd, i * RING + k, k)
                            pool.wait_ge(s_acc, V + RING)

                    @block.sync
                    def _(sp):
                        if tab is not None:
                            announce(sp, s_idx, s_val, s_landed)
                            return
                        with sp.Fori(0, V // RING) as i:
                            for k in range(RING):
                                g = group_of(sp, i * RING + k)
                                sp.wait_ge(s_wv, i * RING + k + 1)
                                sp.dma_start(vr[:, k, :, :], edge_v[bass.ds(g * P, P), :].rearrange("p (t d) -> p t d", d=D)).then_inc(s_val[k], 16)

                    @block.vector
                    def _(dve):
                        v_ = nc.vector

                        def front(v, k, fill):
                            h = k % RING
                            slot = k % RING if tab is None else slot_of(dve, v)
                            dve.wait_ge(s_o, v + 1)
                            for t in range(GT):
                                v_.tensor_scalar(oh[:, h, t, :], iota[:, :], dst_tab[:, bass.ds(v * GT + t, 1)], None, ALU.is_equal)
                            if tab is None:
                                dve.wait_ge(s_val[k % RING], fill)
                            dve.wait_ge(s_we, v + 1)
                            e = wv[:, h, :, D:D + heads]
                            v_.tensor_tensor(wv[:, h, :, 0:D].rearrange("p t (h d) -> p t h d", h=heads),
                                             vr[:, bass.ds(slot, 1), :, :].rearrange("p o t (h d) -> p (o t) h d", h=heads),
                                             e.unsqueeze(3).to_broadcast([P, GT, heads, D // heads]), ALU.mult).then_inc(s_wv, 1)

                        v_.memset(acc[:, :], 0.0)
                        v_.memset(zacc[:, :], 0.0).then_inc(s_z, 1)
                        dve.sem_inc(s_wv, RING)
                        dve.wait_ge(s_z, 1)
                        for v in range(AHEAD):
                            front(v, v, 16)
                        whole = (V - AHEAD) // RING
                        with dve.Fori(0, whole) as i:
                            for k in range(RING):
                                front(i * RING + (k + AHEAD), k + AHEAD, (i + (k + AHEAD) // RING) * 16 + 16)
                                if tab is not None:
                                    back(dve, v_, i * RING + k, k)
                        for v in range(whole * RING, V):
                            if v + AHEAD < V:
                                front(v + AHEAD, (v + AHEAD) % RING, ((v + AHEAD) // RING) * 16 + 16)
                            if tab is not None:
                                back(dve, v_, v, v % RING)
                        dve.wait_ge(s_acc, V + RING)
                        if finish is not None:
                            finish(dve, None, s_fin, s_e)

                    @block.scalar
                    def _(act):
                        def weights(v, k):
                            g = group_of(act, v)
                            act.wait_ge(s_o, v + 1)
                            if tab is not None:
                                act.wait_ge(s_landed, g + 1)
                            nc.scalar.activation(wv[:, k % RING, :, D:D + cols],
                                                 x[:, :, bass.ds(g * GT, GT)].rearrange("p h t -> p t h"), ACT.Copy).then_inc(s_we, 1)

                        def take(v, k):
                            if tab is None:
                                act.wait_ge(s_acc, v + 1)
                                act.wait_ge(s_o, v + 1 + RING)
                                nc.scalar.activation(so[:, k, :], ps_o[k][:, 0:D + cols], ACT.Copy).then_inc(s_take, 1)

                        act.sem_inc(s_take, RING)
                        for v in range(AHEAD):
                            weights(v, v)
                        with act.Fori(0, (V - AHEAD) // RING) as i:
                            for k in range(RING):
                                weights(i * RING + (k + AHEAD), k + AHEAD)
                                take(i * RING + k, k)
                        for v in range((V - AHEAD) // RING * RING, V):
                            if v + AHEAD < V:
                                weights(v + AHEAD, v + AHEAD)
                            take(v, v % RING)
                        if finish is not None:
                            finish(None, act, s_fin, s_e)

                    @block.tensor
                    def _(pe):
                        pe.sem_inc(s_o, RING)
                        pe.sem_inc(s_acc, RING)
                        with pe.Fori(0, V // RING) as i:
                            for k in range(RING):
                                v = i * RING + k
                                h = k % RING
                                pe.wait_ge(s_wv, v + 1 + RING)
                                pe.wait_ge(s_we, v + 1)
                                pe.wait_ge(s_acc if tab is not None else s_take, v + 1)
                                for t in range(GT):
                                    m = nc.tensor.matmul(ps_o[h][:, 0:D + cols], oh[:, h, t, :], wv[:, h, t, :],
                                                         start=(t == 0), stop=(t == GT - 1))
                                m.then_inc(s_o, 1)

        def gat_sums(l):
            es = sb(gat, f"f{l}_self", [P, NBP])
            has = sb(gat, f"f{l}_has", [P, NBP])
            me = sb(gat, f"f{l}_max", [P, NBP])
            mm_ = sb(gat, f"f{l}_all_max", [P, NBP])
            z = sb(gat, f"f{l}_z", [P, NBP])

            def finish(dve, act, s_ch, s_e):
                z3 = zx[:, :].rearrange("p (b c) -> p b c", c=COLS)

                def flat(c):
                    return z3[:, :, c:c + 1].rearrange("p b o -> p (b o)")

                if dve is None:
                    for t in (of_sum, of_self):
                        act.wait_ge(s_ch, F_EXP)
                        nc.scalar.activation(t[:, :], t[:, :], ACT.Exp).then_inc(s_e, 1)
                    return
                v = nc.vector
                c = Count(s_ch)

                def link(ins):
                    dve.wait_ge(s_ch, c.inc(ins))

                link(v.tensor_tensor(z[:, :], scol[:, :], dcol[:, :], ALU.add))
                link(v.scalar_tensor_tensor(es[:, :], z[:, :], SLOPE, z[:, :], ALU.mult, ALU.max))
                link(v.tensor_scalar(has[:, :], flat(0), 0.0, None, ALU.is_gt))
                link(v.tensor_scalar(me[:, :], has[:, :], -1.0, 1.0, ALU.mult, ALU.add))
                link(v.tensor_tensor(me[:, :], me[:, :], es[:, :], ALU.mult))
                link(v.tensor_tensor(has[:, :], has[:, :], flat(1), ALU.mult))
                link(v.tensor_tensor(me[:, :], me[:, :], has[:, :], ALU.add))
                link(v.tensor_tensor(mm_[:, :], me[:, :], es[:, :], ALU.max))
                link(v.tensor_tensor(of_sum[:, :], me[:, :], mm_[:, :], ALU.subtract))
                link(v.tensor_tensor(of_self[:, :], es[:, :], mm_[:, :], ALU.subtract))
                assert c.n == F_EXP
                dve.wait_ge(s_e, 2)
                link(v.tensor_tensor(z[:, :], flat(0), of_sum[:, :], ALU.mult))
                link(v.tensor_tensor(z[:, :], z[:, :], of_self[:, :], ALU.add))
                link(v.reciprocal(z[:, :], z[:, :]))
                link(v.tensor_tensor(of_sum[:, :], of_sum[:, :], z[:, :], ALU.mult))
                link(v.tensor_tensor(of_self[:, :], of_self[:, :], z[:, :], ALU.mult))
                if l == 0:
                    link(v.tensor_scalar(deg[:, :], flat(2), 1.0, None, ALU.add))

            edge_sums(f"e{l}", gx, 1, COLS, zx, gat_tab[l], finish)

        F_EXP = 10

        def residual_norm(name, prep):
            with phase() as st:
                mean = sb(st, f"{name}_mean", [P, NBP])
                var = sb(st, f"{name}_var", [P, NBP])
                sd = sb(st, f"{name}_sd", [P, NBP])
                s_ch = sem(st, f"{name}_chain")
                s_var = sem(st, f"{name}_var_ready")
                s_sd = sem(st, f"{name}_sd_ready")
                t3 = tmp[:, :].rearrange("p (b d) -> p b d", d=D)
                x3 = x_n[:, :].rearrange("p (b d) -> p b d", d=D)
                with nc.Block() as block:
                    @block.vector
                    def _(dve):
                        v = nc.vector
                        c = Count(s_ch)

                        def link(ins):
                            dve.wait_ge(s_ch, c.inc(ins))

                        prep(link, st, t3, x3)
                        link(v.tensor_reduce(mean[:, :], t3, AX, ALU.add))
                        link(v.tensor_scalar(mean[:, :], mean[:, :], 1.0 / D, None, ALU.mult))
                        link(v.tensor_tensor(t3, t3, wide(mean[:, :], D), ALU.subtract))
                        link(v.tensor_tensor(x3, t3, t3, ALU.mult))
                        v.tensor_reduce(var[:, :], x3, AX, ALU.add).then_inc(s_var, 1)
                        dve.wait_ge(s_sd, 1)
                        link(v.reciprocal(sd[:, :], sd[:, :]))
                        link(v.tensor_tensor(x3, t3, wide(sd[:, :], D), ALU.mult))

                    @block.scalar
                    def _(act):
                        act.wait_ge(s_var, 1)
                        nc.scalar.activation(sd[:, :], var[:, :], ACT.Sqrt, bias=eps_c[:, :], scale=1.0 / D).then_inc(s_sd, 1)

        def every(b):
            return b[:, :].unsqueeze(1).to_broadcast([P, NBP, D])

        def gat_out(link, st, t3, x3):
            v = nc.vector
            a3 = acc[:, :].rearrange("p (b d) -> p b d", d=D)
            link(v.tensor_tensor(t3, t3, wide(of_self[:, :], D), ALU.mult))
            link(v.tensor_tensor(a3, a3, wide(of_sum[:, :], D), ALU.mult))
            link(v.tensor_tensor(t3, t3, a3, ALU.add))
            link(v.tensor_tensor(t3, t3, every(b_lyr[1]), ALU.add))
            link(v.tensor_tensor(t3, t3, x3, ALU.add))

        def table_nodes(name, take, w_first, b_first, keep, w_second, width, tabs, tab_width, give, start=None):
            with phase() as st:
                xs = sb(st, f"{name}_xs", [P, 4 * D])
                xT = sb(st, f"{name}_xT", [P, 4 * P])
                hT = sb(st, f"{name}_hT", [P, 4 * P])
                gsb = sb(st, f"{name}_gsb", [P, 4, tab_width])
                scr = sb(st, f"{name}_scr", [P, 4, D])
                ps_a = ps(st, f"{name}_psa", [P, 4 * P])
                ps_b = ps(st, f"{name}_psb", [P, 4 * P])
                ps_c = ps(st, f"{name}_psc", [P, 4, 256])
                s_xs = sem(st, f"{name}_xs_ready")
                s_tr = sem(st, f"{name}_transposed")
                s_xT = sem(st, f"{name}_xT_ready")
                s_h = sem(st, f"{name}_h_done")
                s_hT = sem(st, f"{name}_hT_ready")
                s_g = sem(st, f"{name}_products_done")
                s_gsb = sem(st, f"{name}_rows_ready")
                s_out = sem(st, f"{name}_stored")
                s_free = sem(st, f"{name}_store_buffer_free")
                s_ch = sem(st, f"{name}_chain")
                s_pre = sem(st, f"{name}_start")
                s_act = sem(st, f"{name}_act")
                with nc.Block() as block:
                    @block.vector
                    def _(dve):
                        v = nc.vector
                        if start is not None:
                            start(dve, v, s_pre, s_act)
                        with dve.Fori(0, QUADS) as q:
                            take(dve, v, q, xs).then_inc(s_xs, 1)
                            dve.wait_ge(s_tr, q + 1)
                            v.tensor_copy(xT[:, :], ps_a[:, :]).then_inc(s_xT, 1)
                            dve.wait_ge(s_g, q + 1)
                            dve.wait_ge(s_free, q + 1)
                            give(dve, v, q, ps_c, xs, gsb, scr, s_ch).then_inc(s_gsb, 1)
                        dve.wait_ge(s_gsb, QUADS)

                    @block.tensor
                    def _(pe):
                        with pe.Fori(0, QUADS) as q:
                            pe.wait_ge(s_xs, q + 1)
                            for j in range(4):
                                i = nc.tensor.transpose(ps_a[:, j * P:(j + 1) * P], xs[:, j * D:(j + 1) * D], ident[:, :])
                            i.then_inc(s_tr, 1)
                            pe.wait_ge(s_xT, q + 1)
                            if w_first is not None:
                                nc.tensor.matmul(ps_b[:, :], w_first[:, :], xT[:, :], start=True, stop=True).then_inc(s_h, 1)
                                pe.wait_ge(s_hT, q + 1)
                            lhs = hT if w_first is not None else xT
                            for j in range(4):
                                i = nc.tensor.matmul(ps_c[:, j, 0:width], lhs[:, j * P:(j + 1) * P], w_second,
                                                     start=True, stop=True)
                            i.then_inc(s_g, 1)

                    @block.scalar
                    def _(act):
                        if start is not None:
                            start(act, None, s_pre, s_act)
                        if w_first is not None:
                            with act.Fori(0, QUADS) as q:
                                act.wait_ge(s_h, q + 1)
                                nc.scalar.activation(quad(keep, q), ps_b[:, :], ACT.Identity, bias=b_first[:, :])
                                nc.scalar.activation(hT[:, :], ps_b[:, :], ACT.Identity, bias=b_first[:, :]).then_inc(s_hT, 1)

                    @block.sync
                    def _(sp):
                        sp.sem_inc(s_free, 1)
                        with sp.Fori(0, QUADS) as q:
                            sp.wait_ge(s_gsb, q + 1)
                            for tab, lo, hi in tabs:
                                sp.dma_start(table_rows(tab, q), gsb[:, :, lo:hi]).then_inc(s_out, 16)
                            sp.wait_ge(s_out, (q + 1) * (16 * len(tabs)))
                            sp.sem_inc(s_free, 1)

        def take_x(dve, v, q, xs):
            return v.tensor_copy(xs[:, :], quad(x_n, q))

        def sum_edges(name, tab, weighted):
            with phase() as st:
                rows = sb(st, f"{name}_rows", [P, SLOTS, GT, D])
                oh = sb(st, f"{name}_oh", [P, 2, GT, P])
                ps_o = [ps(st, f"{name}_pso{i}", [P, 512]) for i in range(2)]
                s_idx = [sem(st, f"{name}_idx{k}") for k in range(SLOTS)]
                s_row = landed(name)
                s_landed = sem(st, f"{name}_groups_landed")
                s_oh = sem(st, f"{name}_onehot_ready")
                s_o = sem(st, f"{name}_sums_done")
                s_acc = sem(st, f"{name}_sums_added")
                with nc.Block() as block:
                    @block.gpsimd
                    def _(pool):
                        pool.sem_inc(s_o, RING)
                        gather_rows(pool, rows, tab, s_idx, s_row, s_o)

                    @block.sync
                    def _(sp):
                        announce(sp, s_idx, s_row, s_landed)

                    @block.vector
                    def _(dve):
                        v_ = nc.vector

                        def front(v, k):
                            for t in range(GT):
                                col_ = bass.ds(v * GT + t, 1)
                                if weighted:
                                    i = v_.tensor_scalar(oh[:, k % 2, t, :], iota[:, :], dst_tab[:, col_], w_tab[:, col_],
                                                         ALU.is_equal, ALU.mult)
                                else:
                                    i = v_.tensor_scalar(oh[:, k % 2, t, :], iota[:, :], dst_tab[:, col_], None, ALU.is_equal)
                            i.then_inc(s_oh, 1)

                        def back(v, k):
                            b = dve.value_load(blk_row[0:1, bass.ds(v, 1)], min_val=0, max_val=BLOCKS - 1)
                            dve.wait_ge(s_acc, v + 2)
                            dve.wait_ge(s_o, v + 1 + RING)
                            ab = acc[:, bass.ds(b * D, D)]
                            v_.tensor_tensor(ab, ab, ps_o[k % 2][:, 0:D], ALU.add).then_inc(s_acc, 1)

                        front(0, 0)

                        def body(v, k):
                            front(v + 1, k + 1)
                            back(v, k)

                        steps(dve, body)
                        back(V - 1, (V - 1) % RING)
                        dve.wait_ge(s_acc, V + 2)

                    @block.tensor
                    def _(pe):
                        pe.sem_inc(s_acc, 2)
                        with pe.Fori(0, V // RING) as i:
                            for k in range(RING):
                                v = i * RING + k
                                g = group_of(pe, v)
                                slot = slot_of(pe, v)
                                pe.wait_ge(s_oh, v + 1)
                                pe.wait_ge(s_landed, g + 1)
                                pe.wait_ge(s_acc, v + 1)
                                for t in range(GT):
                                    m = nc.tensor.matmul(ps_o[k % 2][:, 0:D], oh[:, k % 2, t, :], rows[:, bass.ds(slot, 1), t, :].rearrange("p o d -> p (o d)"),
                                                         start=(t == 0), stop=(t == GT - 1))
                                m.then_inc(s_o, 1)


        def gcn_start(eng, v, s_pre, s_act):
            if v is None:
                eng.wait_ge(s_pre, 1)
                nc.scalar.activation(dis[:, :], dis[:, :], ACT.Sqrt).then_inc(s_act, 1)
                return
            v.tensor_scalar(dis[:, :], deg[:, :], 1e-30, None, ALU.max).then_inc(s_pre, 1)
            v.tensor_scalar(deg[:, :], deg[:, :], 0.0, None, ALU.is_gt).then_inc(s_pre, 1)
            eng.wait_ge(s_pre, 2)
            eng.wait_ge(s_act, 1)
            v.reciprocal(dis[:, :], dis[:, :]).then_inc(s_pre, 1)
            eng.wait_ge(s_pre, 3)
            v.tensor_tensor(dis[:, :], dis[:, :], deg[:, :], ALU.mult).then_inc(s_pre, 1)
            eng.wait_ge(s_pre, 4)

        def gcn_give(dve, v, q, ps_c, xs, gsb, scr, s_ch):
            dq = wide(dis[:, bass.ds(q * 4, 4)], D)
            v.tensor_tensor(quad(acc, q).rearrange("p (j d) -> p j d", d=D), ps_c[:, :, 0:D], dq, ALU.mult)
            return v.tensor_tensor(gsb[:, :, :], ps_c[:, :, 0:D], dq, ALU.mult)

        def gcn_out(link, st, t3, x3):
            v = nc.vector
            link(v.tensor_tensor(t3, acc[:, :].rearrange("p (b d) -> p b d", d=D), wide(dis[:, :], D), ALU.mult))
            link(v.tensor_tensor(t3, t3, every(b_gcn), ALU.add))
            link(v.tensor_tensor(t3, t3, x3, ALU.add))

        def ggn_start(eng, v, s_pre, s_act):
            if v is not None:
                v.memset(acc[:, :], 0.0)

        def ggn_give(dve, v, q, ps_c, xs, gsb, scr, s_ch):
            return v.tensor_copy(gsb[:, :, :], ps_c[:, :, 0:D])

        def ggn_gates():
            with phase() as st:
                xs = sb(st, "gru_xs", [P, 4 * D])
                aT = sb(st, "gru_aT", [P, 4 * P])
                er = sb(st, "gru_r", [P, 4 * P])
                ez = sb(st, "gru_z", [P, 4 * P])
                nn = sb(st, "gru_n", [P, 4 * P])
                hn = sb(st, "gru_h", [P, 4 * P])
                ps_a = ps(st, "gru_psa", [P, 4 * P])
                ps_g = [ps(st, f"gru_psg{i}", [P, 4 * P]) for i in range(4)]
                ps_c = ps(st, "gru_psc", [P, 4, D])
                s_xs = sem(st, "gru_xs_ready")
                s_tr = sem(st, "gru_transposed")
                s_aT = sem(st, "gru_aT_ready")
                s_g = sem(st, "gru_gates_done")
                s_e = sem(st, "gru_exp_ready")
                s_n = sem(st, "gru_n_in")
                s_t = sem(st, "gru_tanh_ready")
                s_hn = sem(st, "gru_h_ready")
                s_c = sem(st, "gru_out_done")
                s_ac = sem(st, "gru_out_taken")
                s_ch = sem(st, "gru_chain")
                NCH = 5
                with nc.Block() as block:
                    @block.vector
                    def _(dve):
                        v = nc.vector
                        with dve.Fori(0, QUADS) as q:
                            v.tensor_copy(xs[:, :], quad(acc, q)).then_inc(s_xs, 1)
                            dve.wait_ge(s_tr, q + 1)
                            v.tensor_copy(aT[:, :], ps_a[:, :]).then_inc(s_aT, 1)
                            dve.wait_ge(s_e, q + 1)
                            for g in (er, ez):
                                v.tensor_scalar(g[:, :], g[:, :], 0.5, 0.5, ALU.mult, ALU.add).then_inc(s_ch, 1)
                            dve.wait_ge(s_ch, q * NCH + 2)
                            v.scalar_tensor_tensor(nn[:, :], ps_g[3][:, :], b_hh[:, 2:3], er[:, :], ALU.add, ALU.mult).then_inc(s_ch, 1)
                            dve.wait_ge(s_ch, q * NCH + 3)
                            v.tensor_tensor(nn[:, :], nn[:, :], ps_g[2][:, :], ALU.add).then_inc(s_n, 1)
                            dve.wait_ge(s_t, q + 1)
                            v.tensor_tensor(hn[:, :], quad(tmp, q), nn[:, :], ALU.subtract).then_inc(s_ch, 1)
                            dve.wait_ge(s_ch, q * NCH + 4)
                            v.tensor_tensor(hn[:, :], hn[:, :], ez[:, :], ALU.mult).then_inc(s_ch, 1)
                            dve.wait_ge(s_ch, q * NCH + 5)
                            v.tensor_tensor(hn[:, :], hn[:, :], nn[:, :], ALU.add).then_inc(s_hn, 1)
                            dve.wait_ge(s_c, q + 1)
                            v.tensor_tensor(quad(acc, q).rearrange("p (j d) -> p j d", d=D), ps_c[:, :, :],
                                            b_out[:, :].unsqueeze(1).to_broadcast([P, 4, D]), ALU.add).then_inc(s_ac, 1)
                        dve.wait_ge(s_ac, QUADS)

                    @block.tensor
                    def _(pe):
                        with pe.Fori(0, QUADS) as q:
                            pe.wait_ge(s_xs, q + 1)
                            for j in range(4):
                                i = nc.tensor.transpose(ps_a[:, j * P:(j + 1) * P], xs[:, j * D:(j + 1) * D], ident[:, :])
                            i.then_inc(s_tr, 1)
                            pe.wait_ge(s_aT, q + 1)
                            for g in range(2):
                                nc.tensor.matmul(ps_g[g][:, :], w_ihT[:, g, :], aT[:, :], start=True, stop=False)
                                nc.tensor.matmul(ps_g[g][:, :], w_hhT[:, g, :], quad(tmp, q), start=False, stop=True)
                            nc.tensor.matmul(ps_g[2][:, :], w_ihT[:, 2, :], aT[:, :], start=True, stop=True)
                            nc.tensor.matmul(ps_g[3][:, :], w_hhT[:, 2, :], quad(tmp, q), start=True, stop=True).then_inc(s_g, 1)
                            pe.wait_ge(s_hn, q + 1)
                            for j in range(4):
                                i = nc.tensor.matmul(ps_c[:, j, :], hn[:, j * P:(j + 1) * P], w_outT[:, :], start=True, stop=True)
                            i.then_inc(s_c, 1)

                    @block.scalar
                    def _(act):
                        with act.Fori(0, QUADS) as q:
                            act.wait_ge(s_g, q + 1)
                            nc.scalar.activation(er[:, :], ps_g[0][:, :], ACT.Tanh, bias=half_rz[:, 0:1], scale=0.5)
                            nc.scalar.activation(ez[:, :], ps_g[1][:, :], ACT.Tanh, bias=half_rz[:, 1:2], scale=0.5).then_inc(s_e, 1)
                            act.wait_ge(s_n, q + 1)
                            nc.scalar.activation(nn[:, :], nn[:, :], ACT.Tanh, bias=b_ih[:, 2:3]).then_inc(s_t, 1)

        def ggn_out(link, st, t3, x3):
            link(nc.vector.tensor_tensor(t3, acc[:, :].rearrange("p (b d) -> p b d", d=D), x3, ALU.add))


        def rel_start(eng, v, s_pre, s_act):
            if v is not None:
                v.memset(zrel[:, :], 0.0)

        def rel_give(dve, v, q, ps_c, xs, gsb, scr, s_ch):
            def bias(b):
                return b[:, :].unsqueeze(1).to_broadcast([P, 4, D])
            q3 = gsb[:, :, 2 * D:]
            v.tensor_copy(gsb[:, :, 0:D], xs[:, :].rearrange("p (j d) -> p j d", d=D))
            v.tensor_tensor(gsb[:, :, D:2 * D], ps_c[:, :, 0:D], bias(b_1), ALU.add)
            v.tensor_tensor(scr[:, :, :], ps_c[:, :, D:2 * D], bias(b_q), ALU.add).then_inc(s_ch, 1)
            dve.wait_ge(s_ch, q * 4 + 1)
            v.tensor_scalar(scr[:, :, :], scr[:, :, :], float(HD) ** -0.5, None, ALU.mult).then_inc(s_ch, 1)
            dve.wait_ge(s_ch, q * 4 + 2)
            v.tensor_copy(q3[:, :, 0:D], scr[:, :, :])
            v.tensor_tensor(xs[:, :].rearrange("p (j d) -> p j d", d=D), scr[:, :, :], bias(b_k), ALU.mult).then_inc(s_ch, 1)
            dve.wait_ge(s_ch, q * 4 + 3)
            v.tensor_reduce(q3[:, :, D:D + HEADS], xs[:, :].rearrange("p (j h d) -> p j h d", h=HEADS, d=HD), AX, ALU.add).then_inc(s_ch, 1)
            dve.wait_ge(s_ch, q * 4 + 4)
            return v.tensor_scalar(q3[:, :, D + HEADS:QW], nv[:, bass.ds(q * 4, 4)].unsqueeze(2), 1.0, None, ALU.mult)

        def rel_scores():
            with phase() as st:
                rows = sb(st, "s_rows", [P, RING, GT, 2 * D])
                qrows = sb(st, "s_qrows", [P, RING, GT, QW])
                dst_slot = sb(st, "s_dst_slot", [P, RING, GT], I32)
                trow = sb(st, "s_trow", [P, RING, GE], BF16)
                tid_i = sb(st, "s_tid_i", [P, 1], I32)
                tid = sb(st, "s_tid", [P, 2])
                oh = sb(st, "s_oh", [P, 2, GE], BF16)
                dt = sb(st, "s_dt", [P, 2, GT])
                th = sb(st, "s_th", [P, 2, GT])
                tm = sb(st, "s_tm", [P, 2, GT])
                tmh = sb(st, "s_tmh", [P, 2, GT])
                hm = sb(st, "s_hm", [P, GT, D])
                junk = sb(st, "s_junk", [P, GT, D])
                gz = sb(st, "s_gz", [P, 2, GT])
                ga = sb(st, "s_ga", [P, 2, GT])
                gc = sb(st, "s_gc", [P, 2, GT])
                msg = sb(st, "s_msg", [P, GT, D])
                msgT = sb(st, "s_msgT", [P, GE])
                pq = sb(st, "s_pq", [P, GT, D])
                sc = sb(st, "s_sc", [P, GT, HEADS])
                vs = sb(st, "s_vs", [P, RING, GE])
                ps_r = [ps(st, f"s_psr{i}", [P, GT, 2 * D]) for i in range(2)]
                ps_t = ps(st, "s_pst", [P, GE])
                ps_k = ps(st, "s_psk", [P, GT, D])
                ps_v = ps(st, "s_psv", [P, GE])
                s_idx = [sem(st, f"s_idx{k}") for k in range(RING)]
                s_row = landed("s")
                s_trow = [sem(st, f"s_trow{k}") for k in range(RING)]
                s_tid = sem(st, "s_tid_ready")
                s_oh = sem(st, "s_onehot_ready")
                s_r = sem(st, "s_relation_rows")
                s_dt = sem(st, "s_dt_ready")
                s_th = sem(st, "s_time_tanh")
                s_z = sem(st, "s_gate_logits")
                s_g = sem(st, "s_gate_tanh")
                s_msg = sem(st, "s_messages")
                s_mt = sem(st, "s_messages_transposed")
                s_mT = sem(st, "s_messagesT_ready")
                s_k = sem(st, "s_keys")
                s_v = sem(st, "s_values")
                s_sc = sem(st, "s_scores_done")
                s_vs = sem(st, "s_values_copied")
                s_vfree = sem(st, "s_value_buffer_free")
                s_out = [sem(st, f"s_values_stored{k}") for k in range(RING)]
                s_ch = sem(st, "s_chain_logits")
                s_cm = sem(st, "s_chain_messages")
                s_cs = sem(st, "s_chain_scores")
                T = [slice(t * P, (t + 1) * P) for t in range(GT)]
                FILL = 2 * 16 * GT
                LEAD = 2

                def at(i, k, d):
                    return i * RING + (k + d), (k + d) % RING, i + (k + d) // RING

                def rounds(eng, body):
                    whole = (GROUPS - RING) // RING
                    with eng.Fori(0, whole) as i:
                        for k in range(RING):
                            body(i, k, lambda d: True)
                    for g in range(whole * RING, GROUPS):
                        body(g // RING, g % RING, lambda d: g + d < GROUPS)

                with nc.Block() as block:
                    @block.gpsimd
                    def _(pool):
                        pool.sem_inc(s_sc, RING)
                        nc.gpsimd.iota(tid_i[:, :], pattern=[[0, 1]], base=0, channel_multiplier=1).then_inc(s_tid, 1)
                        with pool.Fori(0, GROUPS // RING) as i:
                            for k in range(RING):
                                g = i * RING + k
                                pool.wait_ge(s_sc, g + 1)
                                pool.wait_ge(s_idx[k], i * 32 + 32)
                                pool.sem_inc(s_turn, 1)
                                for t in range(GT):
                                    pool.indirect_dma_start(qrows[:, k, t, :], None, q_tab[:, :],
                                                            bass.IndirectOffsetOnAxis(ap=dst_slot[:, k, t:t + 1], axis=0)).then_inc(s_row[k], 16)
                                    pool.indirect_dma_start(rows[:, k, t, :], None, rel_tab[:, :],
                                                            bass.IndirectOffsetOnAxis(ap=src_slot[:, k, t:t + 1], axis=0)).then_inc(s_row[k], 16)

                    @block.sync
                    def _(sp):
                        def types(i, k, d):
                            g, s, _ = at(i, k, d)
                            sp.wait_ge(s_oh, g + 1)
                            sp.dma_start(trow[:, s, :], type_rows[bass.ds(g, 1), :].to_broadcast([P, GE])).then_inc(s_trow[s], 16)

                        def indices(g, k):
                            sp.dma_start(src_slot[:, k, :], src_g[:, bass.ds(g * GT, GT)]).then_inc(s_idx[k], 16)
                            sp.dma_start(dst_slot[:, k, :], dst_g[:, bass.ds(g * GT, GT)]).then_inc(s_idx[k], 16)

                        def body(i, k, has):
                            g, _, _ = at(i, k, 0)
                            if has(LEAD):
                                types(i, k, LEAD)
                            if not isinstance(i, int) or i > 0:
                                sp.wait_ge(s_out[k], i * 16)
                                sp.sem_inc(s_vfree, 1)
                            sp.wait_ge(s_row[k], i * FILL + FILL)
                            if has(RING):
                                indices(g + RING, k)

                        for k in range(RING):
                            indices(k, k)
                        for g in range(LEAD):
                            types(0, g, 0)
                        sp.sem_inc(s_vfree, RING)
                        for k in range(RING):
                            body(0, k, lambda d: True)
                        whole = (GROUPS - RING) // RING
                        with sp.Fori(1, whole) as i:
                            for k in range(RING):
                                body(i, k, lambda d: True)
                        for g in range(whole * RING, GROUPS):
                            body(g // RING, g % RING, lambda d: g + d < GROUPS)
                        for k in range(RING):
                            sp.wait_ge(s_out[k], GROUPS // RING * 16)

                    @block.vector
                    def _(dve):
                        v = nc.vector

                        def early(i, k, d):
                            g, s, r = at(i, k, d)
                            dve.wait_ge(s_trow[s], r * 16 + 16)
                            dve.wait_ge(s_r, g + 1)
                            v.tensor_scalar(oh[:, s % 2, :], trow[:, s, :], tid[:, 0:1], None, ALU.is_equal).then_inc(s_oh, 1)
                            dve.wait_ge(s_row[s], r * FILL + FILL)
                            v.tensor_tensor(dt[:, s % 2, :], qrows[:, s, :, D + HEADS:QW].rearrange("p t o -> p (t o)"),
                                            w_g[:, bass.ds(g * GT, GT)], ALU.subtract).then_inc(s_dt, 1)

                        def logits(i, k, d):
                            g, s, _ = at(i, k, d)
                            h = s % 2
                            dve.wait_ge(s_th, g + 1)
                            v.tensor_scalar(tmh[:, h, :], th[:, h, :], 0.25, 0.25, ALU.mult, ALU.add)
                            v.tensor_scalar(tm[:, h, :], th[:, h, :], 0.5, 0.5, ALU.mult, ALU.add).then_inc(s_ch, 1)
                            dve.wait_ge(s_ch, g * 2 + 1)
                            dve.wait_ge(s_r, g + 3)
                            for t in range(GT):
                                n = v.scalar_tensor_tensor(hm[:, t, :], ps_r[h][:, t, D:2 * D], tm[:, h, t:t + 1], rows[:, s, t, D:2 * D],
                                                           ALU.mult, ALU.add)
                            n.then_inc(s_ch, 1)
                            dve.wait_ge(s_ch, g * 2 + 2)
                            for t in range(GT):
                                n = v.scalar_tensor_tensor(junk[:, t, :], hm[:, t, :], 0.0, w_2[:, :], ALU.max, ALU.mult,
                                                           accum_out=gz[:, h, t:t + 1])
                            n.then_inc(s_z, 1)

                        def messages(i, k, d):
                            g, s, _ = at(i, k, d)
                            h = s % 2
                            dve.wait_ge(s_g, g + 1)
                            v.scalar_tensor_tensor(gc[:, h, :], ga[:, h, :], 1.0, tmh[:, h, :], ALU.add, ALU.mult).then_inc(s_cm, 1)
                            dve.wait_ge(s_cm, g + 1)
                            dve.wait_ge(s_mt, g + 1)
                            for t in range(GT):
                                n = v.scalar_tensor_tensor(msg[:, t, :], ps_r[h][:, t, 0:D], gc[:, h, t:t + 1], rows[:, s, t, 0:D],
                                                           ALU.mult, ALU.mult)
                            n.then_inc(s_msg, 1)

                        def scores(i, k):
                            g, s, _ = at(i, k, 0)
                            dve.wait_ge(s_k, g + 1)
                            v.tensor_tensor(pq[:, :, :], ps_k[:, :, :], qrows[:, s, :, 0:D], ALU.mult).then_inc(s_cs, 1)
                            dve.wait_ge(s_cs, g * 2 + 1)
                            v.tensor_reduce(sc[:, :, :].rearrange("p t h -> p (t h)"),
                                            pq[:, :, :].rearrange("p t (h d) -> p (t h) d", d=HD), AX, ALU.add).then_inc(s_cs, 1)
                            dve.wait_ge(s_cs, g * 2 + 2)
                            v.tensor_tensor(score[:, :, bass.ds(g * GT, GT)].rearrange("p h t -> p t h"), sc[:, :, :],
                                            qrows[:, s, :, D:D + HEADS], ALU.add).then_inc(s_sc, 1)

                        def body(i, k, has):
                            if has(2):
                                early(i, k, 2)
                            if has(1):
                                logits(i, k, 1)
                            scores(i, k)
                            if has(1):
                                messages(i, k, 1)

                        dve.wait_ge(s_tid, 1)
                        v.tensor_copy(tid[:, 0:1], tid_i[:, :]).then_inc(s_tid, 1)
                        dve.wait_ge(s_tid, 2)
                        v.tensor_scalar(tid[:, 1:2], tid[:, 0:1], float(TYPES), -float(TYPES), ALU.is_ge, ALU.mult).then_inc(s_tid, 1)
                        dve.wait_ge(s_tid, 3)
                        v.tensor_tensor(tid[:, 0:1], tid[:, 0:1], tid[:, 1:2], ALU.add).then_inc(s_tid, 1)
                        dve.wait_ge(s_tid, 4)
                        dve.sem_inc(s_oh, RING)
                        dve.sem_inc(s_msg, 2)
                        early(0, 0, 0)
                        early(0, 1, 0)
                        logits(0, 0, 0)
                        messages(0, 0, 0)
                        rounds(dve, body)
                        dve.wait_ge(s_sc, GROUPS + RING)

                    @block.tensor
                    def _(pe):
                        mm = nc.tensor.matmul

                        def relations(i, k, d):
                            g, s, _ = at(i, k, d)
                            h = s % 2
                            pe.wait_ge(s_oh, g + 1 + RING)
                            pe.wait_ge(s_msg, g + 1)
                            for t in range(GT):
                                mm(ps_r[h][:, t, :], oh[:, h, T[t]], rel_hm[:, :], start=True, stop=False)
                                n = mm(ps_r[h][:, t, :], oh[0:TYPES, h, T[t]], rel_lo[0:TYPES, :], start=False, stop=True)
                            n.then_inc(s_r, 1)

                        def turn(i, k, d):
                            g, s, _ = at(i, k, d)
                            pe.wait_ge(s_msg, g + 3)
                            for t in range(GT):
                                n = nc.tensor.transpose(ps_t[:, T[t]], msg[:, t, :], ident[:, :])
                            n.then_inc(s_mt, 1)

                        def keys(i, k):
                            g, s, _ = at(i, k, 0)
                            pe.wait_ge(s_mT, g + 1)
                            pe.wait_ge(s_sc, g + RING)
                            for t in range(GT):
                                n = mm(ps_k[:, t, :], msgT[:, T[t]], w_kv[:, 0, :], start=True, stop=True)
                            n.then_inc(s_k, 1)
                            pe.wait_ge(s_vs, g + 1)
                            for t in range(GT):
                                n = mm(ps_v[:, T[t]], msgT[:, T[t]], w_kv[:, 1, :], start=True, stop=True)
                            n.then_inc(s_v, 1)

                        def body(i, k, has):
                            keys(i, k)
                            if has(2):
                                relations(i, k, 2)
                            if has(1):
                                turn(i, k, 1)

                        pe.sem_inc(s_r, 2)
                        pe.sem_inc(s_mt, 1)
                        relations(0, 0, 0)
                        relations(0, 1, 0)
                        turn(0, 0, 0)
                        rounds(pe, body)

                    @block.scalar
                    def _(act):
                        f = nc.scalar.activation

                        def time(i, k, d):
                            g, s, _ = at(i, k, d)
                            act.wait_ge(s_dt, g + 1)
                            f(th[:, s % 2, :], dt[:, s % 2, :], ACT.Tanh, scale=half_rtc[:, :]).then_inc(s_th, 1)

                        def gate(i, k, d):
                            g, s, _ = at(i, k, d)
                            act.wait_ge(s_z, g + 1)
                            f(ga[:, s % 2, :], gz[:, s % 2, :], ACT.Tanh, scale=0.5, bias=half_b2[:, :]).then_inc(s_g, 1)

                        def values(i, k):
                            g, s, _ = at(i, k, 0)
                            act.wait_ge(s_v, g + 1)
                            act.wait_ge(s_vfree, g + 1)
                            f(vs[:, s, :], ps_v[:, :], ACT.Copy).then_inc(s_vs, 1)
                            act.wait_ge(s_vs, g + 2)
                            act.dma_start(edge_v[bass.ds(g * P, P), :], vs[:, s, :]).then_inc(s_out[s], 16)

                        def turned(i, k, d):
                            g, s, _ = at(i, k, d)
                            act.wait_ge(s_mt, g + 2)
                            f(msgT[:, :], ps_t[:, :], ACT.Copy).then_inc(s_mT, 1)

                        def body(i, k, has):
                            if has(2):
                                time(i, k, 2)
                            if has(1):
                                gate(i, k, 1)
                            values(i, k)
                            if has(1):
                                turned(i, k, 1)

                        act.sem_inc(s_vs, 1)
                        time(0, 0, 0)
                        time(0, 1, 0)
                        gate(0, 0, 0)
                        turned(0, 0, 0)
                        rounds(act, body)

        def rel_out(link, st, t3, x3):
            v = nc.vector
            rz = sb(st, "ro_rz", [P, NBP * HEADS])
            has = sb(st, "ro_has", [P, NBP * HEADS])

            def heads(t):
                return t[:, :].rearrange("p (b d) -> p b d", d=HD)

            link(v.tensor_scalar(rz[:, :], zrel[:, :], 1e-30, None, ALU.max))
            link(v.reciprocal(rz[:, :], rz[:, :]))
            link(v.tensor_scalar(has[:, :], zrel[:, :], 0.0, None, ALU.is_gt))
            link(v.tensor_tensor(heads(tmp), heads(acc), wide(rz[:, :], HD), ALU.mult))
            link(v.tensor_tensor(acc[:, :].rearrange("p (b d) -> p b d", d=D), every(b_v),
                                 has[:, :].rearrange("p (b h) -> p b h", h=HEADS)[:, :, 0:1].to_broadcast([P, NBP, D]), ALU.mult))
            link(v.tensor_tensor(t3, t3, acc[:, :].rearrange("p (b d) -> p b d", d=D), ALU.add))
            link(v.tensor_tensor(t3, t3, x3, ALU.add))

        gat_nodes(0)
        gat_logits(0)
        segment_softmax("g0_sm", gx[:, 0:1, :], 1, gx[:, 1, :])
        gat_sums(0)
        gat_nodes(1)
        gat_logits(1)
        segment_softmax("g1_sm", gx[:, 0:1, :], 1, gx[:, 1, :])
        gat_sums(1)
        residual_norm("ln0", gat_out)
        gat.close()
        table_nodes("gcn", take_x, None, None, None, w_gcn[:, :], D, [(gcn_tab, 0, D)], D, gcn_give, gcn_start)
        sum_edges("gcn_e", gcn_tab, True)
        residual_norm("ln1", gcn_out)
        rel = ExitStack()
        QW = D + HEADS + 1
        score = sb(rel, "score", [P, HEADS, TILES])
        zrel = sb(rel, "zrel", [P, NBP * HEADS])
        table_nodes("reln", take_x, None, None, None, w_xq[:, :, :].rearrange("p a d -> p (a d)"), 2 * D,
                    [(rel_tab, 0, 2 * D), (q_tab, 2 * D, 2 * D + QW)], 2 * D + QW, rel_give, rel_start)
        rel_scores()
        segment_softmax("rel_sm", score, HEADS)
        edge_sums("rel_e", score, HEADS, HEADS, zrel, None)
        residual_norm("ln2", rel_out)
        table_nodes("ggn", take_x, w_inT, b_in, tmp, w_msg[:, :], D, [(ggn_tab, 0, D)], D, ggn_give, ggn_start)
        sum_edges("ggn_e", ggn_tab, False)
        ggn_gates()
        residual_norm("ln3", ggn_out)
        rel.close()
        s = sem(top, 'out_stored')
        with nc.Block() as block:
            @block.sync
            def _(sp):
                sp.dma_start(out[0:(BLOCKS - 1) * P, :].rearrange("(b p) d -> p b d", p=P), x_n[:, 0:(BLOCKS - 1) * D].rearrange("p (b d) -> p b d", d=D)).then_inc(s, 16)
                sp.dma_start(out[(BLOCKS - 1) * P:N, :], x_n[0:N - (BLOCKS - 1) * P, (BLOCKS - 1) * D:BLOCKS * D]).then_inc(s, 16)
                sp.wait_ge(s, 32)


_INS = ['x', 'src', 'dst', 'edge_type_64', 'edge_weight', 'node_vec', 'L0_gnn_W_node', 'L0_gnn_b_node', 'L0_gnn_lyr_W',
        'L0_gnn_att_src', 'L0_gnn_att_dst', 'L0_gnn_lyr_bias', 'L1_gnn_W', 'L1_gnn_b', 'L2_gnn_rel_table', 'L2_gnn_Wq',
        'L2_gnn_bq', 'L2_gnn_Wk', 'L2_gnn_bk', 'L2_gnn_Wv', 'L2_gnn_bv', 'L2_gnn_W1', 'L2_gnn_b1', 'L2_gnn_W2', 'L2_gnn_b2',
        'L2_gnn_time_coeff', 'L3_gnn_W_in', 'L3_gnn_b_in', 'L3_gnn_W_msg', 'L3_gnn_W_ih', 'L3_gnn_b_ih', 'L3_gnn_W_hh',
        'L3_gnn_b_hh', 'L3_gnn_W_out', 'L3_gnn_b_out']


def kernel(**inputs):
    import concourse.bacc as _bacc
    from concourse.bass_utils import run_bass_kernel_spmd as _run

    nc = _bacc.Bacc("TRN2", target_bir_lowering=False, num_devices=1)
    arrays, args = {}, {}
    for name in _INS:
        a = np.ascontiguousarray(inputs[name])
        if a.ndim == 0:
            a = a.reshape(1)
        arrays[f"in_{name}"] = a
        args[name] = nc.dram_tensor(f"in_{name}", a.shape, mybir.dt.from_np(a.dtype), kind="ExternalInput").ap()
    out = nc.dram_tensor("out_0", (N, D), F32, kind="ExternalOutput").ap()
    build(nc, args, out)
    r = _run(nc, [arrays], core_ids=[0])
    return r.results[0]["out_0"]
```

```python
from contextlib import ExitStack, contextmanager

import numpy as np

import concourse.bass as bass
from concourse import mybir

F32 = mybir.dt.float32
I32 = mybir.dt.int32
BF16 = mybir.dt.bfloat16
ALU = mybir.AluOpType
ACT = mybir.ActivationFunctionType
AX = mybir.AxisListType.X

P = 128
N = 6250
E = 100000
D = 128
BLOCKS = -(-N // P)
QUADS = -(-BLOCKS // 4)
NBP = QUADS * 4
NPAD = NBP * P
GT = 4
GE = GT * P
GROUPS = -(-E // GE)
HALF_G = GROUPS // 2
TILES = GROUPS * GT
V = GROUPS + BLOCKS - 1
VC = -(-V // P)
VP = VC * P
FULL = E // GE
REST = E - FULL * GE
PAD = GE - REST
NO_NODE = 8191
BIG = float(2.0 ** 100)
RING = 4
SLOTS = 14
STASH = SLOTS // 2
SLOPE = 0.2
EPS = 1e-5
HEADS = 8
HD = D // HEADS
TYPES = 64


class Count:

    def __init__(self, sem):
        self.sem, self.n = sem, 0

    def inc(self, ins, by=1):
        ins.then_inc(self.sem, by)
        self.n += by
        return self.n


def build(nc, A, out):
    top = ExitStack()
    with top:
        def sb(stack, name, shape, dt=F32):
            return stack.enter_context(nc.sbuf_tensor(name, shape, dt))

        def ps(stack, name, shape, dt=F32):
            return stack.enter_context(nc.psum_tensor(name, shape, dt))

        used = []

        def sem(stack, name):
            s = stack.enter_context(nc.semaphore(name))
            used.append(s)
            return s

        @contextmanager
        def phase():
            with ExitStack() as st:
                used.clear()
                yield st
                with nc.Block() as block:
                    @block.gpsimd
                    def _(pool):
                        for s in used:
                            pool.sem_clear(s)

        ident = sb(top, "ident", [P, P])
        iota = sb(top, "iota", [P, P])
        x_n = sb(top, "x_n", [P, NBP * D])
        acc = sb(top, "acc", [P, NBP * D])
        tmp = sb(top, "tmp", [P, NBP * D])
        dst_tab = sb(top, "dst_tab", [P, VP * GT])
        w_tab = sb(top, "w_tab", [P, VP * GT])
        blk_row = sb(top, "blk_row", [1, VP], I32)
        grp_row = sb(top, "grp_row", [1, VP], I32)
        src_g = sb(top, "src_g", [P, TILES], I32)
        dst_g = sb(top, "dst_g", [P, TILES], I32)
        w_g = sb(top, "w_g", [P, TILES])
        hi_g = sb(top, "hi_g", [P, 2, TILES])
        slot_row = sb(top, "slot_row", [1, VP], I32)
        done_row = sb(top, "done_row", [1, GROUPS], I32)
        src_slot = sb(top, "src_slot", [P, SLOTS, GT], I32)
        deg = sb(top, "deg", [P, NBP])

        edge_rows = nc.dram_tensor("edge_rows", (GROUPS, 4 * GE), I32).ap()
        dst_flat = nc.dram_tensor("dst_flat", (GROUPS * GE + 2,), I32).ap()
        type_rows = nc.dram_tensor("type_rows", (GROUPS, GE), BF16).ap()
        lo_rows = nc.dram_tensor("lo_rows", (GROUPS, 2 * GE), BF16).ap()
        edge_v = nc.dram_tensor("edge_v", (GROUPS * P, GE), F32).ap()
        gat_tab = [nc.dram_tensor(f"gat_tab{l}", (NPAD, D), F32).ap() for l in range(2)]
        gcn_tab = nc.dram_tensor("gcn_tab", (NPAD, D), F32).ap()
        q_tab = nc.dram_tensor("q_tab", (NPAD, D + HEADS + 1), F32).ap()
        rel_tab = nc.dram_tensor("rel_tab", (NPAD, 2 * D), F32).ap()
        ggn_tab = nc.dram_tensor("ggn_tab", (NPAD, D), F32).ap()

        def row(ap):
            return ap.rearrange("(o f) -> o f", o=1)

        with phase() as st:
            padv = sb(st, "padv", [1, 2, PAD + 8], I32)
            grow = sb(st, "grow", [HALF_G, 2, 4 * GE], I32)
            gf = sb(st, "gf", [HALF_G, 2, 3, GE])
            tb = sb(st, "tb", [HALF_G, 2, GE], BF16)
            lo_i = sb(st, "lo_i", [HALF_G, 2, 2 * GE], I32)
            lo = sb(st, "lo", [HALF_G, 2, 2 * GE], BF16)
            hi_i = sb(st, "hi_i", [P, 2, TILES], I32)
            gmax = sb(st, "gmax", [HALF_G, 2], I32)
            gsh = sb(st, "gsh", [HALF_G, 2], I32)
            last = sb(st, "last", [HALF_G, 2])
            giota = sb(st, "giota", [HALF_G, 2], I32)
            giotaf = sb(st, "giotaf", [HALF_G, 2])
            viota = sb(st, "viota", [P, VC], I32)
            viotaf = sb(st, "viotaf", [P, VC])
            iota_i = sb(st, "iota_i", [P, P], I32)
            cmp = sb(st, "cmp", [P, VC, GROUPS])
            gv = sb(st, "gv", [P, VC])
            gvi = sb(st, "gvi", [P, VC], I32)
            bv = sb(st, "bv", [P, VC])
            bv128 = sb(st, "bv128", [P, VC])
            er = sb(st, "er", [P, VC, 4, GE], I32)
            ef = sb(st, "ef", [P, VC, 2, GE])
            ps_last = ps(st, "ps_last", [P, GROUPS])
            ps_blk = ps(st, "ps_blk", [1, VP])
            ps_grp = ps(st, "ps_grp", [1, VP])
            ps_slot = ps(st, "ps_slot", [1, VP])
            slotv = sb(st, "slotv", [P, VC])
            mult = sb(st, "mult", [P, GROUPS // SLOTS])
            ps_tr = ps(st, "ps_tr", [P, 2, GE])
            s_c = sem(st, "p_c")
            s_cp = sem(st, "p_cp")
            s_pad = sem(st, "p_pad")
            s_dr = sem(st, "p_dr")
            s_dl = sem(st, "p_dl")
            s_last = sem(st, "p_last")
            s_pl = sem(st, "p_pl")
            s_gv = sem(st, "p_gv")
            s_er = top.enter_context(nc.semaphore("p_edge_rows"))
            s_ef = sem(st, "p_ef")
            s_tr = sem(st, "p_tr")
            s_trc = sem(st, "p_trc")
            s_x = sem(st, "p_x")
            s_bv = sem(st, "p_bv")
            s_tb = sem(st, "p_types")
            s_gf = sem(st, "p_group_arrays")
            s_z = sem(st, "p_z")
            with nc.Block() as block:
                @block.sync
                def _(sp):
                    n = 0
                    sp.wait_ge(s_pad, 2)
                    for a, name in enumerate(("dst", "src", "edge_type_64", "edge_weight")):
                        arr = A[name] if a < 3 else A[name].bitcast(I32)
                        sp.dma_start(edge_rows[0:FULL, a * GE:(a + 1) * GE],
                                     arr[0:FULL * GE].rearrange("(g e) -> g e", e=GE)).then_inc(s_dr, 16)
                        sp.dma_start(edge_rows[FULL:GROUPS, a * GE:a * GE + REST],
                                     row(arr[FULL * GE:E])).then_inc(s_dr, 16)
                        sp.dma_start(edge_rows[FULL:GROUPS, a * GE + REST:(a + 1) * GE],
                                     padv[0:1, 0 if a == 0 else 1, 0:PAD]).then_inc(s_dr, 16)
                    dst = A["dst"]
                    sp.dma_start(row(dst_flat[0:1]), padv[0:1, 0, 0:1]).then_inc(s_dr, 16)
                    sp.dma_start(row(dst_flat[1:1 + E]), row(dst)).then_inc(s_dr, 16)
                    sp.dma_start(row(dst_flat[1 + E:GROUPS * GE + 2]), padv[0:1, 0, 0:PAD + 1]).then_inc(s_dr, 16)
                    n = 15 * 16
                    sp.wait_ge(s_dr, n)
                    sp.dma_start(grow[:, :, :], edge_rows[:, :].rearrange("(c p) e -> p c e", c=2)).then_inc(s_dl, 16)
                    sp.wait_ge(s_z, 1)
                    sp.dma_start(x_n[:, 0:(BLOCKS - 1) * D].rearrange("p (b d) -> p b d", d=D),
                                 A["x"][0:(BLOCKS - 1) * P, :].rearrange("(b p) d -> p b d", p=P)).then_inc(s_x, 16)
                    sp.dma_start(x_n[0:N - (BLOCKS - 1) * P, (BLOCKS - 1) * D:BLOCKS * D],
                                 A["x"][(BLOCKS - 1) * P:N, :]).then_inc(s_x, 16)
                    sp.wait_ge(s_tb, 1)
                    sp.dma_start(type_rows[:, :].rearrange("(c p) e -> p c e", c=2), tb[:, :, :]).then_inc(s_x, 16)
                    sp.wait_ge(s_tb, 2)
                    sp.dma_start(lo_rows[:, :].rearrange("(c p) e -> p c e", c=2), lo[:, :, :]).then_inc(s_x, 16)
                    sp.wait_ge(s_x, 64)

                @block.gpsimd
                def _(pool):
                    g = nc.gpsimd
                    g.iota(giota[:, :], pattern=[[HALF_G, 2]], base=0, channel_multiplier=1).then_inc(s_cp, 1)
                    g.iota(viota[:, :], pattern=[[P, VC]], base=0, channel_multiplier=1).then_inc(s_cp, 1)
                    g.iota(iota_i[:, :], pattern=[[1, P]], base=0, channel_multiplier=0).then_inc(s_cp, 1)
                    g.memset(ident[:, :], 0.0).then_inc(s_cp, 1)
                    pool.wait_ge(s_cp, 4)
                    g.affine_select(out=ident[:, :], in_=ident[:, :], compare_op=ALU.not_equal, fill=1.0,
                                    base=0, pattern=[[-1, P]], channel_multiplier=1).then_inc(s_cp, 1)
                    pool.wait_ge(s_gv, 1)
                    for c in range(VC):
                        pool.indirect_dma_start(er[:, c, :, :].rearrange("p a e -> p (a e)"), None, edge_rows[:, :],
                                                bass.IndirectOffsetOnAxis(ap=gvi[:, c:c + 1], axis=0)).then_inc(s_er, 16)

                @block.vector
                def _(dve):
                    v = nc.vector
                    c = Count(s_c)

                    def link(ins):
                        dve.wait_ge(s_c, c.inc(ins))

                    v.memset(padv[0:1, 0, :], NO_NODE).then_inc(s_pad, 1)
                    v.memset(padv[0:1, 1, :], 0).then_inc(s_pad, 1)
                    v.memset(x_n[:, :], 0.0).then_inc(s_z, 1)
                    dve.wait_ge(s_cp, 5)
                    v.tensor_copy(giotaf[:, :], giota[:, :])
                    v.tensor_copy(viotaf[:, :], viota[:, :])
                    link(v.tensor_copy(iota[:, :], iota_i[:, :]))
                    dve.wait_ge(s_dl, 16)
                    link(v.tensor_reduce(gmax[:, :], grow[:, :, 0:GE], AX, ALU.max))
                    link(v.tensor_scalar(gsh[:, :], gmax[:, :], 7, None, ALU.arith_shift_right))
                    link(v.tensor_scalar(last[:, :], gsh[:, :], float(BLOCKS - 1), None, ALU.min))
                    v.tensor_tensor(last[:, :], last[:, :], giotaf[:, :], ALU.add).then_inc(s_last, 1)
                    dve.wait_ge(s_pl, 1)
                    for k in range(VC):
                        link(v.tensor_scalar(cmp[:, k, :], ps_last[:, :], viotaf[:, k:k + 1], None, ALU.is_lt))
                    link(v.tensor_reduce(gv[:, :], cmp[:, :, :], AX, ALU.add))
                    link(v.tensor_scalar(gv[:, :], gv[:, :], float(GROUPS - 1), None, ALU.min))
                    v.tensor_copy(gvi[:, :], gv[:, :]).then_inc(s_gv, 1)
                    M = GROUPS // SLOTS
                    link(v.tensor_scalar(mult[:, :], iota[:, 0:M], float(SLOTS), None, ALU.mult))
                    for k in range(VC):
                        link(v.tensor_scalar(cmp[:, k, 0:M], mult[:, :], gv[:, k:k + 1], None, ALU.is_le))
                    link(v.tensor_reduce(slotv[:, :], cmp[:, :, 0:M], AX, ALU.add))
                    link(v.tensor_scalar(slotv[:, :], slotv[:, :], -1.0, -float(SLOTS), ALU.add, ALU.mult))
                    link(v.tensor_tensor(slotv[:, :], gv[:, :], slotv[:, :], ALU.add))
                    v.tensor_scalar(done_row[:, :], ps_last[0:1, :], 1.0, None, ALU.add)
                    link(v.tensor_tensor(bv[:, :], viotaf[:, :], gv[:, :], ALU.subtract))
                    link(v.tensor_scalar(bv[:, :], bv[:, :], float(BLOCKS - 1), None, ALU.min))
                    v.tensor_scalar(bv128[:, :], bv[:, :], float(P), None, ALU.mult).then_inc(s_bv, 1)
                    dve.wait_ge(s_bv, 1)
                    v.tensor_copy(tb[:, :, :], grow[:, :, 2 * GE:3 * GE]).then_inc(s_tb, 1)
                    link(v.tensor_scalar(lo_i[:, :, :], grow[:, :, 0:2 * GE], P - 1, None, ALU.bitwise_and))
                    v.tensor_copy(lo[:, :, :], lo_i[:, :, :]).then_inc(s_tb, 1)
                    link(v.tensor_copy(gf[:, :, 0:2, :], grow[:, :, 0:2 * GE].rearrange("p c (a e) -> p c a e", a=2)))
                    link(v.tensor_scalar(gf[:, :, 0, :], gf[:, :, 0, :], float(NPAD - 1), None, ALU.min))
                    v.tensor_copy(gf[:, :, 2, :], grow[:, :, 3 * GE:4 * GE].bitcast(F32)).then_inc(s_gf, 1)
                    dve.wait_ge(s_er, 16 * VC)
                    for k in range(VC):
                        link(v.tensor_copy(ef[:, k, 0, :], er[:, k, 0, :]))
                        link(v.tensor_copy(ef[:, k, 1, :], er[:, k, 3, :].bitcast(F32)))
                        v.tensor_scalar(ef[:, k, 0, :], ef[:, k, 0, :], bv128[:, k:k + 1], None, ALU.subtract).then_inc(s_ef, 1)
                    n = 0
                    for k in range(VC):
                        for a, tab in enumerate((dst_tab, w_tab)):
                            dve.wait_ge(s_tr, n + 1)
                            v.tensor_copy(tab[:, k * P * GT:(k + 1) * P * GT].rearrange("p (v t) -> p t v", t=GT),
                                          ps_tr[:, n % 2, :].rearrange("p (t v) -> p t v", t=GT)).then_inc(s_trc, 1)
                            n += 1
                    HT = HALF_G * GT
                    for half in range(2):
                        for a, tab in enumerate((dst_g, src_g, w_g)):
                            dve.wait_ge(s_tr, n + 1)
                            v.tensor_copy(tab[:, half * HT:(half + 1) * HT].rearrange("p (g t) -> p t g", t=GT),
                                          ps_tr[:, n % 2, 0:HT].rearrange("p (t g) -> p t g", t=GT)).then_inc(s_trc, 1)
                            n += 1
                    dve.wait_ge(s_tr, n + 1)
                    v.tensor_copy(grp_row[:, :], ps_grp[:, :])
                    v.tensor_copy(slot_row[:, :], ps_slot[:, :])
                    v.tensor_copy(blk_row[:, :], ps_blk[:, :]).then_inc(s_trc, 1)
                    dve.wait_ge(s_trc, n)
                    link(v.tensor_scalar(hi_i[:, 0, :], dst_g[:, :], 7, None, ALU.arith_shift_right))
                    link(v.tensor_scalar(hi_i[:, 1, :], src_g[:, :], 7, None, ALU.arith_shift_right))
                    link(v.tensor_copy(hi_g[:, 0, :], hi_i[:, 0, :]))
                    link(v.tensor_copy(hi_g[:, 1, :], hi_i[:, 1, :]))
                    dve.wait_ge(s_trc, n + 1)

                @block.tensor
                def _(pe):
                    pe.wait_ge(s_cp, 5)
                    pe.wait_ge(s_last, 1)
                    for c in range(2):
                        i = nc.tensor.matmul(ps_last[:, c * HALF_G:(c + 1) * HALF_G],
                                             last[:, c:c + 1].to_broadcast([HALF_G, P]), ident[0:HALF_G, 0:HALF_G],
                                             start=True, stop=True)
                    i.then_inc(s_pl, 1)
                    n = 0
                    pe.wait_ge(s_ef, VC)
                    for k in range(VC):
                        for a in range(2):
                            if n >= 2:
                                pe.wait_ge(s_trc, n - 1)
                            for t in range(GT):
                                i = nc.tensor.transpose(ps_tr[:, n % 2, t * P:(t + 1) * P],
                                                        ef[:, k, a, t * P:(t + 1) * P], ident[:, :])
                            i.then_inc(s_tr, 1)
                            n += 1
                    pe.wait_ge(s_gf, 1)
                    for c in range(2):
                        for a in range(3):
                            pe.wait_ge(s_trc, n - 1)
                            for t in range(GT):
                                i = nc.tensor.transpose(ps_tr[:, n % 2, t * HALF_G:(t + 1) * HALF_G],
                                                        gf[:, c, a, t * P:(t + 1) * P], ident[0:HALF_G, 0:HALF_G])
                            i.then_inc(s_tr, 1)
                            n += 1
                    pe.wait_ge(s_bv, 1)
                    for k in range(VC):
                        nc.tensor.matmul(ps_slot[:, k * P:(k + 1) * P], slotv[:, k:k + 1], ident[:, :], start=True, stop=True)
                        nc.tensor.matmul(ps_grp[:, k * P:(k + 1) * P], gv[:, k:k + 1], ident[:, :], start=True, stop=True)
                        i = nc.tensor.matmul(ps_blk[:, k * P:(k + 1) * P], bv[:, k:k + 1], ident[:, :], start=True, stop=True)
                    i.then_inc(s_tr, 1)

        def load(n, shape, src_ap):
            t = sb(top, "w_" + n, shape)
            loads.append((t, src_ap))
            return t

        def col(ap):
            return ap.rearrange("(p o) -> p o", o=1)

        def rep(ap):
            return ap.partition_broadcast(P)

        loads = []
        w_node = load("node", [P, D], A["L0_gnn_W_node"])
        b_node = load("b_node", [P, 1], col(A["L0_gnn_b_node"]))
        w_lyr = load("lyr", [P, 2, D], A["L0_gnn_lyr_W"].rearrange("l k f -> k l f"))
        att = load("att", [P, 2, 2], None)
        b_lyr = [load(f"b_lyr{l}", [P, D], rep(A["L0_gnn_lyr_bias"][l, :])) for l in range(2)]
        w_gcn = load("gcn", [P, D], A["L1_gnn_W"])
        b_gcn = load("b_gcn", [P, D], rep(A["L1_gnn_b"]))
        rel_t = load("rel", [2 * TYPES, D], None)
        w_xq = load("xq", [P, 2, D], None)
        w_1b = load("w1b", [P, D], A["L2_gnn_W1"][D:2 * D, :])
        w_1c = load("w1c", [P, D], rep(A["L2_gnn_W1"][2 * D, :]))
        b_1 = load("b1", [P, D], rep(A["L2_gnn_b1"]))
        w_2 = load("w2", [P, D], rep(A["L2_gnn_W2"].rearrange("k o -> (k o)")))
        b_2 = load("b2", [P, 1], rep(A["L2_gnn_b2"]))
        b_q = load("bq", [P, D], rep(A["L2_gnn_bq"]))
        b_k = load("bk", [P, D], rep(A["L2_gnn_bk"]))
        b_v = load("bv", [P, D], rep(A["L2_gnn_bv"]))
        w_kv = load("kv", [P, 2, D], None)
        tc = load("tc", [P, 1], rep(A["L2_gnn_time_coeff"]))
        w_in = load("in", [P, D], A["L3_gnn_W_in"])
        b_in = load("b_in", [P, 1], col(A["L3_gnn_b_in"]))
        w_msg = load("msg", [P, D], A["L3_gnn_W_msg"])
        w_ih = load("ih", [P, 3, D], A["L3_gnn_W_ih"].rearrange("(g p) k -> p g k", p=P))
        w_hh = load("hh", [P, 3, D], A["L3_gnn_W_hh"].rearrange("(g p) k -> p g k", p=P))
        b_ih = load("b_ih", [P, 3], None)
        b_hh = load("b_hh", [P, 3], None)
        w_out = load("out", [P, D], A["L3_gnn_W_out"])
        b_out = load("b_out", [P, D], rep(A["L3_gnn_b_out"]))
        loads = [x for x in loads if x[1] is not None]
        for l in range(2):
            loads.append((att[:, l, 0:1], col(A["L0_gnn_att_src"][l, :])))
            loads.append((att[:, l, 1:2], col(A["L0_gnn_att_dst"][l, :])))
        for i in range(2):
            loads.append((rel_t[i * TYPES:(i + 1) * TYPES, :], A["L2_gnn_rel_table"]))
        loads.append((w_xq[:, 0, :], A["L2_gnn_W1"][0:D, :]))
        loads.append((w_xq[:, 1, :], A["L2_gnn_Wq"]))
        loads.append((w_kv[:, 0, :], A["L2_gnn_Wk"]))
        loads.append((w_kv[:, 1, :], A["L2_gnn_Wv"]))
        for g in range(3):
            loads.append((b_ih[:, g:g + 1], col(A["L3_gnn_b_ih"][g * D:(g + 1) * D])))
            loads.append((b_hh[:, g:g + 1], col(A["L3_gnn_b_hh"][g * D:(g + 1) * D])))
        nv = sb(top, "nv", [P, NBP])

        w_gat = sb(top, "w_gat", [P, 2, D + 2])
        rel_hm = sb(top, "rel_hm", [P, 2 * D], BF16)
        rel_lo = sb(top, "rel_lo", [P, 2 * D], BF16)
        w_inT = sb(top, "w_inT", [P, D])
        w_ihT = sb(top, "w_ihT", [P, 3, D])
        w_hhT = sb(top, "w_hhT", [P, 3, D])
        w_outT = sb(top, "w_outT", [P, D])
        half_rz = sb(top, "half_rz", [P, 2])
        half_rtc = sb(top, "half_rtc", [P, 1])
        half_b2 = sb(top, "half_b2", [P, 1])
        dis = sb(top, "dis", [P, NBP])
        ones = sb(top, "ones", [P, 1])
        eps_c = sb(top, "eps_c", [P, 1])
        with phase() as st:
            wT = sb(st, "wT", [P, 2, D])
            relT = sb(st, "relT", [P, P])
            relR = sb(st, "relR", [P, 2 * D])
            rel_r1 = sb(st, "rel_r1", [P, 2 * D])
            rel_hi = sb(st, "rel_hi", [P, 2 * D], BF16)
            ps_t = [ps(st, f"ps_wt{i}", [P, D]) for i in range(2)]
            s_ld = sem(st, "w_ld")
            s_wt = sem(st, "w_t")
            s_wc = sem(st, "w_c")
            s_wd = sem(st, "w_d")
            s_nv = sem(st, "w_nv")
            NL = 16 * len(loads)
            trans = [(w_lyr[:, 0, :], wT[:, 0, :]), (w_lyr[:, 1, :], wT[:, 1, :]), (w_in[:, :], w_inT[:, :]),
                     (w_out[:, :], w_outT[:, :]), (rel_t[:, :], relT[:, :])]
            trans += [(w_ih[:, g, :], w_ihT[:, g, :]) for g in range(3)]
            trans += [(w_hh[:, g, :], w_hhT[:, g, :]) for g in range(3)]
            with nc.Block() as block:
                @block.sync
                def _(sp):
                    with nc.allow_non_contiguous_dma(reason="small bias columns"):
                        for dst, s in loads:
                            sp.dma_start(dst[tuple(slice(None) for _ in dst.shape)], s).then_inc(s_ld, 16)
                        sp.wait_ge(s_nv, 1)
                        sp.dma_start(nv[:, 0:BLOCKS - 1], A["node_vec"][0:(BLOCKS - 1) * P].rearrange("(b p) -> p b", p=P)).then_inc(s_ld, 16)
                        sp.dma_start(nv[0:N - (BLOCKS - 1) * P, BLOCKS - 1:BLOCKS],
                                     col(A["node_vec"][(BLOCKS - 1) * P:N])).then_inc(s_ld, 16)
                    sp.wait_ge(s_ld, NL + 32)

                @block.tensor
                def _(pe):
                    pe.wait_ge(s_ld, NL + 32)
                    n = 0
                    for n, (s, _) in enumerate(trans):
                        if n >= 2:
                            pe.wait_ge(s_wc, n - 1)
                        k, m = s.shape
                        nc.tensor.transpose(ps_t[n % 2][0:m, 0:k], s, ident[0:k, 0:k]).then_inc(s_wt, 1)
                    n = len(trans)
                    for l in range(2):
                        pe.wait_ge(s_wc, n - 1)
                        nc.tensor.matmul(ps_t[n % 2][:, 0:2], wT[:, l, :], att[:, l, :], start=True, stop=True).then_inc(s_wt, 1)
                        n += 1
                    pe.wait_ge(s_wc, n - 1)
                    nc.tensor.matmul(ps_t[n % 2][:, :], relT[:, :], w_1b[:, :], start=True, stop=True).then_inc(s_wt, 1)

                @block.vector
                def _(dve):
                    v = nc.vector
                    c = Count(s_wd)

                    def link(ins):
                        dve.wait_ge(s_wd, c.inc(ins))

                    v.memset(nv[:, :], 0.0).then_inc(s_nv, 1)
                    v.memset(ones[:, :], 1.0)
                    v.memset(eps_c[:, :], EPS)
                    dve.wait_ge(s_ld, NL + 32)
                    for n, (s, d) in enumerate(trans):
                        k, m = s.shape
                        dve.wait_ge(s_wt, n + 1)
                        v.tensor_copy(d, ps_t[n % 2][0:m, 0:k]).then_inc(s_wc, 1)
                    n = len(trans)
                    for l in range(2):
                        dve.wait_ge(s_wt, n + 1)
                        v.tensor_copy(w_gat[:, l, 0:D], w_lyr[:, l, :])
                        v.tensor_copy(w_gat[:, l, D:D + 2], ps_t[n % 2][:, 0:2]).then_inc(s_wc, 1)
                        n += 1
                    dve.wait_ge(s_wt, n + 1)
                    v.tensor_copy(relR[:, 0:D], rel_t[:, :])
                    v.tensor_tensor(relR[:, D:2 * D], ps_t[n % 2][:, :], w_1c[:, :], ALU.add).then_inc(s_wc, 1)
                    link(v.tensor_tensor(half_rz[:, :], b_ih[:, 0:2], b_hh[:, 0:2], ALU.add))
                    link(v.tensor_scalar(half_rz[:, :], half_rz[:, :], 0.5, None, ALU.mult))
                    link(v.tensor_scalar(half_rtc[:, :], tc[:, :], -1.0, None, ALU.mult))
                    link(v.tensor_tensor(half_rtc[:, :], half_rtc[:, :], tc[:, :], ALU.max))
                    link(v.tensor_scalar(half_rtc[:, :], half_rtc[:, :], 1e-9, None, ALU.add))
                    link(v.reciprocal(half_rtc[:, :], half_rtc[:, :]))
                    link(v.tensor_scalar(half_rtc[:, :], half_rtc[:, :], 0.5, None, ALU.mult))
                    link(v.tensor_scalar(half_b2[:, :], b_2[:, :], 0.5, None, ALU.mult))
                    dve.wait_ge(s_wc, n + 1)
                    link(v.tensor_copy(rel_hi[:, :], relR[:, :]))
                    link(v.tensor_tensor(rel_r1[:, :], relR[:, :], rel_hi[:, :], ALU.subtract))
                    link(v.tensor_copy(rel_hm[:, :], rel_r1[:, :]))
                    link(v.tensor_tensor(relR[:, :], rel_r1[:, :], rel_hm[:, :], ALU.subtract))
                    link(v.tensor_copy(rel_lo[:, :], relR[:, :]))
                    link(v.tensor_copy(rel_hm[0:TYPES, :], rel_hi[0:TYPES, :]))

        def quad(t, q, width=D):
            return t[:, bass.ds(q * (4 * width), 4 * width)]

        def table_rows(tab, q):
            return tab[bass.ds(q * (4 * P), 4 * P), :].rearrange("(j p) c -> p j c", p=P)

        def wide(ap, n):
            return ap.unsqueeze(2).to_broadcast([P, ap.shape[1], n])

        gat = ExitStack()
        COLS = 3
        gx = sb(gat, "gx", [P, COLS, TILES])
        zx = sb(gat, "zx", [P, NBP * COLS])
        scol = sb(gat, "scol", [P, NBP])
        dcol = sb(gat, "dcol", [P, NBP])
        of_sum = sb(gat, "of_sum", [P, NBP])
        of_self = sb(gat, "of_self", [P, NBP])

        def gat_nodes(l):
            def take_out(dve, v, q, xs, scr, s_ct):
                a3 = quad(acc, q).rearrange("p (j d) -> p j d", d=D)
                g3 = quad(tmp, q).rearrange("p (j d) -> p j d", d=D)
                x3 = xs.rearrange("p (j d) -> p j d", d=D)
                v.tensor_tensor(x3, a3, wide(of_sum[:, bass.ds(q * 4, 4)], D), ALU.mult)
                v.tensor_tensor(scr[:, :, :], g3, wide(of_self[:, bass.ds(q * 4, 4)], D), ALU.mult).then_inc(s_ct, 1)
                dve.wait_ge(s_ct, q * 2 + 1)
                v.tensor_tensor(x3, x3, scr[:, :, :], ALU.add).then_inc(s_ct, 1)
                dve.wait_ge(s_ct, q * 2 + 2)
                return v.tensor_tensor(x3, x3, b_lyr[0][:, :].unsqueeze(1).to_broadcast([P, 4, D]), ALU.add)

            def give(dve, v, q, ps_c, xs, gsb, scr, s_ch):
                v.tensor_copy(gsb, ps_c[:, :, 0:D])
                v.tensor_copy(quad(tmp, q).rearrange("p (j d) -> p j d", d=D), ps_c[:, :, 0:D])
                v.tensor_copy(scol[:, bass.ds(q * 4, 4)].unsqueeze(2), ps_c[:, :, D:D + 1])
                return v.tensor_copy(dcol[:, bass.ds(q * 4, 4)].unsqueeze(2), ps_c[:, :, D + 1:D + 2])

            table_nodes(f"n{l}", take_x if l == 0 else take_out, w_node if l == 0 else None, b_node, None,
                        w_gat[:, l, :], D + 2, [(gat_tab[l], 0, D)], D, give)

        def gather_rows(pool, rows, tab, s_idx, s_row, s_used, stashed=False):
            mine = range(0, SLOTS, 2 if stashed else 1)

            def gather(r, k):
                pool.wait_ge(s_idx[k], r * 16 + 16)
                pool.sem_inc(s_turn, 1)
                for t in range(GT):
                    pool.indirect_dma_start(rows[:, k, t, :], None, tab[:, :],
                                            bass.IndirectOffsetOnAxis(ap=src_slot[:, k, t:t + 1], axis=0)).then_inc(s_row[k], 16)

            for k in mine:
                gather(0, k)
            with pool.Fori(1, GROUPS // SLOTS) as i:
                for k in mine:
                    n = pool.value_load(done_row[0:1, bass.ds(i * SLOTS + (k - SLOTS), 1)], min_val=1, max_val=V)
                    pool.wait_ge(s_used, n + RING)
                    gather(i, k)

        def announce(sp, s_idx, s_row, s_landed, rows=None, s_used=None):
            AHEAD = 8
            rounds = GROUPS // SLOTS
            stashed = rows is not None

            def indices(g, k):
                sp.dma_start(src_slot[:, k, :], src_g[:, bass.ds(g * GT, GT)]).then_inc(s_idx[k], 16)

            def bring(g, k):
                sp.dma_start(rows[:, k, :, :], edge_v[bass.ds(g * P, P), :].rearrange("p (t d) -> p t d", d=D)).then_inc(s_row[k], 16)

            def step(r, k):
                odd = stashed and k % 2 == 1
                fill = 16 if odd else 16 * GT
                sp.wait_ge(s_row[k], r * fill + fill)
                sp.sem_inc(s_landed, 1)
                if not odd:
                    if not isinstance(r, int) or r < rounds - 1:
                        indices(r * SLOTS + (k + SLOTS), k)
                    return
                ahead = r * SLOTS + (k + AHEAD)
                if isinstance(r, int) and ahead >= GROUPS:
                    return
                if not isinstance(r, int) or ahead >= SLOTS:
                    n = sp.value_load(done_row[0:1, bass.ds(r * SLOTS + (k + AHEAD - SLOTS), 1)], min_val=1, max_val=V)
                    sp.wait_ge(s_used, n + RING)
                bring(ahead, (k + AHEAD) % SLOTS)

            for k in range(SLOTS):
                if not (stashed and k % 2 == 1):
                    indices(k, k)
                elif k < AHEAD:
                    bring(k, k)
            for k in range(SLOTS):
                step(0, k)
            with sp.Fori(1, rounds - 1) as i:
                for k in range(SLOTS):
                    step(i, k)
            for k in range(SLOTS):
                step(rounds - 1, k)

        def group_of(eng, v):
            return eng.value_load(grp_row[0:1, bass.ds(v, 1)], min_val=0, max_val=GROUPS - 1)

        def slot_of(eng, v):
            return eng.value_load(slot_row[0:1, bass.ds(v, 1)], min_val=0, max_val=SLOTS - 1)

        def landed(name, slots=SLOTS):
            return [top.enter_context(nc.semaphore(f"{name}_landed{k}")) for k in range(slots)]

        s_turn = sem(top, "gather_turn")

        def steps(first, body):
            whole = (V - 1) // RING
            with first.Fori(0, whole) as i:
                for k in range(RING):
                    body(i * RING + k, k)
            for v in range(whole * RING, V - 1):
                body(v, v % RING)

        def gat_logits(l):
            with phase() as st:
                part = sb(st, f"g{l}_parts", [P, 2, 3, NBP], BF16)
                rest = sb(st, f"g{l}_rest", [P, 2, NBP])
                trow = sb(st, f"g{l}_lo_rows", [P, RING, 2 * GE], BF16)
                oh = sb(st, f"g{l}_oh", [P, RING, 2 * GE], BF16)
                pid = sb(st, f"g{l}_pid", [P, 1])
                neg_pid = sb(st, f"g{l}_neg_pid", [P, 1])
                sq = sb(st, f"g{l}_sq", [P, 2, GE])
                pid_i = sb(st, f"g{l}_pid_i", [P, 1], I32)
                eq = sb(st, f"g{l}_eq", [P, 2, 2, GT, NBP])
                pick = sb(st, f"g{l}_pick", [P, 2, 2, GT])
                u = sb(st, f"g{l}_u", [P, TILES])
                ps_c = [ps(st, f"g{l}_psc{i}", [P, 2 * GT, 64]) for i in range(2)]
                s_pid = sem(st, f"g{l}_pid_ready")
                s_part = sem(st, f"g{l}_parts_ready")
                s_lo = [sem(st, f"g{l}_lo{k}") for k in range(RING)]
                s_oh = sem(st, f"g{l}_onehot_ready")
                s_oh2 = sem(st, f"g{l}_onehot2_ready")
                s_sq = sem(st, f"g{l}_squares_ready")
                s_c = sem(st, f"g{l}_candidates")
                s_eq = sem(st, f"g{l}_matches_ready")
                s_take = sem(st, f"g{l}_candidates_taken")
                s_pick = sem(st, f"g{l}_picked")
                s_u = sem(st, f"g{l}_sum_ready")
                stash = sb(st, f"g{l}_stash", [P, STASH, GT, D])
                s_idx = [sem(st, f"g{l}_idx{k}") for k in range(STASH)]
                s_st = [sem(st, f"g{l}_stashed{k}") for k in range(STASH)]
                s_land = landed(f"g{l}", STASH)
                LEAD = 2
                tabs = (dcol, scol)
                with nc.Block() as block:
                    @block.gpsimd
                    def _(pool):
                        nc.gpsimd.iota(pid_i[:, :], pattern=[[0, 1]], base=0, channel_multiplier=1).then_inc(s_pid, 1)
                        pool.wait_ge(s_pid, 1)
                        nc.gpsimd.tensor_copy(pid[:, :], pid_i[:, :]).then_inc(s_pid, 1)
                        pool.wait_ge(s_pid, 2)

                        def gather(r, k):
                            pool.wait_ge(s_idx[k], r * 16 + 16)
                            if not isinstance(r, int):
                                pool.wait_ge(s_st[k], r * 16)
                            pool.sem_inc(s_turn, 1)
                            for t in range(GT):
                                pool.indirect_dma_start(stash[:, k, t, :], None, gat_tab[l][:, :],
                                                        bass.IndirectOffsetOnAxis(ap=src_slot[:, k, t:t + 1], axis=0)).then_inc(s_land[k], 16)

                        for k in range(STASH):
                            gather(0, k)
                        with pool.Fori(1, GROUPS // SLOTS) as i:
                            for k in range(STASH):
                                gather(i, k)

                    @block.scalar
                    def _(act):
                        act.wait_ge(s_pid, 2)
                        nc.scalar.activation(neg_pid[:, :], pid[:, :], ACT.Copy, scale=-1.0).then_inc(s_pid, 1)
                        act.wait_ge(s_pid, 3)
                        act.sem_inc(s_oh2, RING)

                        def digits(g, k):
                            act.dma_start(trow[:, k % RING, :], lo_rows[bass.ds(g, 1), :].to_broadcast([P, 2 * GE])).then_inc(s_lo[k % RING], 16)

                        def onehot(i, k, more):
                            g = i * RING + k
                            act.wait_ge(s_c, g + 1)
                            act.wait_ge(s_lo[k], i * 16 + 16)
                            nc.scalar.activation(sq[:, k % 2, :], trow[:, k, GE:2 * GE], ACT.Square, bias=neg_pid[:, :]).then_inc(s_sq, 1)
                            act.wait_ge(s_sq, g + 1)
                            nc.scalar.activation(oh[:, k, GE:2 * GE], sq[:, k % 2, :], ACT.Relu, scale=-1.0, bias=1.0).then_inc(s_oh2, 1)
                            if more:
                                act.wait_ge(s_oh, g + 1 + RING)
                                digits(g + RING, k)

                        rounds = GROUPS // RING
                        for k in range(RING):
                            digits(k, k)
                        with act.Fori(0, rounds - 1) as i:
                            for k in range(RING):
                                onehot(i, k, True)
                        for k in range(RING):
                            onehot(rounds - 1, k, False)

                    @block.sync
                    def _(sp):
                        def indices(g, k):
                            sp.dma_start(src_slot[:, k, :], src_g[:, bass.ds(g * GT, GT)]).then_inc(s_idx[k], 16)

                        def store(r, k):
                            sp.wait_ge(s_land[k], r * (16 * GT) + 16 * GT)
                            sp.dma_start(edge_v[bass.ds(r * (SLOTS * P) + (2 * k + 1) * P, P), :],
                                         stash[:, k, :, :].rearrange("p t d -> p (t d)")).then_inc(s_st[k], 16)

                        rounds = GROUPS // SLOTS
                        for k in range(STASH):
                            indices(2 * k + 1, k)
                        with sp.Fori(0, rounds - 1) as i:
                            for k in range(STASH):
                                store(i, k)
                                indices(i * SLOTS + (SLOTS + 2 * k + 1), k)
                        for k in range(STASH):
                            store(rounds - 1, k)
                        for k in range(STASH):
                            sp.wait_ge(s_st[k], rounds * 16)

                    @block.vector
                    def _(dve):
                        v = nc.vector

                        def onehot(g, k, r):
                            dve.wait_ge(s_lo[k % RING], r * 16 + 16)
                            dve.wait_ge(s_c, g + 1)
                            v.tensor_scalar(oh[:, k % RING, 0:GE], trow[:, k % RING, 0:GE], pid[:, :], None, ALU.is_equal).then_inc(s_oh, 1)

                        def match(g, k):
                            hi = hi_g[:, :, bass.ds(g * GT, GT)].unsqueeze(3).to_broadcast([P, 2, GT, NBP])
                            dve.wait_ge(s_pick, g + 1)
                            v.tensor_tensor(eq[:, k % 2, :, :, :], iota[:, 0:NBP].unsqueeze(1).unsqueeze(1).to_broadcast([P, 2, GT, NBP]), hi,
                                            ALU.is_equal).then_inc(s_eq, 1)

                        def take(g, k):
                            cand = ps_c[k % 2][:, :, 0:NBP].rearrange("p (a t) b -> p a t b", a=2)
                            dve.wait_ge(s_c, g + 1 + RING)
                            dve.wait_ge(s_eq, g + 1)
                            v.tensor_tensor(eq[:, k % 2, :, :, :], eq[:, k % 2, :, :, :], cand, ALU.mult).then_inc(s_take, 1)

                        def choose(g, k):
                            dve.wait_ge(s_take, g + 3)
                            v.tensor_reduce(pick[:, k % 2, :, :], eq[:, k % 2, :, :, :], AX, ALU.add).then_inc(s_pick, 1)

                        def add(g, k):
                            dve.wait_ge(s_pick, g + 3)
                            v.tensor_tensor(u[:, bass.ds(g * GT, GT)], pick[:, k % 2, 0, :], pick[:, k % 2, 1, :], ALU.add).then_inc(s_u, 1)

                        def body(i, k, has):
                            g = i * RING + k
                            if has(2):
                                onehot(g + 2, k + 2, i + (k + 2) // RING)
                            if has(1):
                                take(g + 1, k + 1)
                            add(g, k)
                            if has(2):
                                match(g + 2, k + 2)
                            if has(1):
                                dve.wait_ge(s_u, g + 1)
                                choose(g + 1, k + 1)

                        dve.sem_inc(s_take, 2)
                        dve.sem_inc(s_pick, 2)
                        n = 0
                        for a, tab in enumerate(tabs):
                            left = tab[:, :]
                            for i in range(3):
                                v.tensor_copy(part[:, a, i, :], left).then_inc(s_part, 1)
                                n += 1
                                dve.wait_ge(s_part, n)
                                if i < 2:
                                    v.tensor_tensor(rest[:, a, :], left, part[:, a, i, :], ALU.subtract).then_inc(s_part, 1)
                                    n += 1
                                    dve.wait_ge(s_part, n)
                                    left = rest[:, a, :]
                        dve.sem_inc(s_oh, RING)
                        dve.wait_ge(s_pid, 2)
                        for g in range(LEAD):
                            onehot(g, g, 0)
                            match(g, g)
                        take(0, 0)
                        choose(0, 0)
                        whole = (GROUPS - LEAD) // RING
                        with dve.Fori(0, whole) as i:
                            for k in range(RING):
                                body(i, k, lambda d: True)
                        for g in range(whole * RING, GROUPS):
                            body(g // RING, g % RING, lambda d: g + d < GROUPS)
                        dve.wait_ge(s_u, GROUPS)
                        v.tensor_copy(gx[:, 2, :], w_g[:, :]).then_inc(s_u, 1)
                        v.scalar_tensor_tensor(gx[:, 0, :], u[:, :], SLOPE, u[:, :], ALU.mult, ALU.max).then_inc(s_u, 1)
                        dve.wait_ge(s_u, GROUPS + 2)

                    @block.tensor
                    def _(pe):
                        pe.sem_inc(s_c, RING)
                        pe.wait_ge(s_part, 10)
                        with pe.Fori(0, GROUPS // RING) as i:
                            for k in range(RING):
                                g = i * RING + k
                                pe.wait_ge(s_oh, g + 1 + RING)
                                pe.wait_ge(s_oh2, g + 1 + RING)
                                pe.wait_ge(s_take, g + 1)
                                for a in range(2):
                                    for t in range(GT):
                                        for n in range(3):
                                            m = nc.tensor.matmul(ps_c[k % 2][:, a * GT + t, 0:NBP], oh[:, k, a * GE + t * P:a * GE + (t + 1) * P],
                                                                 part[:, a, n, :], start=(n == 0), stop=(n == 2))
                                m.then_inc(s_c, 1)

        def segment_softmax(name, x, heads, last_max=None):
            CH = {1: 112, HEADS: 16}[heads]
            J = TILES // CH
            R = heads * CH
            W = J * P
            with phase() as st:
                if heads == 1:
                    xs = sb(st, name + "_x", [R, W])[:, :]
                    new = sb(st, name + "_new", [R, W + 1])[:, :]
                else:
                    xs = tmp[0:R, 0:W]
                    new = acc[0:R, 0:W + 1]
                da = sb(st, name + "_dst", [R, W + 1], I32)
                db = sb(st, name + "_dst_before", [R, W + 1], I32)
                fw = db[:, 0:W].bitcast(F32)
                bw = da[:, 0:W].bitcast(F32)
                tail = sb(st, name + "_tail", [R, 4])
                edge = sb(st, name + "_edge", [1, 2, R])
                first = sb(st, name + "_first", [1, 2, R])
                run = sb(st, name + "_run", [1, R])
                has = edge[:, 1, :]
                give = edge[:, 0, :]
                start = sb(st, name + "_start", [R, 1])
                ps_x = [ps(st, f"{name}_psx{i}", [P, 512]) for i in range(2)]
                ps_e = ps(st, name + "_pse", [1, 2, P])
                ps_s = ps(st, name + "_pss", [P, 1])
                s_d = sem(st, name + "_dst_in")
                s_x = sem(st, name + "_chunks")
                s_xc = sem(st, name + "_chunks_copied")
                s_t = sem(st, name + "_tails")
                s_e = sem(st, name + "_edges")
                s_g = sem(st, name + "_given")
                s_s = sem(st, name + "_starts")
                s_m = sem(st, name + "_max_ready")
                s_o = sem(st, name + "_max_back")
                s_oc = sem(st, name + "_max_taken")
                s_c = sem(st, name + "_chain")
                xj = x[:, :, :].rearrange("p h (c j) -> p (h c) j", j=J)
                parts = [(j, min(4, J - j)) for j in range(0, J, 4)]
                with nc.Block() as block:
                    @block.sync
                    def _(sp):
                        def load(t, o):
                            for h in range(heads):
                                sp.dma_start(t[h * CH:(h + 1) * CH, 0:W],
                                             dst_flat[o:o + TILES * P].rearrange("(c i) -> c i", c=CH)).then_inc(s_d, 16)
                                with nc.allow_non_contiguous_dma(reason="one edge of each chunk"):
                                    sp.dma_start(t[h * CH:(h + 1) * CH, W:W + 1],
                                                 dst_flat[o + W:o + CH * W + 1:W].rearrange("(c i) -> c i", i=1)).then_inc(s_d, 16)
                        load(da, 1)
                        load(db, 0)
                        sp.wait_ge(s_d, 4 * 16 * heads)

                    @block.tensor
                    def _(pe):
                        for n, (j, m) in enumerate(parts):
                            if n >= 2:
                                pe.wait_ge(s_xc, n - 1)
                            for i in range(m):
                                t = nc.tensor.transpose(ps_x[n % 2][0:R, i * P:(i + 1) * P], xj[:, :, j + i], ident[:, :])
                            t.then_inc(s_x, 1)
                        for way in range(2):
                            pe.wait_ge(s_t, way + 1)
                            for i in range(2):
                                t = nc.tensor.matmul(ps_e[:, i, 0:R], tail[:, 2 * way + i:2 * way + i + 1], ident[0:R, 0:R], start=True, stop=True)
                            t.then_inc(s_e, 1)
                            pe.wait_ge(s_g, way + 1)
                            nc.tensor.matmul(ps_s[0:R, :], give, ones[0:1, :], start=True, stop=True).then_inc(s_s, 1)
                        pe.wait_ge(s_m, 1)
                        for n, (j, m) in enumerate(parts if last_max is None else parts + parts):
                            if n >= 2:
                                pe.wait_ge(s_oc, n - 1)
                            if n == len(parts):
                                pe.wait_ge(s_m, 2)
                            for i in range(m):
                                t = nc.tensor.transpose(ps_x[n % 2][:, i * R:(i + 1) * R], (fw if n < len(parts) else bw)[:, (j + i) * P:(j + i + 1) * P], ident[0:R, 0:R])
                            t.then_inc(s_o, 1)

                    @block.scalar
                    def _(act):
                        for n, (j, m) in enumerate(parts):
                            act.wait_ge(s_x, n + 1)
                            nc.scalar.activation(xs[:, j * P:(j + m) * P], ps_x[n % 2][0:R, 0:m * P], ACT.Copy).then_inc(s_xc, 1)
                        act.wait_ge(s_oc, len(parts))
                        nc.scalar.activation(x[:, :, :], x[:, :, :], ACT.Exp).then_inc(s_xc, 1)
                        act.wait_ge(s_xc, len(parts) + 1)

                    @block.vector
                    def _(dve):
                        v = nc.vector
                        c = Count(s_c)

                        def link(ins):
                            dve.wait_ge(s_c, c.inc(ins))

                        f3 = first[:, :, :].rearrange("o w (h c) -> o w h c", c=CH)
                        link(v.memset(first[:, :, :], 0.0))
                        v.memset(f3[:, 0, :, 0:1], -BIG)
                        link(v.memset(f3[:, 1, :, CH - 1:CH], -BIG))

                        def scan(out, way, init):
                            def rev(ap):
                                return ap[:, ::-1] if way else ap
                            return v.tensor_tensor_scan(rev(out), rev(new[:, way:W + way]), rev(xs), init, ALU.add, ALU.max)

                        for way in range(2):
                            if way == 0:
                                dve.wait_ge(s_d, 4 * 16 * heads)
                                link(v.tensor_tensor(new, da[:, :], db[:, :], ALU.not_equal))
                                link(v.tensor_scalar(new, new, -BIG, None, ALU.mult))
                            cut = new[:, way:W + way]
                            out = bw if way else fw
                            dve.wait_ge(s_xc, len(parts))
                            link(scan(out, way, -BIG))
                            end = 0 if way else W - 1
                            v.tensor_copy(tail[:, 2 * way:2 * way + 1], out[:, end:end + 1])
                            link(v.tensor_reduce(tail[:, 2 * way + 1:2 * way + 2], cut, AX, ALU.min))
                            v.tensor_copy(run[0:1, 0:1], first[0:1, 0, 0:1]).then_inc(s_t, 1)
                            dve.wait_ge(s_e, way + 1)
                            link(v.tensor_copy(edge[:, :, :], ps_e[:, :, 0:R]))
                            link(v.tensor_tensor(has, has, first[:, way, :], ALU.add))
                            h_, e_, r_ = has, edge[:, 0, :], run[:, :]
                            if way:
                                h_, e_, r_ = h_[:, ::-1], e_[:, ::-1], r_[:, ::-1]
                            link(v.tensor_tensor_scan(r_, h_, e_, -BIG, ALU.add, ALU.max))
                            g3 = give.rearrange("o (h c) -> o h c", c=CH)
                            r3 = run[:, :].rearrange("o (h c) -> o h c", c=CH)
                            link(v.memset(give, -BIG))
                            if way:
                                v.tensor_copy(g3[:, :, 0:CH - 1], r3[:, :, 1:CH]).then_inc(s_g, 1)
                            else:
                                v.tensor_copy(g3[:, :, 1:CH], r3[:, :, 0:CH - 1]).then_inc(s_g, 1)
                            dve.wait_ge(s_s, way + 1)
                            link(v.tensor_copy(start[:, :], ps_s[0:R, :]))
                            scan(out, way, start[:, :])
                        link(v.tensor_copy(run[0:1, 0:1], first[0:1, 0, 0:1]))
                        v.tensor_tensor(fw, fw, bw, ALU.max).then_inc(s_m, 1)
                        if last_max is not None:
                            dve.wait_ge(s_m, 1)
                            v.scalar_tensor_tensor(bw, new[:, 1:W + 1], 0.0, fw, ALU.is_lt, ALU.mult).then_inc(s_m, 1)
                        for n, (j, m) in enumerate(parts):
                            dve.wait_ge(s_o, n + 1)
                            v.tensor_tensor(xj[:, :, j:j + m], xj[:, :, j:j + m],
                                            ps_x[n % 2][:, 0:m * R].rearrange("p (j r) -> p r j", r=R), ALU.subtract).then_inc(s_oc, 1)
                        if last_max is not None:
                            lj = last_max.rearrange("p (c j) -> p c j", j=J)
                            for n, (j, m) in enumerate(parts):
                                dve.wait_ge(s_o, len(parts) + n + 1)
                                v.tensor_copy(lj[:, :, j:j + m], ps_x[(len(parts) + n) % 2][:, 0:m * R].rearrange("p (j r) -> p r j", r=R)).then_inc(s_oc, 1)
                        dve.wait_ge(s_oc, len(parts) * (1 if last_max is None else 2))

        def edge_sums(name, x, heads, cols, zacc, tab, finish=None):
            with phase() as st:
                vr = sb(st, name + "_values", [P, RING if tab is None else SLOTS, GT, D])
                oh = sb(st, name + "_oh", [P, RING, GT, P])
                wv = sb(st, name + "_wv", [P, RING, GT, D + cols])
                ps_o = [ps(st, name + f"_pso{i}", [P, 512]) for i in range(RING)]
                s_val = [sem(st, name + f"_val{k}") for k in range(RING)] if tab is None else landed(name)
                s_idx = [sem(st, name + f"_idx{k}") for k in range(SLOTS)] if tab is not None else None
                s_landed = sem(st, name + "_groups_landed")
                s_fin = sem(st, name + "_finish")
                s_e = sem(st, name + "_finish_exp")
                s_wv = sem(st, name + "_weighted_ready")
                s_we = sem(st, name + "_weights_ready")
                s_o = sem(st, name + "_sums_done")
                s_acc = sem(st, name + "_sums_added")
                s_z = sem(st, name + "_cleared")
                s_take = sem(st, name + "_sums_copied")
                if tab is None:
                    so = sb(st, name + "_sums", [P, RING, D + cols])

                AHEAD = 2

                def back(eng, v_, v, k):
                    h = k % RING
                    b = eng.value_load(blk_row[0:1, bass.ds(v, 1)], min_val=0, max_val=BLOCKS - 1)
                    ab = acc[:, bass.ds(b * D, D)]
                    zb = zacc[:, bass.ds(b * cols, cols)]
                    eng.wait_ge(s_acc, v + RING)
                    sums = ps_o[h] if tab is not None else so[:, h, :]
                    eng.wait_ge(s_o if tab is not None else s_take, v + 1 + RING)
                    if tab is None:
                        eng.sem_inc(s_turn, 1)
                    v_.tensor_tensor(ab, ab, sums[:, 0:D], ALU.add)
                    v_.tensor_tensor(zb, zb, sums[:, D:D + cols], ALU.add).then_inc(s_acc, 1)

                with nc.Block() as block:
                    @block.gpsimd
                    def _(pool):
                        if tab is not None:
                            gather_rows(pool, vr, tab, s_idx, s_val, s_wv, True)
                        else:
                            pool.wait_ge(s_z, 1)
                            with pool.Fori(0, V // RING) as i:
                                for k in range(RING):
                                    back(pool, nc.gpsimd, i * RING + k, k)
                            pool.wait_ge(s_acc, V + RING)

                    @block.sync
                    def _(sp):
                        if tab is not None:
                            announce(sp, s_idx, s_val, s_landed, vr, s_wv)
                            return
                        with sp.Fori(0, V // RING) as i:
                            for k in range(RING):
                                g = group_of(sp, i * RING + k)
                                sp.wait_ge(s_wv, i * RING + k + 1)
                                sp.dma_start(vr[:, k, :, :], edge_v[bass.ds(g * P, P), :].rearrange("p (t d) -> p t d", d=D)).then_inc(s_val[k], 16)

                    @block.vector
                    def _(dve):
                        v_ = nc.vector

                        def front(v, k, fill):
                            h = k % RING
                            slot = k % RING if tab is None else slot_of(dve, v)
                            dve.wait_ge(s_o, v + 1)
                            v_.tensor_tensor(oh[:, h, :, :], iota[:, :].unsqueeze(1).to_broadcast([P, GT, P]),
                                             dst_tab[:, bass.ds(v * GT, GT)].unsqueeze(2).to_broadcast([P, GT, P]), ALU.is_equal)
                            if tab is None:
                                dve.wait_ge(s_val[k % RING], fill)
                            dve.wait_ge(s_we, v + 1)
                            e = wv[:, h, :, D:D + heads]
                            v_.tensor_tensor(wv[:, h, :, 0:D].rearrange("p t (h d) -> p t h d", h=heads),
                                             vr[:, bass.ds(slot, 1), :, :].rearrange("p o t (h d) -> p (o t) h d", h=heads),
                                             e.unsqueeze(3).to_broadcast([P, GT, heads, D // heads]), ALU.mult).then_inc(s_wv, 1)

                        v_.memset(acc[:, :], 0.0)
                        v_.memset(zacc[:, :], 0.0).then_inc(s_z, 1)
                        dve.sem_inc(s_wv, RING)
                        dve.wait_ge(s_z, 1)
                        for v in range(AHEAD):
                            front(v, v, 16)
                        whole = (V - AHEAD) // RING
                        with dve.Fori(0, whole) as i:
                            for k in range(RING):
                                front(i * RING + (k + AHEAD), k + AHEAD, (i + (k + AHEAD) // RING) * 16 + 16)
                                if tab is not None:
                                    back(dve, v_, i * RING + k, k)
                        for v in range(whole * RING, V):
                            if v + AHEAD < V:
                                front(v + AHEAD, (v + AHEAD) % RING, ((v + AHEAD) // RING) * 16 + 16)
                            if tab is not None:
                                back(dve, v_, v, v % RING)
                        dve.wait_ge(s_acc, V + RING)
                        if finish is not None:
                            finish(dve, None, s_fin, s_e)

                    @block.scalar
                    def _(act):
                        def weights(v, k):
                            g = group_of(act, v)
                            act.wait_ge(s_o, v + 1)
                            if tab is not None:
                                act.wait_ge(s_landed, g + 1)
                            nc.scalar.activation(wv[:, k % RING, :, D:D + cols],
                                                 x[:, :, bass.ds(g * GT, GT)].rearrange("p h t -> p t h"), ACT.Copy).then_inc(s_we, 1)

                        def take(v, k):
                            if tab is None:
                                act.wait_ge(s_acc, v + 1)
                                act.wait_ge(s_o, v + 1 + RING)
                                nc.scalar.activation(so[:, k, :], ps_o[k][:, 0:D + cols], ACT.Copy).then_inc(s_take, 1)

                        act.sem_inc(s_take, RING)
                        for v in range(AHEAD):
                            weights(v, v)
                        with act.Fori(0, (V - AHEAD) // RING) as i:
                            for k in range(RING):
                                weights(i * RING + (k + AHEAD), k + AHEAD)
                                take(i * RING + k, k)
                        for v in range((V - AHEAD) // RING * RING, V):
                            if v + AHEAD < V:
                                weights(v + AHEAD, v + AHEAD)
                            take(v, v % RING)
                        if finish is not None:
                            finish(None, act, s_fin, s_e)

                    @block.tensor
                    def _(pe):
                        pe.sem_inc(s_o, RING)
                        pe.sem_inc(s_acc, RING)
                        with pe.Fori(0, V // RING) as i:
                            for k in range(RING):
                                v = i * RING + k
                                h = k % RING
                                pe.wait_ge(s_wv, v + 1 + RING)
                                pe.wait_ge(s_we, v + 1)
                                pe.wait_ge(s_acc if tab is not None else s_take, v + 1)
                                for t in range(GT):
                                    m = nc.tensor.matmul(ps_o[h][:, 0:D + cols], oh[:, h, t, :], wv[:, h, t, :],
                                                         start=(t == 0), stop=(t == GT - 1))
                                m.then_inc(s_o, 1)

        def gat_sums(l):
            es = sb(gat, f"f{l}_self", [P, NBP])
            has = sb(gat, f"f{l}_has", [P, NBP])
            me = sb(gat, f"f{l}_max", [P, NBP])
            mm_ = sb(gat, f"f{l}_all_max", [P, NBP])
            z = sb(gat, f"f{l}_z", [P, NBP])

            def finish(dve, act, s_ch, s_e):
                z3 = zx[:, :].rearrange("p (b c) -> p b c", c=COLS)

                def flat(c):
                    return z3[:, :, c:c + 1].rearrange("p b o -> p (b o)")

                if dve is None:
                    for t in (of_sum, of_self):
                        act.wait_ge(s_ch, F_EXP)
                        nc.scalar.activation(t[:, :], t[:, :], ACT.Exp).then_inc(s_e, 1)
                    return
                v = nc.vector
                c = Count(s_ch)

                def link(ins):
                    dve.wait_ge(s_ch, c.inc(ins))

                link(v.tensor_tensor(z[:, :], scol[:, :], dcol[:, :], ALU.add))
                link(v.scalar_tensor_tensor(es[:, :], z[:, :], SLOPE, z[:, :], ALU.mult, ALU.max))
                link(v.tensor_scalar(has[:, :], flat(0), 0.0, None, ALU.is_gt))
                link(v.tensor_scalar(me[:, :], has[:, :], -1.0, 1.0, ALU.mult, ALU.add))
                link(v.tensor_tensor(me[:, :], me[:, :], es[:, :], ALU.mult))
                link(v.tensor_tensor(has[:, :], has[:, :], flat(1), ALU.mult))
                link(v.tensor_tensor(me[:, :], me[:, :], has[:, :], ALU.add))
                link(v.tensor_tensor(mm_[:, :], me[:, :], es[:, :], ALU.max))
                link(v.tensor_tensor(of_sum[:, :], me[:, :], mm_[:, :], ALU.subtract))
                link(v.tensor_tensor(of_self[:, :], es[:, :], mm_[:, :], ALU.subtract))
                assert c.n == F_EXP
                dve.wait_ge(s_e, 2)
                link(v.tensor_tensor(z[:, :], flat(0), of_sum[:, :], ALU.mult))
                link(v.tensor_tensor(z[:, :], z[:, :], of_self[:, :], ALU.add))
                link(v.reciprocal(z[:, :], z[:, :]))
                link(v.tensor_tensor(of_sum[:, :], of_sum[:, :], z[:, :], ALU.mult))
                link(v.tensor_tensor(of_self[:, :], of_self[:, :], z[:, :], ALU.mult))
                if l == 0:
                    link(v.tensor_scalar(deg[:, :], flat(2), 1.0, None, ALU.add))

            edge_sums(f"e{l}", gx, 1, COLS, zx, gat_tab[l], finish)

        F_EXP = 10

        def residual_norm(name, prep):
            with phase() as st:
                mean = sb(st, f"{name}_mean", [P, NBP])
                var = sb(st, f"{name}_var", [P, NBP])
                sd = sb(st, f"{name}_sd", [P, NBP])
                s_ch = sem(st, f"{name}_chain")
                s_var = sem(st, f"{name}_var_ready")
                s_sd = sem(st, f"{name}_sd_ready")
                t3 = tmp[:, :].rearrange("p (b d) -> p b d", d=D)
                x3 = x_n[:, :].rearrange("p (b d) -> p b d", d=D)
                with nc.Block() as block:
                    @block.vector
                    def _(dve):
                        v = nc.vector
                        c = Count(s_ch)

                        def link(ins):
                            dve.wait_ge(s_ch, c.inc(ins))

                        prep(link, st, t3, x3)
                        link(v.tensor_reduce(mean[:, :], t3, AX, ALU.add))
                        link(v.tensor_scalar(mean[:, :], mean[:, :], 1.0 / D, None, ALU.mult))
                        link(v.tensor_tensor(t3, t3, wide(mean[:, :], D), ALU.subtract))
                        link(v.tensor_tensor(x3, t3, t3, ALU.mult))
                        v.tensor_reduce(var[:, :], x3, AX, ALU.add).then_inc(s_var, 1)
                        dve.wait_ge(s_sd, 1)
                        link(v.reciprocal(sd[:, :], sd[:, :]))
                        link(v.tensor_tensor(x3, t3, wide(sd[:, :], D), ALU.mult))

                    @block.scalar
                    def _(act):
                        act.wait_ge(s_var, 1)
                        nc.scalar.activation(sd[:, :], var[:, :], ACT.Sqrt, bias=eps_c[:, :], scale=1.0 / D).then_inc(s_sd, 1)

        def every(b):
            return b[:, :].unsqueeze(1).to_broadcast([P, NBP, D])

        def gat_out(link, st, t3, x3):
            v = nc.vector
            a3 = acc[:, :].rearrange("p (b d) -> p b d", d=D)
            link(v.tensor_tensor(t3, t3, wide(of_self[:, :], D), ALU.mult))
            link(v.tensor_tensor(a3, a3, wide(of_sum[:, :], D), ALU.mult))
            link(v.tensor_tensor(t3, t3, a3, ALU.add))
            link(v.tensor_tensor(t3, t3, every(b_lyr[1]), ALU.add))
            link(v.tensor_tensor(t3, t3, x3, ALU.add))

        def quads(eng, body, lead):
            whole = (QUADS - lead) // 2
            with eng.Fori(0, whole) as i:
                for k in range(2):
                    body(i * 2 + k, k, lambda d: True)
            for q in range(whole * 2, QUADS):
                body(q, q % 2, lambda d: q + d < QUADS)

        def table_nodes(name, take, w_first, b_first, keep, w_second, width, tabs, tab_width, give, start=None):
            with phase() as st:
                xs = sb(st, f"{name}_xs", [P, 2, 4 * D])
                xT = sb(st, f"{name}_xT", [P, 2, 4 * P])
                hT = sb(st, f"{name}_hT", [P, 2, 4 * P])
                gsb = sb(st, f"{name}_gsb", [P, 2, 4, tab_width])
                scr = sb(st, f"{name}_scr", [P, 4, D])
                scr_t = sb(st, f"{name}_scr_t", [P, 4, D])
                ps_a = [ps(st, f"{name}_psa{i}", [P, 4 * P]) for i in range(2)]
                ps_b = [ps(st, f"{name}_psb{i}", [P, 4 * P]) for i in range(2)]
                ps_c = [ps(st, f"{name}_psc{i}", [P, 4, 256]) for i in range(2)]
                s_xs = sem(st, f"{name}_xs_ready")
                s_tr = sem(st, f"{name}_transposed")
                s_xT = sem(st, f"{name}_xT_ready")
                s_h = sem(st, f"{name}_h_done")
                s_hT = sem(st, f"{name}_hT_ready")
                s_g = sem(st, f"{name}_products_done")
                s_gsb = sem(st, f"{name}_rows_ready")
                s_out = sem(st, f"{name}_stored")
                s_free = sem(st, f"{name}_store_buffer_free")
                s_ch = sem(st, f"{name}_chain")
                s_ct = sem(st, f"{name}_take_chain")
                s_pre = sem(st, f"{name}_start")
                s_act = sem(st, f"{name}_act")
                with nc.Block() as block:
                    @block.vector
                    def _(dve):
                        v = nc.vector

                        def bring(q, k):
                            dve.wait_ge(s_tr, q + 1)
                            take(dve, v, q, xs[:, k, :], scr_t, s_ct).then_inc(s_xs, 1)

                        def body(q, k, has):
                            dve.wait_ge(s_g, q + 3)
                            dve.wait_ge(s_free, q + 1)
                            give(dve, v, q, ps_c[k], xs[:, k, :], gsb[:, k, :, :], scr, s_ch).then_inc(s_gsb, 1)
                            if has(2):
                                bring(q + 2, k)

                        if start is not None:
                            start(dve, v, s_pre, s_act)
                        dve.sem_inc(s_gsb, 2)
                        bring(0, 0)
                        bring(1, 1)
                        quads(dve, body, 2)
                        dve.wait_ge(s_gsb, QUADS + 2)

                    @block.tensor
                    def _(pe):
                        def turn(q, k):
                            pe.wait_ge(s_xs, q + 1)
                            pe.wait_ge(s_xT, q + 1)
                            for j in range(4):
                                i = nc.tensor.transpose(ps_a[k][:, j * P:(j + 1) * P], xs[:, k, j * D:(j + 1) * D], ident[:, :])
                            i.then_inc(s_tr, 1)

                        def body(q, k, has):
                            pe.wait_ge(s_xT, q + 3)
                            if w_first is not None:
                                pe.wait_ge(s_hT, q + 1)
                                nc.tensor.matmul(ps_b[k][:, :], w_first[:, :], xT[:, k, :], start=True, stop=True).then_inc(s_h, 1)
                                pe.wait_ge(s_hT, q + 3)
                            lhs = hT if w_first is not None else xT
                            pe.wait_ge(s_gsb, q + 1)
                            for j in range(4):
                                i = nc.tensor.matmul(ps_c[k][:, j, 0:width], lhs[:, k, j * P:(j + 1) * P], w_second,
                                                     start=True, stop=True)
                            i.then_inc(s_g, 1)
                            if has(1):
                                turn(q + 1, 1 - k)

                        pe.sem_inc(s_tr, 2)
                        pe.sem_inc(s_g, 2)
                        turn(0, 0)
                        quads(pe, body, 1)

                    @block.scalar
                    def _(act):
                        def copy(q, k):
                            act.wait_ge(s_tr, q + 3)
                            act.wait_ge(s_g, q + 1)
                            nc.scalar.activation(xT[:, k, :], ps_a[k][:, :], ACT.Identity).then_inc(s_xT, 1)

                        def body(q, k, has):
                            if w_first is not None:
                                act.wait_ge(s_h, q + 1)
                                if keep is not None:
                                    nc.scalar.activation(quad(keep, q), ps_b[k][:, :], ACT.Identity, bias=b_first[:, :])
                                nc.scalar.activation(hT[:, k, :], ps_b[k][:, :], ACT.Identity, bias=b_first[:, :]).then_inc(s_hT, 1)
                            if has(1):
                                copy(q + 1, 1 - k)

                        if start is not None:
                            start(act, None, s_pre, s_act)
                        act.sem_inc(s_xT, 2)
                        act.sem_inc(s_hT, 2)
                        copy(0, 0)
                        quads(act, body, 1)

                    @block.sync
                    def _(sp):
                        def body(q, k, has):
                            sp.wait_ge(s_gsb, q + 3)
                            for tab, lo, hi in tabs:
                                sp.dma_start(table_rows(tab, q), gsb[:, k, :, lo:hi]).then_inc(s_out, 16)
                            sp.wait_ge(s_out, (q + 1) * (16 * len(tabs)))
                            sp.sem_inc(s_free, 1)

                        sp.sem_inc(s_free, 2)
                        quads(sp, body, 0)

        def take_x(dve, v, q, xs, scr, s_ct):
            return v.tensor_copy(xs, quad(x_n, q))

        def sum_edges(name, tab, weighted):
            with phase() as st:
                rows = sb(st, f"{name}_rows", [P, SLOTS, GT, D])
                oh = sb(st, f"{name}_oh", [P, 2, GT, P])
                ps_o = [ps(st, f"{name}_pso{i}", [P, 512]) for i in range(2)]
                s_idx = [sem(st, f"{name}_idx{k}") for k in range(SLOTS)]
                s_row = landed(name)
                s_landed = sem(st, f"{name}_groups_landed")
                s_oh = sem(st, f"{name}_onehot_ready")
                s_o = sem(st, f"{name}_sums_done")
                s_acc = sem(st, f"{name}_sums_added")
                with nc.Block() as block:
                    @block.gpsimd
                    def _(pool):
                        pool.sem_inc(s_o, RING)
                        gather_rows(pool, rows, tab, s_idx, s_row, s_o)

                    @block.sync
                    def _(sp):
                        announce(sp, s_idx, s_row, s_landed)

                    @block.vector
                    def _(dve):
                        v_ = nc.vector

                        def front(v, k):
                            for t in range(GT):
                                col_ = bass.ds(v * GT + t, 1)
                                if weighted:
                                    i = v_.tensor_scalar(oh[:, k % 2, t, :], iota[:, :], dst_tab[:, col_], w_tab[:, col_],
                                                         ALU.is_equal, ALU.mult)
                                else:
                                    i = v_.tensor_scalar(oh[:, k % 2, t, :], iota[:, :], dst_tab[:, col_], None, ALU.is_equal)
                            i.then_inc(s_oh, 1)

                        def back(v, k):
                            b = dve.value_load(blk_row[0:1, bass.ds(v, 1)], min_val=0, max_val=BLOCKS - 1)
                            dve.wait_ge(s_acc, v + 2)
                            dve.wait_ge(s_o, v + 1 + RING)
                            ab = acc[:, bass.ds(b * D, D)]
                            v_.tensor_tensor(ab, ab, ps_o[k % 2][:, 0:D], ALU.add).then_inc(s_acc, 1)

                        front(0, 0)

                        def body(v, k):
                            front(v + 1, k + 1)
                            back(v, k)

                        steps(dve, body)
                        back(V - 1, (V - 1) % RING)
                        dve.wait_ge(s_acc, V + 2)

                    @block.tensor
                    def _(pe):
                        pe.sem_inc(s_acc, 2)
                        with pe.Fori(0, V // RING) as i:
                            for k in range(RING):
                                v = i * RING + k
                                g = group_of(pe, v)
                                slot = slot_of(pe, v)
                                pe.wait_ge(s_oh, v + 1)
                                pe.wait_ge(s_landed, g + 1)
                                pe.wait_ge(s_acc, v + 1)
                                for t in range(GT):
                                    m = nc.tensor.matmul(ps_o[k % 2][:, 0:D], oh[:, k % 2, t, :], rows[:, bass.ds(slot, 1), t, :].rearrange("p o d -> p (o d)"),
                                                         start=(t == 0), stop=(t == GT - 1))
                                m.then_inc(s_o, 1)


        def gcn_start(eng, v, s_pre, s_act):
            if v is None:
                eng.wait_ge(s_pre, 1)
                nc.scalar.activation(dis[:, :], dis[:, :], ACT.Sqrt).then_inc(s_act, 1)
                return
            v.tensor_scalar(dis[:, :], deg[:, :], 1e-30, None, ALU.max).then_inc(s_pre, 1)
            v.tensor_scalar(deg[:, :], deg[:, :], 0.0, None, ALU.is_gt).then_inc(s_pre, 1)
            eng.wait_ge(s_pre, 2)
            eng.wait_ge(s_act, 1)
            v.reciprocal(dis[:, :], dis[:, :]).then_inc(s_pre, 1)
            eng.wait_ge(s_pre, 3)
            v.tensor_tensor(dis[:, :], dis[:, :], deg[:, :], ALU.mult).then_inc(s_pre, 1)
            eng.wait_ge(s_pre, 4)

        def gcn_give(dve, v, q, ps_c, xs, gsb, scr, s_ch):
            dq = wide(dis[:, bass.ds(q * 4, 4)], D)
            v.tensor_tensor(quad(acc, q).rearrange("p (j d) -> p j d", d=D), ps_c[:, :, 0:D], dq, ALU.mult)
            return v.tensor_tensor(gsb, ps_c[:, :, 0:D], dq, ALU.mult)

        def gcn_out(link, st, t3, x3):
            v = nc.vector
            link(v.tensor_tensor(t3, acc[:, :].rearrange("p (b d) -> p b d", d=D), wide(dis[:, :], D), ALU.mult))
            link(v.tensor_tensor(t3, t3, every(b_gcn), ALU.add))
            link(v.tensor_tensor(t3, t3, x3, ALU.add))

        def ggn_start(eng, v, s_pre, s_act):
            if v is not None:
                v.memset(acc[:, :], 0.0)

        def ggn_give(dve, v, q, ps_c, xs, gsb, scr, s_ch):
            return v.tensor_copy(gsb, ps_c[:, :, 0:D])

        def ggn_gates():
            with phase() as st:
                xs = sb(st, "gru_xs", [P, 2, 4 * D])
                aT = sb(st, "gru_aT", [P, 2, 4 * P])
                er = sb(st, "gru_r", [P, 4 * P])
                ez = sb(st, "gru_z", [P, 2, 4 * P])
                nn = sb(st, "gru_n", [P, 4 * P])
                hn = sb(st, "gru_h", [P, 2, 4 * P])
                ps_a = ps(st, "gru_psa", [P, 4 * P])
                ps_g = [ps(st, f"gru_psg{i}", [P, 4 * P]) for i in range(4)]
                ps_c = [ps(st, f"gru_psc{i}", [P, 4, D]) for i in range(2)]
                s_xs = sem(st, "gru_xs_ready")
                s_tr = sem(st, "gru_transposed")
                s_aT = sem(st, "gru_aT_ready")
                s_g = sem(st, "gru_gates_done")
                s_e = sem(st, "gru_tanh_rz_ready")
                s_n = sem(st, "gru_n_in")
                s_t = sem(st, "gru_tanh_ready")
                s_hn = sem(st, "gru_h_ready")
                s_c = sem(st, "gru_out_done")
                s_ac = sem(st, "gru_out_taken")
                s_ch = sem(st, "gru_chain")
                NCH = 5
                with nc.Block() as block:
                    @block.vector
                    def _(dve):
                        v = nc.vector

                        def bring(q, k):
                            dve.wait_ge(s_tr, q + 1)
                            v.tensor_copy(xs[:, k, :], quad(acc, q)).then_inc(s_xs, 1)

                        def put(q, k):
                            dve.wait_ge(s_c, q + 3)
                            v.tensor_tensor(quad(acc, q).rearrange("p (j d) -> p j d", d=D), ps_c[k][:, :, :],
                                            b_out[:, :].unsqueeze(1).to_broadcast([P, 4, D]), ALU.add).then_inc(s_ac, 1)

                        def gates(q, k):
                            dve.wait_ge(s_e, q + 1)
                            for g in (er[:, :], ez[:, k, :]):
                                v.tensor_scalar(g, g, 0.5, 0.5, ALU.mult, ALU.add).then_inc(s_ch, 1)
                            dve.wait_ge(s_ch, q * NCH + 2)
                            v.scalar_tensor_tensor(nn[:, :], ps_g[3][:, :], b_hh[:, 2:3], er[:, :], ALU.add, ALU.mult).then_inc(s_ch, 1)
                            dve.wait_ge(s_ch, q * NCH + 3)
                            v.tensor_tensor(nn[:, :], nn[:, :], ps_g[2][:, :], ALU.add).then_inc(s_n, 1)

                        def state(q, k):
                            h = hn[:, k, :]
                            dve.wait_ge(s_t, q + 1)
                            dve.wait_ge(s_c, q + 1)
                            v.tensor_tensor(h, quad(tmp, q), nn[:, :], ALU.subtract).then_inc(s_ch, 1)
                            dve.wait_ge(s_ch, q * NCH + 4)
                            v.tensor_tensor(h, h, ez[:, k, :], ALU.mult).then_inc(s_ch, 1)
                            dve.wait_ge(s_ch, q * NCH + 5)
                            v.tensor_tensor(h, h, nn[:, :], ALU.add).then_inc(s_hn, 1)

                        def body(q, k, has):
                            gates(q + 1, 1 - k) if has(1) else None
                            put(q, k)
                            if has(1):
                                state(q + 1, 1 - k)
                            if has(3):
                                bring(q + 3, 1 - k)

                        dve.sem_inc(s_n, 1)
                        dve.sem_inc(s_ac, 2)
                        bring(0, 0)
                        bring(1, 1)
                        gates(0, 0)
                        state(0, 0)
                        bring(2, 0)
                        quads(dve, body, 3)
                        dve.wait_ge(s_ac, QUADS + 2)

                    @block.tensor
                    def _(pe):
                        def turn(q, k):
                            pe.wait_ge(s_xs, q + 1)
                            pe.wait_ge(s_aT, q) if not isinstance(q, int) or q > 0 else None
                            for j in range(4):
                                i = nc.tensor.transpose(ps_a[:, j * P:(j + 1) * P], xs[:, k, j * D:(j + 1) * D], ident[:, :])
                            i.then_inc(s_tr, 1)

                        def gates(q, k):
                            pe.wait_ge(s_aT, q + 1)
                            pe.wait_ge(s_n, q + 1)
                            for g in range(2):
                                nc.tensor.matmul(ps_g[g][:, :], w_ihT[:, g, :], aT[:, k, :], start=True, stop=False)
                                nc.tensor.matmul(ps_g[g][:, :], w_hhT[:, g, :], quad(tmp, q), start=False, stop=True)
                            nc.tensor.matmul(ps_g[2][:, :], w_ihT[:, 2, :], aT[:, k, :], start=True, stop=True)
                            nc.tensor.matmul(ps_g[3][:, :], w_hhT[:, 2, :], quad(tmp, q), start=True, stop=True).then_inc(s_g, 1)

                        def body(q, k, has):
                            if has(1):
                                gates(q + 1, 1 - k)
                            if has(2):
                                turn(q + 2, k)
                            pe.wait_ge(s_hn, q + 1)
                            pe.wait_ge(s_ac, q + 1)
                            for j in range(4):
                                i = nc.tensor.matmul(ps_c[k][:, j, :], hn[:, k, j * P:(j + 1) * P], w_outT[:, :], start=True, stop=True)
                            i.then_inc(s_c, 1)

                        pe.sem_inc(s_tr, 2)
                        pe.sem_inc(s_c, 2)
                        turn(0, 0)
                        gates(0, 0)
                        turn(1, 1)
                        quads(pe, body, 2)

                    @block.scalar
                    def _(act):
                        def copy(q, k):
                            act.wait_ge(s_tr, q + 3)
                            nc.scalar.activation(aT[:, k, :], ps_a[:, :], ACT.Copy).then_inc(s_aT, 1)

                        def body(q, k, has):
                            act.wait_ge(s_g, q + 1)
                            nc.scalar.activation(er[:, :], ps_g[0][:, :], ACT.Tanh, bias=half_rz[:, 0:1], scale=0.5)
                            nc.scalar.activation(ez[:, k, :], ps_g[1][:, :], ACT.Tanh, bias=half_rz[:, 1:2], scale=0.5).then_inc(s_e, 1)
                            if has(1):
                                copy(q + 1, 1 - k)
                            act.wait_ge(s_n, q + 2)
                            nc.scalar.activation(nn[:, :], nn[:, :], ACT.Tanh, bias=b_ih[:, 2:3]).then_inc(s_t, 1)

                        copy(0, 0)
                        quads(act, body, 1)

        def ggn_out(link, st, t3, x3):
            link(nc.vector.tensor_tensor(t3, acc[:, :].rearrange("p (b d) -> p b d", d=D), x3, ALU.add))


        def rel_start(eng, v, s_pre, s_act):
            if v is not None:
                v.memset(zrel[:, :], 0.0)

        def rel_give(dve, v, q, ps_c, xs, gsb, scr, s_ch):
            def bias(b):
                return b[:, :].unsqueeze(1).to_broadcast([P, 4, D])
            q3 = gsb[:, :, 2 * D:]
            v.tensor_copy(gsb[:, :, 0:D], xs.rearrange("p (j d) -> p j d", d=D))
            v.tensor_tensor(gsb[:, :, D:2 * D], ps_c[:, :, 0:D], bias(b_1), ALU.add)
            v.tensor_tensor(scr[:, :, :], ps_c[:, :, D:2 * D], bias(b_q), ALU.add).then_inc(s_ch, 1)
            dve.wait_ge(s_ch, q * 4 + 1)
            v.tensor_scalar(scr[:, :, :], scr[:, :, :], float(HD) ** -0.5, None, ALU.mult).then_inc(s_ch, 1)
            dve.wait_ge(s_ch, q * 4 + 2)
            v.tensor_copy(q3[:, :, 0:D], scr[:, :, :])
            v.tensor_tensor(xs.rearrange("p (j d) -> p j d", d=D), scr[:, :, :], bias(b_k), ALU.mult).then_inc(s_ch, 1)
            dve.wait_ge(s_ch, q * 4 + 3)
            v.tensor_reduce(q3[:, :, D:D + HEADS], xs.rearrange("p (j h d) -> p j h d", h=HEADS, d=HD), AX, ALU.add).then_inc(s_ch, 1)
            dve.wait_ge(s_ch, q * 4 + 4)
            return v.tensor_scalar(q3[:, :, D + HEADS:QW], nv[:, bass.ds(q * 4, 4)].unsqueeze(2), 1.0, None, ALU.mult)

        def rel_scores():
            with phase() as st:
                rows = sb(st, "s_rows", [P, RING, GT, 2 * D])
                qrows = sb(st, "s_qrows", [P, RING, GT, QW])
                dst_slot = sb(st, "s_dst_slot", [P, RING, GT], I32)
                trow = sb(st, "s_trow", [P, RING, GE], BF16)
                tid_i = sb(st, "s_tid_i", [P, 1], I32)
                tid = sb(st, "s_tid", [P, 2])
                oh = sb(st, "s_oh", [P, 2, GE], BF16)
                dt = sb(st, "s_dt", [P, 2, GT])
                th = sb(st, "s_th", [P, 2, GT])
                tm = sb(st, "s_tm", [P, 2, GT])
                tmh = sb(st, "s_tmh", [P, 2, GT])
                hm = sb(st, "s_hm", [P, GT, D])
                junk = sb(st, "s_junk", [P, GT, D])
                gz = sb(st, "s_gz", [P, 2, GT])
                ga = sb(st, "s_ga", [P, 2, GT])
                gc = sb(st, "s_gc", [P, 2, GT])
                msg = sb(st, "s_msg", [P, GT, D])
                msgT = sb(st, "s_msgT", [P, GE])
                pq = sb(st, "s_pq", [P, GT, D])
                sc = sb(st, "s_sc", [P, GT, HEADS])
                vs = sb(st, "s_vs", [P, RING, GE])
                ps_r = [ps(st, f"s_psr{i}", [P, GT, 2 * D]) for i in range(2)]
                ps_t = ps(st, "s_pst", [P, GE])
                ps_k = ps(st, "s_psk", [P, GT, D])
                ps_v = ps(st, "s_psv", [P, GE])
                s_idx = [sem(st, f"s_idx{k}") for k in range(RING)]
                s_row = landed("s")
                s_trow = [sem(st, f"s_trow{k}") for k in range(RING)]
                s_tid = sem(st, "s_tid_ready")
                s_oh = sem(st, "s_onehot_ready")
                s_r = sem(st, "s_relation_rows")
                s_dt = sem(st, "s_dt_ready")
                s_th = sem(st, "s_time_tanh")
                s_z = sem(st, "s_gate_logits")
                s_g = sem(st, "s_gate_tanh")
                s_msg = sem(st, "s_messages")
                s_mt = sem(st, "s_messages_transposed")
                s_mT = sem(st, "s_messagesT_ready")
                s_k = sem(st, "s_keys")
                s_v = sem(st, "s_values")
                s_sc = sem(st, "s_scores_done")
                s_vs = sem(st, "s_values_copied")
                s_vfree = sem(st, "s_value_buffer_free")
                s_out = [sem(st, f"s_values_stored{k}") for k in range(RING)]
                s_ch = sem(st, "s_chain_logits")
                s_cm = sem(st, "s_chain_messages")
                s_cs = sem(st, "s_chain_scores")
                T = [slice(t * P, (t + 1) * P) for t in range(GT)]
                FILL = 2 * 16 * GT
                LEAD = 2

                def at(i, k, d):
                    return i * RING + (k + d), (k + d) % RING, i + (k + d) // RING

                def rounds(eng, body):
                    whole = (GROUPS - RING) // RING
                    with eng.Fori(0, whole) as i:
                        for k in range(RING):
                            body(i, k, lambda d: True)
                    for g in range(whole * RING, GROUPS):
                        body(g // RING, g % RING, lambda d: g + d < GROUPS)

                with nc.Block() as block:
                    @block.gpsimd
                    def _(pool):
                        pool.sem_inc(s_sc, RING)
                        nc.gpsimd.iota(tid_i[:, :], pattern=[[0, 1]], base=0, channel_multiplier=1).then_inc(s_tid, 1)
                        with pool.Fori(0, GROUPS // RING) as i:
                            for k in range(RING):
                                g = i * RING + k
                                pool.wait_ge(s_sc, g + 1)
                                pool.wait_ge(s_idx[k], i * 32 + 32)
                                pool.sem_inc(s_turn, 1)
                                for t in range(GT):
                                    pool.indirect_dma_start(qrows[:, k, t, :], None, q_tab[:, :],
                                                            bass.IndirectOffsetOnAxis(ap=dst_slot[:, k, t:t + 1], axis=0)).then_inc(s_row[k], 16)
                                    pool.indirect_dma_start(rows[:, k, t, :], None, rel_tab[:, :],
                                                            bass.IndirectOffsetOnAxis(ap=src_slot[:, k, t:t + 1], axis=0)).then_inc(s_row[k], 16)

                    @block.sync
                    def _(sp):
                        def types(i, k, d):
                            g, s, _ = at(i, k, d)
                            sp.wait_ge(s_oh, g + 1)
                            sp.dma_start(trow[:, s, :], type_rows[bass.ds(g, 1), :].to_broadcast([P, GE])).then_inc(s_trow[s], 16)

                        def indices(g, k):
                            sp.dma_start(src_slot[:, k, :], src_g[:, bass.ds(g * GT, GT)]).then_inc(s_idx[k], 16)
                            sp.dma_start(dst_slot[:, k, :], dst_g[:, bass.ds(g * GT, GT)]).then_inc(s_idx[k], 16)

                        def body(i, k, has):
                            g, _, _ = at(i, k, 0)
                            if has(LEAD):
                                types(i, k, LEAD)
                            if not isinstance(i, int) or i > 0:
                                sp.wait_ge(s_out[k], i * 16)
                                sp.sem_inc(s_vfree, 1)
                            sp.wait_ge(s_row[k], i * FILL + FILL)
                            if has(RING):
                                indices(g + RING, k)

                        for k in range(RING):
                            indices(k, k)
                        for g in range(LEAD):
                            types(0, g, 0)
                        sp.sem_inc(s_vfree, RING)
                        for k in range(RING):
                            body(0, k, lambda d: True)
                        whole = (GROUPS - RING) // RING
                        with sp.Fori(1, whole) as i:
                            for k in range(RING):
                                body(i, k, lambda d: True)
                        for g in range(whole * RING, GROUPS):
                            body(g // RING, g % RING, lambda d: g + d < GROUPS)
                        for k in range(RING):
                            sp.wait_ge(s_out[k], GROUPS // RING * 16)

                    @block.vector
                    def _(dve):
                        v = nc.vector

                        def early(i, k, d):
                            g, s, r = at(i, k, d)
                            dve.wait_ge(s_trow[s], r * 16 + 16)
                            dve.wait_ge(s_r, g + 1)
                            v.tensor_scalar(oh[:, s % 2, :], trow[:, s, :], tid[:, 0:1], None, ALU.is_equal).then_inc(s_oh, 1)
                            dve.wait_ge(s_row[s], r * FILL + FILL)
                            v.tensor_tensor(dt[:, s % 2, :], qrows[:, s, :, D + HEADS:QW].rearrange("p t o -> p (t o)"),
                                            w_g[:, bass.ds(g * GT, GT)], ALU.subtract).then_inc(s_dt, 1)

                        def logits(i, k, d):
                            g, s, _ = at(i, k, d)
                            h = s % 2
                            dve.wait_ge(s_th, g + 1)
                            v.tensor_scalar(tmh[:, h, :], th[:, h, :], 0.25, 0.25, ALU.mult, ALU.add)
                            v.tensor_scalar(tm[:, h, :], th[:, h, :], 0.5, 0.5, ALU.mult, ALU.add).then_inc(s_ch, 1)
                            dve.wait_ge(s_ch, g * 2 + 1)
                            dve.wait_ge(s_r, g + 3)
                            for t in range(GT):
                                n = v.scalar_tensor_tensor(hm[:, t, :], ps_r[h][:, t, D:2 * D], tm[:, h, t:t + 1], rows[:, s, t, D:2 * D],
                                                           ALU.mult, ALU.add)
                            n.then_inc(s_ch, 1)
                            dve.wait_ge(s_ch, g * 2 + 2)
                            for t in range(GT):
                                n = v.scalar_tensor_tensor(junk[:, t, :], hm[:, t, :], 0.0, w_2[:, :], ALU.max, ALU.mult,
                                                           accum_out=gz[:, h, t:t + 1])
                            n.then_inc(s_z, 1)

                        def messages(i, k, d):
                            g, s, _ = at(i, k, d)
                            h = s % 2
                            dve.wait_ge(s_g, g + 1)
                            v.scalar_tensor_tensor(gc[:, h, :], ga[:, h, :], 1.0, tmh[:, h, :], ALU.add, ALU.mult).then_inc(s_cm, 1)
                            dve.wait_ge(s_cm, g + 1)
                            dve.wait_ge(s_mt, g + 1)
                            for t in range(GT):
                                n = v.scalar_tensor_tensor(msg[:, t, :], ps_r[h][:, t, 0:D], gc[:, h, t:t + 1], rows[:, s, t, 0:D],
                                                           ALU.mult, ALU.mult)
                            n.then_inc(s_msg, 1)

                        def scores(i, k):
                            g, s, _ = at(i, k, 0)
                            dve.wait_ge(s_k, g + 1)
                            v.tensor_tensor(pq[:, :, :], ps_k[:, :, :], qrows[:, s, :, 0:D], ALU.mult).then_inc(s_cs, 1)
                            dve.wait_ge(s_cs, g * 2 + 1)
                            v.tensor_reduce(sc[:, :, :].rearrange("p t h -> p (t h)"),
                                            pq[:, :, :].rearrange("p t (h d) -> p (t h) d", d=HD), AX, ALU.add).then_inc(s_cs, 1)
                            dve.wait_ge(s_cs, g * 2 + 2)
                            v.tensor_tensor(score[:, :, bass.ds(g * GT, GT)].rearrange("p h t -> p t h"), sc[:, :, :],
                                            qrows[:, s, :, D:D + HEADS], ALU.add).then_inc(s_sc, 1)

                        def body(i, k, has):
                            if has(2):
                                early(i, k, 2)
                            if has(1):
                                logits(i, k, 1)
                            scores(i, k)
                            if has(1):
                                messages(i, k, 1)

                        dve.wait_ge(s_tid, 1)
                        v.tensor_copy(tid[:, 0:1], tid_i[:, :]).then_inc(s_tid, 1)
                        dve.wait_ge(s_tid, 2)
                        v.tensor_scalar(tid[:, 1:2], tid[:, 0:1], float(TYPES), -float(TYPES), ALU.is_ge, ALU.mult).then_inc(s_tid, 1)
                        dve.wait_ge(s_tid, 3)
                        v.tensor_tensor(tid[:, 0:1], tid[:, 0:1], tid[:, 1:2], ALU.add).then_inc(s_tid, 1)
                        dve.wait_ge(s_tid, 4)
                        dve.sem_inc(s_oh, RING)
                        dve.sem_inc(s_msg, 2)
                        early(0, 0, 0)
                        early(0, 1, 0)
                        logits(0, 0, 0)
                        messages(0, 0, 0)
                        rounds(dve, body)
                        dve.wait_ge(s_sc, GROUPS + RING)

                    @block.tensor
                    def _(pe):
                        mm = nc.tensor.matmul

                        def relations(i, k, d):
                            g, s, _ = at(i, k, d)
                            h = s % 2
                            pe.wait_ge(s_oh, g + 1 + RING)
                            pe.wait_ge(s_msg, g + 1)
                            for t in range(GT):
                                mm(ps_r[h][:, t, :], oh[:, h, T[t]], rel_hm[:, :], start=True, stop=False)
                                n = mm(ps_r[h][:, t, :], oh[0:TYPES, h, T[t]], rel_lo[0:TYPES, :], start=False, stop=True)
                            n.then_inc(s_r, 1)

                        def turn(i, k, d):
                            g, s, _ = at(i, k, d)
                            pe.wait_ge(s_msg, g + 3)
                            for t in range(GT):
                                n = nc.tensor.transpose(ps_t[:, T[t]], msg[:, t, :], ident[:, :])
                            n.then_inc(s_mt, 1)

                        def keys(i, k):
                            g, s, _ = at(i, k, 0)
                            pe.wait_ge(s_mT, g + 1)
                            pe.wait_ge(s_sc, g + RING)
                            for t in range(GT):
                                n = mm(ps_k[:, t, :], msgT[:, T[t]], w_kv[:, 0, :], start=True, stop=True)
                            n.then_inc(s_k, 1)
                            pe.wait_ge(s_vs, g + 1)
                            for t in range(GT):
                                n = mm(ps_v[:, T[t]], msgT[:, T[t]], w_kv[:, 1, :], start=True, stop=True)
                            n.then_inc(s_v, 1)

                        def body(i, k, has):
                            keys(i, k)
                            if has(2):
                                relations(i, k, 2)
                            if has(1):
                                turn(i, k, 1)

                        pe.sem_inc(s_r, 2)
                        pe.sem_inc(s_mt, 1)
                        relations(0, 0, 0)
                        relations(0, 1, 0)
                        turn(0, 0, 0)
                        rounds(pe, body)

                    @block.scalar
                    def _(act):
                        f = nc.scalar.activation

                        def time(i, k, d):
                            g, s, _ = at(i, k, d)
                            act.wait_ge(s_dt, g + 1)
                            f(th[:, s % 2, :], dt[:, s % 2, :], ACT.Tanh, scale=half_rtc[:, :]).then_inc(s_th, 1)

                        def gate(i, k, d):
                            g, s, _ = at(i, k, d)
                            act.wait_ge(s_z, g + 1)
                            f(ga[:, s % 2, :], gz[:, s % 2, :], ACT.Tanh, scale=0.5, bias=half_b2[:, :]).then_inc(s_g, 1)

                        def values(i, k):
                            g, s, _ = at(i, k, 0)
                            act.wait_ge(s_v, g + 1)
                            act.wait_ge(s_vfree, g + 1)
                            f(vs[:, s, :], ps_v[:, :], ACT.Copy).then_inc(s_vs, 1)
                            act.wait_ge(s_vs, g + 2)
                            act.dma_start(edge_v[bass.ds(g * P, P), :], vs[:, s, :]).then_inc(s_out[s], 16)

                        def turned(i, k, d):
                            g, s, _ = at(i, k, d)
                            act.wait_ge(s_mt, g + 2)
                            f(msgT[:, :], ps_t[:, :], ACT.Copy).then_inc(s_mT, 1)

                        def body(i, k, has):
                            if has(2):
                                time(i, k, 2)
                            if has(1):
                                gate(i, k, 1)
                            values(i, k)
                            if has(1):
                                turned(i, k, 1)

                        act.sem_inc(s_vs, 1)
                        time(0, 0, 0)
                        time(0, 1, 0)
                        gate(0, 0, 0)
                        turned(0, 0, 0)
                        rounds(act, body)

        def rel_out(link, st, t3, x3):
            v = nc.vector
            rz = sb(st, "ro_rz", [P, NBP * HEADS])
            has = sb(st, "ro_has", [P, NBP * HEADS])

            def heads(t):
                return t[:, :].rearrange("p (b d) -> p b d", d=HD)

            link(v.tensor_scalar(rz[:, :], zrel[:, :], 1e-30, None, ALU.max))
            link(v.reciprocal(rz[:, :], rz[:, :]))
            link(v.tensor_scalar(has[:, :], zrel[:, :], 0.0, None, ALU.is_gt))
            link(v.tensor_tensor(heads(tmp), heads(acc), wide(rz[:, :], HD), ALU.mult))
            link(v.tensor_tensor(acc[:, :].rearrange("p (b d) -> p b d", d=D), every(b_v),
                                 has[:, :].rearrange("p (b h) -> p b h", h=HEADS)[:, :, 0:1].to_broadcast([P, NBP, D]), ALU.mult))
            link(v.tensor_tensor(t3, t3, acc[:, :].rearrange("p (b d) -> p b d", d=D), ALU.add))
            link(v.tensor_tensor(t3, t3, x3, ALU.add))

        gat_nodes(0)
        gat_logits(0)
        segment_softmax("g0_sm", gx[:, 0:1, :], 1, gx[:, 1, :])
        gat_sums(0)
        gat_nodes(1)
        gat_logits(1)
        segment_softmax("g1_sm", gx[:, 0:1, :], 1, gx[:, 1, :])
        gat_sums(1)
        residual_norm("ln0", gat_out)
        gat.close()
        table_nodes("gcn", take_x, None, None, None, w_gcn[:, :], D, [(gcn_tab, 0, D)], D, gcn_give, gcn_start)
        sum_edges("gcn_e", gcn_tab, True)
        residual_norm("ln1", gcn_out)
        rel = ExitStack()
        QW = D + HEADS + 1
        score = sb(rel, "score", [P, HEADS, TILES])
        zrel = sb(rel, "zrel", [P, NBP * HEADS])
        table_nodes("reln", take_x, None, None, None, w_xq[:, :, :].rearrange("p a d -> p (a d)"), 2 * D,
                    [(rel_tab, 0, 2 * D), (q_tab, 2 * D, 2 * D + QW)], 2 * D + QW, rel_give, rel_start)
        rel_scores()
        segment_softmax("rel_sm", score, HEADS)
        edge_sums("rel_e", score, HEADS, HEADS, zrel, None)
        residual_norm("ln2", rel_out)
        table_nodes("ggn", take_x, w_inT, b_in, tmp, w_msg[:, :], D, [(ggn_tab, 0, D)], D, ggn_give, ggn_start)
        sum_edges("ggn_e", ggn_tab, False)
        ggn_gates()
        residual_norm("ln3", ggn_out)
        rel.close()
        s = sem(top, 'out_stored')
        with nc.Block() as block:
            @block.sync
            def _(sp):
                sp.dma_start(out[0:(BLOCKS - 1) * P, :].rearrange("(b p) d -> p b d", p=P), x_n[:, 0:(BLOCKS - 1) * D].rearrange("p (b d) -> p b d", d=D)).then_inc(s, 16)
                sp.dma_start(out[(BLOCKS - 1) * P:N, :], x_n[0:N - (BLOCKS - 1) * P, (BLOCKS - 1) * D:BLOCKS * D]).then_inc(s, 16)
                sp.wait_ge(s, 32)


_INS = ['x', 'src', 'dst', 'edge_type_64', 'edge_weight', 'node_vec', 'L0_gnn_W_node', 'L0_gnn_b_node', 'L0_gnn_lyr_W',
        'L0_gnn_att_src', 'L0_gnn_att_dst', 'L0_gnn_lyr_bias', 'L1_gnn_W', 'L1_gnn_b', 'L2_gnn_rel_table', 'L2_gnn_Wq',
        'L2_gnn_bq', 'L2_gnn_Wk', 'L2_gnn_bk', 'L2_gnn_Wv', 'L2_gnn_bv', 'L2_gnn_W1', 'L2_gnn_b1', 'L2_gnn_W2', 'L2_gnn_b2',
        'L2_gnn_time_coeff', 'L3_gnn_W_in', 'L3_gnn_b_in', 'L3_gnn_W_msg', 'L3_gnn_W_ih', 'L3_gnn_b_ih', 'L3_gnn_W_hh',
        'L3_gnn_b_hh', 'L3_gnn_W_out', 'L3_gnn_b_out']


def kernel(**inputs):
    import concourse.bacc as _bacc
    from concourse.bass_utils import run_bass_kernel_spmd as _run

    nc = _bacc.Bacc("TRN2", target_bir_lowering=False, num_devices=1)
    arrays, args = {}, {}
    for name in _INS:
        a = np.ascontiguousarray(inputs[name])
        if a.ndim == 0:
            a = a.reshape(1)
        arrays[f"in_{name}"] = a
        args[name] = nc.dram_tensor(f"in_{name}", a.shape, mybir.dt.from_np(a.dtype), kind="ExternalInput").ap()
    out = nc.dram_tensor("out_0", (N, D), F32, kind="ExternalOutput").ap()
    build(nc, args, out)
    r = _run(nc, [arrays], core_ids=[0])
    return r.results[0]["out_0"]
```
